# Optimizing a Trainium2 kernel written in Bass

```python
import numpy as np
import jax
import jax.numpy as jnp

def _softmax(x, axis=-1):
    return jax.nn.softmax(x, axis=axis)

def _gelu(x):
    return jax.nn.gelu(x, approximate=True)

def _silu(x):
    return jax.nn.silu(x)

def _sigmoid(x):
    return jax.nn.sigmoid(x)

def _layernorm(x, axis=-1, eps=1e-05):
    m = jnp.mean(x, axis=axis, keepdims=True)
    v = jnp.var(x, axis=axis, keepdims=True)
    return (x - m) / jnp.sqrt(v + eps)

def _scatter_add(tgt, idx, src, axis=0):
    return tgt.at[idx].add(src)

def _segment_sum(src, seg, n):
    return jax.ops.segment_sum(src, seg, n)
kernel_name = 'mk_vit_tower_d4_tok_img768_r4_cced93'

def setup_inputs(seed: int=0):
    np.random.seed(seed)
    _w = jnp.asarray

    def _rec_inputs():
        import jax
        import jax.numpy as jnp
        _rk = jax.random.key(seed)
        x = -7.10856e-05 + 0.999911 * jax.random.normal(jax.random.fold_in(_rk, 1), (4, 32, 128, 128), jnp.float32)
        return x
    x = _rec_inputs()

    def _L0_tok_setup():
        import jax, jax.numpy as jnp
        import numpy as np
        B, C, H, W = (8, 32, 128, 128)
        P = 8
        D = 128
        NH, DH = (8, 64)
        M = 512
        L = 2
        DOUT = 192
        INNER = NH * DH

        def _ln(x, g, b, eps=1e-05):
            mu = x.mean(-1, keepdims=True)
            xc = x - mu
            var = (xc * xc).mean(-1, keepdims=True)
            return xc * jax.lax.rsqrt(var + eps) * g + b

        def _forward(im, conv_w, conv_b, ln1_g, ln1_b, qkv_w, out_w, out_b, ln2_g, ln2_b, ff1_w, ff1_b, ff2_w, ff2_b, lnf_g, lnf_b, head_w, head_b):
            b, c, h, w = im.shape
            hp, wp = (h // P, w // P)
            patches = im.reshape(b, c, hp, P, wp, P)
            x = jnp.einsum('bchpwq,dcpq->bhwd', patches, conv_w)
            x = x.reshape(b, hp * wp, -1) + conv_b
            n = hp * wp
            scale = DH ** (-0.5)
            for i in range(ln1_g.shape[0]):
                y = _ln(x, ln1_g[i], ln1_b[i])
                qkv = y @ qkv_w[i]
                q, k, v = jnp.split(qkv, 3, axis=-1)
                to_heads = lambda t: t.reshape(b, n, NH, DH).transpose(0, 2, 1, 3)
                q, k, v = (to_heads(q), to_heads(k), to_heads(v))
                q = jax.nn.softmax(q, axis=-1) * scale
                k = jax.nn.softmax(k, axis=-2)
                ctx = jnp.einsum('bhnd,bhne->bhde', k, v)
                att = jnp.einsum('bhnd,bhde->bhne', q, ctx)
                att = att.transpose(0, 2, 1, 3).reshape(b, n, INNER)
                x = x + att @ out_w[i] + out_b[i]
                y = _ln(x, ln2_g[i], ln2_b[i])
                hdn = jax.nn.gelu(y @ ff1_w[i] + ff1_b[i], approximate=False)
                x = x + hdn @ ff2_w[i] + ff2_b[i]
            return _ln(x, lnf_g, lnf_b) @ head_w + head_b
        key = jax.random.key(seed)
        ks = iter(jax.random.split(key, 32))
        g = lambda shape, s=0.02: (jax.random.normal(next(ks), shape) * s).astype(jnp.float32)
        inp = {'im': jax.random.normal(next(ks), (B, C, H, W), dtype=jnp.float32), 'conv_w': g((D, C, P, P)), 'conv_b': jnp.zeros((D,), jnp.float32), 'ln1_g': jnp.ones((L, D), jnp.float32), 'ln1_b': jnp.zeros((L, D), jnp.float32), 'qkv_w': g((L, D, 3 * INNER)), 'out_w': g((L, INNER, D)), 'out_b': jnp.zeros((L, D), jnp.float32), 'ln2_g': jnp.ones((L, D), jnp.float32), 'ln2_b': jnp.zeros((L, D), jnp.float32), 'ff1_w': g((L, D, M)), 'ff1_b': jnp.zeros((L, M), jnp.float32), 'ff2_w': g((L, M, D)), 'ff2_b': jnp.zeros((L, D), jnp.float32), 'lnf_g': jnp.ones((D,), jnp.float32), 'lnf_b': jnp.zeros((D,), jnp.float32), 'head_w': g((D, DOUT)), 'head_b': jnp.zeros((DOUT,), jnp.float32)}
        return inp
    _L0_tok_all = _L0_tok_setup()
    _L0_tok_in = {k: v for k, v in _L0_tok_all.items() if k in ('conv_w', 'conv_b', 'ln1_g', 'ln1_b', 'qkv_w', 'out_w', 'out_b', 'ln2_g', 'ln2_b', 'ff1_w', 'ff1_b', 'ff2_w', 'ff2_b', 'lnf_g', 'lnf_b', 'head_w', 'head_b')}
    del _L0_tok_all

    def _L0_attn_setup():
        import jax, jax.numpy as jnp
        import numpy as np
        DILATIONS = [(1, 2, 4), (1, 1, 1), (4, 8, 16), (8, 16, 32), (32, 64, 128), (64, 128, 64), (64, 128, 256), (1, 100, 200), (1, 125, 250), (1, 256, 512), (3, 9, 27), (5, 25, 125)]
        MEM_HEADS = (6, 7, 8, 9)
        NUM_HEADS = 12
        HIDDEN = 192
        HEAD_DIM = HIDDEN // NUM_HEADS
        KSZ = 4
        MEM_DIM = 128
        STRIDE = 64

        def causal_dconv(h, w, b, dilation):
            pad = (KSZ - 1) * dilation
            hp = jnp.pad(h, ((0, 0), (0, 0), (pad, 0)))
            out = jax.lax.conv_general_dilated(hp, w[:, None, :], window_strides=(1,), padding='VALID', rhs_dilation=(dilation,), dimension_numbers=('NCH', 'OIH', 'NCH'), feature_group_count=h.shape[1])
            return out + b[None, :, None]

        def neural_memory(x, Wq, Wk, Wv, Wg_w, Wg_b, Wout):
            B, S, D = x.shape
            q = x @ Wq.T
            k = x @ Wk.T
            v = x @ Wv.T
            g = jax.nn.sigmoid(x @ Wg_w.T + Wg_b)
            nC = S // STRIDE
            qc = q.reshape(B, nC, STRIDE, D).transpose(1, 0, 2, 3)
            kc = k.reshape(B, nC, STRIDE, D).transpose(1, 0, 2, 3)
            vc = v.reshape(B, nC, STRIDE, MEM_DIM).transpose(1, 0, 2, 3)
            gc = g.reshape(B, nC, STRIDE, 1).transpose(1, 0, 2, 3)

            def step(M, inp):
                qi, ki, vi, gi = inp
                reads = jnp.einsum('bsd,bdm->bsm', qi, M)
                write = jnp.einsum('bsd,bsm->bdm', ki * gi, vi)
                avg_gate = gi.mean(axis=1, keepdims=True)
                return ((1.0 - avg_gate) * M + write, reads)
            M0 = jnp.zeros((B, D, MEM_DIM), x.dtype)
            _, reads = jax.lax.scan(step, M0, (qc, kc, vc, gc))
            reads = reads.transpose(1, 0, 2, 3).reshape(B, S, MEM_DIM)
            return reads @ Wout.T
        key = jax.random.key(seed)
        ks = jax.random.split(key, 17)
        B, S = (4, 1024)
        s = 0.01
        return {'x': jax.random.normal(ks[0], (B, S, HIDDEN), jnp.float32), 'conv_w': jax.random.normal(ks[1], (NUM_HEADS, 3, HEAD_DIM, KSZ), jnp.float32) * 0.1, 'conv_b': jax.random.normal(ks[2], (NUM_HEADS, 3, HEAD_DIM), jnp.float32) * 0.01, 'mem_Wq': jax.random.normal(ks[3], (4, HEAD_DIM, HEAD_DIM), jnp.float32) * s, 'mem_Wk': jax.random.normal(ks[4], (4, HEAD_DIM, HEAD_DIM), jnp.float32) * s, 'mem_Wv': jax.random.normal(ks[5], (4, MEM_DIM, HEAD_DIM), jnp.float32) * s, 'mem_Wg_w': jax.random.normal(ks[6], (4, 1, HEAD_DIM), jnp.float32) * 0.02, 'mem_Wg_b': jnp.full((4, 1), -2.0, jnp.float32), 'mem_Wout': jax.random.normal(ks[7], (4, HEAD_DIM, MEM_DIM), jnp.float32) * s, 'gate_w': jax.random.normal(ks[8], (2 * HIDDEN, HIDDEN), jnp.float32) * 0.02, 'router_w': jax.random.normal(ks[9], (NUM_HEADS, HIDDEN), jnp.float32) * 0.02, 'router_b': jnp.zeros((NUM_HEADS,), jnp.float32), 'mixg_w': jax.random.normal(ks[10], (HIDDEN, HIDDEN), jnp.float32) * 0.02, 'mixg_b': jnp.full((HIDDEN,), 2.0, jnp.float32), 'mix_w': jax.random.normal(ks[11], (HIDDEN, HIDDEN), jnp.float32) * 0.02, 'mix_b': jnp.zeros((HIDDEN,), jnp.float32)}
    _L0_attn_all = _L0_attn_setup()
    _L0_attn_in = {k: v for k, v in _L0_attn_all.items() if k in ('conv_w', 'conv_b', 'mem_Wq', 'mem_Wk', 'mem_Wv', 'mem_Wg_w', 'mem_Wg_b', 'mem_Wout', 'gate_w', 'router_w', 'router_b', 'mixg_w', 'mixg_b', 'mix_w', 'mix_b')}
    del _L0_attn_all

    def _L0_ffn_setup():
        import math
        import jax, jax.numpy as jnp
        import numpy as np
        EMBED_CHOICES = [96, 144, 192]
        RATIO_CHOICES = [2, 3, 4]
        E_MAX = 192
        H_MAX = 768

        def new_gelu(x):
            c = math.sqrt(2.0 / math.pi)
            return 0.5 * x * (1.0 + jnp.tanh(c * (x + 0.044715 * x * x * x)))

        def _mixed_coeffs(alpha_e, alpha_r):
            h_idx = jnp.arange(H_MAX)
            d_idx = jnp.arange(E_MAX)
            C0 = jnp.zeros((H_MAX, E_MAX), jnp.float32)
            c0b = jnp.zeros((H_MAX,), jnp.float32)
            C1 = jnp.zeros((E_MAX, H_MAX), jnp.float32)
            c1b = jnp.zeros((E_MAX,), jnp.float32)
            for i, e in enumerate(EMBED_CHOICES):
                m_in = (d_idx < e).astype(jnp.float32)
                for j, r in enumerate(RATIO_CHOICES):
                    a = alpha_e[i] * alpha_r[j]
                    m_out = (h_idx < r * e).astype(jnp.float32)
                    C0 = C0 + a * (m_out[:, None] * m_in[None, :])
                    c0b = c0b + a * m_out
                    C1 = C1 + a * (m_in[:, None] * m_out[None, :])
                    c1b = c1b + a * m_in
            return (C0, c0b, C1, c1b)
        key = jax.random.key(seed)
        ks = jax.random.split(key, 6)
        x = jax.random.normal(ks[0], (8, 512, E_MAX), jnp.float32)
        w_fc = jax.random.normal(ks[1], (H_MAX, E_MAX), jnp.float32) * 0.02
        b_fc = jnp.zeros((H_MAX,), jnp.float32)
        w_proj = jax.random.normal(ks[2], (E_MAX, H_MAX), jnp.float32) * 0.02
        b_proj = jnp.zeros((E_MAX,), jnp.float32)
        alpha_e = jax.nn.softmax(jax.random.normal(ks[3], (3,), jnp.float32))
        alpha_r = jax.nn.softmax(jax.random.normal(ks[4], (3,), jnp.float32))
        return {'x': x, 'w_fc': w_fc, 'b_fc': b_fc, 'w_proj': w_proj, 'b_proj': b_proj, 'alpha_e': alpha_e, 'alpha_r': alpha_r}
    _L0_ffn_all = _L0_ffn_setup()
    _L0_ffn_in = {k: v for k, v in _L0_ffn_all.items() if k in ('w_fc', 'b_fc', 'w_proj', 'b_proj', 'alpha_e', 'alpha_r')}
    del _L0_ffn_all

    def _L1_attn_setup():
        import jax, jax.numpy as jnp
        import numpy as np
        NUM_HEADS = 12
        NUM_LANDMARKS = 64

        def iterative_inv(K, n_iter=6):
            I = jnp.eye(K.shape[-1], dtype=K.dtype)
            denom = jnp.max(jnp.sum(K, axis=-2), axis=-1)[..., None, None]
            V = jnp.swapaxes(K, -1, -2) / denom
            for _ in range(n_iter):
                KV = K @ V
                V = 0.25 * V @ (13.0 * I - KV @ (15.0 * I - KV @ (7.0 * I - KV)))
            return V
        key = jax.random.key(seed)
        k1, k2, k3, k4 = jax.random.split(key, 4)
        B, N, C = (8, 1024, 192)
        x = jax.random.normal(k1, (B, N, C), dtype=jnp.float32)
        w_qkv = jax.random.normal(k2, (C, 3 * C), dtype=jnp.float32) * 0.02
        w_proj = jax.random.normal(k3, (C, C), dtype=jnp.float32) * 0.02
        b_proj = jax.random.normal(k4, (C,), dtype=jnp.float32) * 0.02
        return {'x': x, 'w_qkv': w_qkv, 'w_proj': w_proj, 'b_proj': b_proj}
    _L1_attn_all = _L1_attn_setup()
    _L1_attn_in = {k: v for k, v in _L1_attn_all.items() if k in ('w_qkv', 'w_proj', 'b_proj')}
    del _L1_attn_all

    def _L1_ffn_setup():
        import jax, jax.numpy as jnp
        import numpy as np
        TOP_K = 2
        key = jax.random.key(seed)
        ks = jax.random.split(key, 5)
        B, S, D, H, E = (1, 512, 192, 768, 8)
        x = jax.random.normal(ks[0], (B, S, D), dtype=jnp.float32)
        gate_w = jax.random.normal(ks[1], (E, D), dtype=jnp.float32) * 0.02
        w1 = jax.random.normal(ks[2], (E, D, H), dtype=jnp.float32) * 0.02
        b1 = jnp.zeros((E, H), dtype=jnp.float32)
        w2 = jax.random.normal(ks[3], (E, H, D), dtype=jnp.float32) * 0.02
        b2 = jnp.zeros((E, D), dtype=jnp.float32)
        return {'x': x, 'gate_w': gate_w, 'w1': w1, 'b1': b1, 'w2': w2, 'b2': b2}
    _L1_ffn_all = _L1_ffn_setup()
    _L1_ffn_in = {k: v for k, v in _L1_ffn_all.items() if k in ('gate_w', 'w1', 'b1', 'w2', 'b2')}
    del _L1_ffn_all

    def _L2_attn_setup():
        import jax, jax.numpy as jnp
        import numpy as np
        HIDDEN = 192
        TTT_HIDDEN = 512
        CHUNK = 128
        SEQ = 2048
        BATCH = 4
        LR = 0.01

        def _fast_weight(xc, w0, w1, w2):
            return jax.nn.silu(xc @ w0) * (xc @ w2) @ w1

        def _reference_tuple_inner(x, w0, w1, w2):
            b, s, h = x.shape
            num_chunks = s // CHUNK
            x_chunks = x.reshape(b, num_chunks, CHUNK, h).transpose(1, 0, 2, 3)

            def process_chunk(carry, x_chunk):
                cw0, cw1, cw2, acc_loss = carry
                chunk_output = _fast_weight(x_chunk, cw0, cw1, cw2)

                def loss_fn(a0, a1, a2):
                    out = _fast_weight(x_chunk, a0, a1, a2)
                    return jnp.mean((out - x_chunk) ** 2)
                chunk_loss, (g0, g1, g2) = jax.value_and_grad(loss_fn, argnums=(0, 1, 2))(cw0, cw1, cw2)
                new_carry = (cw0 - LR * g0, cw1 - LR * g1, cw2 - LR * g2, acc_loss + chunk_loss)
                return (new_carry, chunk_output)
            init = (w0, w1, w2, jnp.float32(0.0))
            (_, _, _, total_loss), ys = jax.lax.scan(process_chunk, init, x_chunks)
            output = ys.transpose(1, 0, 2, 3).reshape(b, s, h)
            ttt_loss = total_loss / num_chunks
            return (output, ttt_loss)
        key = jax.random.key(seed)
        k1, k2, k3, k4 = jax.random.split(key, 4)
        x = jax.random.normal(k1, (BATCH, SEQ, HIDDEN), dtype=jnp.float32)
        w0 = jax.random.normal(k2, (HIDDEN, TTT_HIDDEN), dtype=jnp.float32) * 0.02
        w1 = jax.random.normal(k3, (TTT_HIDDEN, HIDDEN), dtype=jnp.float32) * 0.02
        w2 = jax.random.normal(k4, (HIDDEN, TTT_HIDDEN), dtype=jnp.float32) * 0.02
        return {'x': x, 'w0': w0, 'w1': w1, 'w2': w2}
    _L2_attn_all = _L2_attn_setup()
    _L2_attn_in = {k: v for k, v in _L2_attn_all.items() if k in ('w0', 'w1', 'w2')}
    del _L2_attn_all

    def _L2_ffn_setup():
        import jax, jax.numpy as jnp
        import numpy as np
        B, S, D, F, E = (8, 512, 192, 768, 16)
        CAP = 64
        EPS = 1e-06

        def _switch_moe_block(x, ln_w, w_router, wi, wo):
            var = jnp.mean(jnp.square(x.astype(jnp.float32)), axis=-1, keepdims=True)
            normed = (x * jax.lax.rsqrt(var + EPS)).astype(x.dtype) * ln_w
            logits = jnp.einsum('bsd,de->bse', normed.astype(jnp.float32), w_router.astype(jnp.float32))
            probs = jax.nn.softmax(logits, axis=-1)
            expert_idx = jnp.argmax(probs, axis=-1)
            onehot = jax.nn.one_hot(expert_idx, E, dtype=jnp.float32)
            priority = jnp.cumsum(onehot, axis=1)
            keep = onehot * (priority <= CAP)
            pos = (priority - 1.0).astype(jnp.int32)
            dispatch = keep[..., None] * jax.nn.one_hot(pos, CAP, dtype=jnp.float32)
            expert_in = jnp.einsum('bsec,bsd->becd', dispatch, normed)
            h = jax.nn.relu(jnp.einsum('becd,edf->becf', expert_in, wi))
            expert_out = jnp.einsum('becf,efd->becd', h, wo)
            combined = jnp.einsum('bsec,becd->bsd', dispatch, expert_out)
            routed = jnp.sum(dispatch, axis=(2, 3)) > 0
            next_states = jnp.where(routed[..., None], combined.astype(x.dtype), normed)
            router_prob = jnp.max(probs, axis=-1, keepdims=True).astype(x.dtype)
            return x + router_prob * next_states
        key = jax.random.key(seed)
        k_x, k_r, k_wi, k_wo = jax.random.split(key, 4)
        x = jax.random.normal(k_x, (B, S, D), dtype=jnp.float32)
        ln_w = jnp.ones((D,), dtype=jnp.float32)
        w_router = jax.random.normal(k_r, (D, E), dtype=jnp.float32) * 0.02
        wi = jax.random.normal(k_wi, (E, D, F), dtype=jnp.float32) * D ** (-0.5)
        wo = jax.random.normal(k_wo, (E, F, D), dtype=jnp.float32) * F ** (-0.5)
        return {'x': x, 'ln_w': ln_w, 'w_router': w_router, 'wi': wi, 'wo': wo}
    _L2_ffn_all = _L2_ffn_setup()
    _L2_ffn_in = {k: v for k, v in _L2_ffn_all.items() if k in ('ln_w', 'w_router', 'wi', 'wo')}
    del _L2_ffn_all

    def _L3_attn_setup():
        import jax, jax.numpy as jnp
        import numpy as np
        EMBED_DIM = 192
        NUM_HEADS = 12
        HEAD_DIM = EMBED_DIM // NUM_HEADS
        SCALING = HEAD_DIM ** (-0.5)
        B, N = (4, 512)
        key = jax.random.key(seed)
        k_x, k_wqkv, k_bqkv, k_wo, k_bo = jax.random.split(key, 5)
        s = EMBED_DIM ** (-0.5)
        return {'x_q': jax.random.normal(k_x, (B, N, EMBED_DIM), dtype=jnp.float32), 'w_qkv': jax.random.normal(k_wqkv, (3 * EMBED_DIM, EMBED_DIM), dtype=jnp.float32) * s, 'b_qkv': jax.random.normal(k_bqkv, (3 * EMBED_DIM,), dtype=jnp.float32) * s, 'w_out': jax.random.normal(k_wo, (EMBED_DIM, EMBED_DIM), dtype=jnp.float32) * s, 'b_out': jax.random.normal(k_bo, (EMBED_DIM,), dtype=jnp.float32) * s}
    _L3_attn_all = _L3_attn_setup()
    _L3_attn_in = {k: v for k, v in _L3_attn_all.items() if k in ('w_qkv', 'b_qkv', 'w_out', 'b_out')}
    del _L3_attn_all

    def _L3_ffn_setup():
        import jax, jax.numpy as jnp
        import numpy as np
        D_MODEL, D_FF, N_EXPERTS, TOP_K = (192, 768, 8, 2)
        B, S = (2, 256)
        LN_EPS = 1e-05

        def _layernorm(x, gamma, beta):
            mu = jnp.mean(x, axis=-1, keepdims=True)
            var = jnp.mean(jnp.square(x - mu), axis=-1, keepdims=True)
            return (x - mu) * jax.lax.rsqrt(var + LN_EPS) * gamma + beta
        key = jax.random.key(seed)
        k1, k2, k3, k4 = jax.random.split(key, 4)
        return {'hidden_states': jax.random.normal(k1, (B, S, D_MODEL), dtype=jnp.float32), 'ln_gamma': jnp.ones((D_MODEL,), dtype=jnp.float32), 'ln_beta': jnp.zeros((D_MODEL,), dtype=jnp.float32), 'router_w': jax.random.normal(k2, (D_MODEL, N_EXPERTS), dtype=jnp.float32) * 0.02, 'w1': jax.random.normal(k3, (N_EXPERTS, D_MODEL, D_FF), dtype=jnp.float32) * 0.02, 'w2': jax.random.normal(k4, (N_EXPERTS, D_FF, D_MODEL), dtype=jnp.float32) * 0.02}
    _L3_ffn_all = _L3_ffn_setup()
    _L3_ffn_in = {k: v for k, v in _L3_ffn_all.items() if k in ('ln_gamma', 'ln_beta', 'router_w', 'w1', 'w2')}
    del _L3_ffn_all
    return {'x': x, 'L0_tok_conv_w': _L0_tok_in['conv_w'], 'L0_tok_conv_b': _L0_tok_in['conv_b'], 'L0_tok_ln1_g': _L0_tok_in['ln1_g'], 'L0_tok_ln1_b': _L0_tok_in['ln1_b'], 'L0_tok_qkv_w': _L0_tok_in['qkv_w'], 'L0_tok_out_w': _L0_tok_in['out_w'], 'L0_tok_out_b': _L0_tok_in['out_b'], 'L0_tok_ln2_g': _L0_tok_in['ln2_g'], 'L0_tok_ln2_b': _L0_tok_in['ln2_b'], 'L0_tok_ff1_w': _L0_tok_in['ff1_w'], 'L0_tok_ff1_b': _L0_tok_in['ff1_b'], 'L0_tok_ff2_w': _L0_tok_in['ff2_w'], 'L0_tok_ff2_b': _L0_tok_in['ff2_b'], 'L0_tok_lnf_g': _L0_tok_in['lnf_g'], 'L0_tok_lnf_b': _L0_tok_in['lnf_b'], 'L0_tok_head_w': _L0_tok_in['head_w'], 'L0_tok_head_b': _L0_tok_in['head_b'], 'L0_attn_conv_w': _L0_attn_in['conv_w'], 'L0_attn_conv_b': _L0_attn_in['conv_b'], 'L0_attn_mem_Wq': _L0_attn_in['mem_Wq'], 'L0_attn_mem_Wk': _L0_attn_in['mem_Wk'], 'L0_attn_mem_Wv': _L0_attn_in['mem_Wv'], 'L0_attn_mem_Wg_w': _L0_attn_in['mem_Wg_w'], 'L0_attn_mem_Wg_b': _L0_attn_in['mem_Wg_b'], 'L0_attn_mem_Wout': _L0_attn_in['mem_Wout'], 'L0_attn_gate_w': _L0_attn_in['gate_w'], 'L0_attn_router_w': _L0_attn_in['router_w'], 'L0_attn_router_b': _L0_attn_in['router_b'], 'L0_attn_mixg_w': _L0_attn_in['mixg_w'], 'L0_attn_mixg_b': _L0_attn_in['mixg_b'], 'L0_attn_mix_w': _L0_attn_in['mix_w'], 'L0_attn_mix_b': _L0_attn_in['mix_b'], 'L0_ffn_w_fc': _L0_ffn_in['w_fc'], 'L0_ffn_b_fc': _L0_ffn_in['b_fc'], 'L0_ffn_w_proj': _L0_ffn_in['w_proj'], 'L0_ffn_b_proj': _L0_ffn_in['b_proj'], 'L0_ffn_alpha_e': _L0_ffn_in['alpha_e'], 'L0_ffn_alpha_r': _L0_ffn_in['alpha_r'], 'L1_attn_w_qkv': _L1_attn_in['w_qkv'], 'L1_attn_w_proj': _L1_attn_in['w_proj'], 'L1_attn_b_proj': _L1_attn_in['b_proj'], 'L1_ffn_gate_w': _L1_ffn_in['gate_w'], 'L1_ffn_w1': _L1_ffn_in['w1'], 'L1_ffn_b1': _L1_ffn_in['b1'], 'L1_ffn_w2': _L1_ffn_in['w2'], 'L1_ffn_b2': _L1_ffn_in['b2'], 'L2_attn_w0': _L2_attn_in['w0'], 'L2_attn_w1': _L2_attn_in['w1'], 'L2_attn_w2': _L2_attn_in['w2'], 'L2_ffn_ln_w': _L2_ffn_in['ln_w'], 'L2_ffn_w_router': _L2_ffn_in['w_router'], 'L2_ffn_wi': _L2_ffn_in['wi'], 'L2_ffn_wo': _L2_ffn_in['wo'], 'L3_attn_w_qkv': _L3_attn_in['w_qkv'], 'L3_attn_b_qkv': _L3_attn_in['b_qkv'], 'L3_attn_w_out': _L3_attn_in['w_out'], 'L3_attn_b_out': _L3_attn_in['b_out'], 'L3_ffn_ln_gamma': _L3_ffn_in['ln_gamma'], 'L3_ffn_ln_beta': _L3_ffn_in['ln_beta'], 'L3_ffn_router_w': _L3_ffn_in['router_w'], 'L3_ffn_w1': _L3_ffn_in['w1'], 'L3_ffn_w2': _L3_ffn_in['w2']}

def reference(x, L0_tok_conv_w, L0_tok_conv_b, L0_tok_ln1_g, L0_tok_ln1_b, L0_tok_qkv_w, L0_tok_out_w, L0_tok_out_b, L0_tok_ln2_g, L0_tok_ln2_b, L0_tok_ff1_w, L0_tok_ff1_b, L0_tok_ff2_w, L0_tok_ff2_b, L0_tok_lnf_g, L0_tok_lnf_b, L0_tok_head_w, L0_tok_head_b, L0_attn_conv_w, L0_attn_conv_b, L0_attn_mem_Wq, L0_attn_mem_Wk, L0_attn_mem_Wv, L0_attn_mem_Wg_w, L0_attn_mem_Wg_b, L0_attn_mem_Wout, L0_attn_gate_w, L0_attn_router_w, L0_attn_router_b, L0_attn_mixg_w, L0_attn_mixg_b, L0_attn_mix_w, L0_attn_mix_b, L0_ffn_w_fc, L0_ffn_b_fc, L0_ffn_w_proj, L0_ffn_b_proj, L0_ffn_alpha_e, L0_ffn_alpha_r, L1_attn_w_qkv, L1_attn_w_proj, L1_attn_b_proj, L1_ffn_gate_w, L1_ffn_w1, L1_ffn_b1, L1_ffn_w2, L1_ffn_b2, L2_attn_w0, L2_attn_w1, L2_attn_w2, L2_ffn_ln_w, L2_ffn_w_router, L2_ffn_wi, L2_ffn_wo, L3_attn_w_qkv, L3_attn_b_qkv, L3_attn_w_out, L3_attn_b_out, L3_ffn_ln_gamma, L3_ffn_ln_beta, L3_ffn_router_w, L3_ffn_w1, L3_ffn_w2):
    import jax
    import jax.numpy as jnp

    def _L0_tok_ref(im, conv_w, conv_b, ln1_g, ln1_b, qkv_w, out_w, out_b, ln2_g, ln2_b, ff1_w, ff1_b, ff2_w, ff2_b, lnf_g, lnf_b, head_w, head_b):
        import jax, jax.numpy as jnp
        import numpy as np
        B, C, H, W = (8, 32, 128, 128)
        P = 8
        D = 128
        NH, DH = (8, 64)
        M = 512
        L = 2
        DOUT = 192
        INNER = NH * DH

        def _ln(x, g, b, eps=1e-05):
            mu = x.mean(-1, keepdims=True)
            xc = x - mu
            var = (xc * xc).mean(-1, keepdims=True)
            return xc * jax.lax.rsqrt(var + eps) * g + b

        def _forward(im, conv_w, conv_b, ln1_g, ln1_b, qkv_w, out_w, out_b, ln2_g, ln2_b, ff1_w, ff1_b, ff2_w, ff2_b, lnf_g, lnf_b, head_w, head_b):
            b, c, h, w = im.shape
            hp, wp = (h // P, w // P)
            patches = im.reshape(b, c, hp, P, wp, P)
            x = jnp.einsum('bchpwq,dcpq->bhwd', patches, conv_w)
            x = x.reshape(b, hp * wp, -1) + conv_b
            n = hp * wp
            scale = DH ** (-0.5)
            for i in range(ln1_g.shape[0]):
                y = _ln(x, ln1_g[i], ln1_b[i])
                qkv = y @ qkv_w[i]
                q, k, v = jnp.split(qkv, 3, axis=-1)
                to_heads = lambda t: t.reshape(b, n, NH, DH).transpose(0, 2, 1, 3)
                q, k, v = (to_heads(q), to_heads(k), to_heads(v))
                q = jax.nn.softmax(q, axis=-1) * scale
                k = jax.nn.softmax(k, axis=-2)
                ctx = jnp.einsum('bhnd,bhne->bhde', k, v)
                att = jnp.einsum('bhnd,bhde->bhne', q, ctx)
                att = att.transpose(0, 2, 1, 3).reshape(b, n, INNER)
                x = x + att @ out_w[i] + out_b[i]
                y = _ln(x, ln2_g[i], ln2_b[i])
                hdn = jax.nn.gelu(y @ ff1_w[i] + ff1_b[i], approximate=False)
                x = x + hdn @ ff2_w[i] + ff2_b[i]
            return _ln(x, lnf_g, lnf_b) @ head_w + head_b
        return _forward(im, conv_w, conv_b, ln1_g, ln1_b, qkv_w, out_w, out_b, ln2_g, ln2_b, ff1_w, ff1_b, ff2_w, ff2_b, lnf_g, lnf_b, head_w, head_b)

    def _L0_attn_ref(x, conv_w, conv_b, mem_Wq, mem_Wk, mem_Wv, mem_Wg_w, mem_Wg_b, mem_Wout, gate_w, router_w, router_b, mixg_w, mixg_b, mix_w, mix_b):
        import jax, jax.numpy as jnp
        import numpy as np
        DILATIONS = [(1, 2, 4), (1, 1, 1), (4, 8, 16), (8, 16, 32), (32, 64, 128), (64, 128, 64), (64, 128, 256), (1, 100, 200), (1, 125, 250), (1, 256, 512), (3, 9, 27), (5, 25, 125)]
        MEM_HEADS = (6, 7, 8, 9)
        NUM_HEADS = 12
        HIDDEN = 192
        HEAD_DIM = HIDDEN // NUM_HEADS
        KSZ = 4
        MEM_DIM = 128
        STRIDE = 64

        def causal_dconv(h, w, b, dilation):
            pad = (KSZ - 1) * dilation
            hp = jnp.pad(h, ((0, 0), (0, 0), (pad, 0)))
            out = jax.lax.conv_general_dilated(hp, w[:, None, :], window_strides=(1,), padding='VALID', rhs_dilation=(dilation,), dimension_numbers=('NCH', 'OIH', 'NCH'), feature_group_count=h.shape[1])
            return out + b[None, :, None]

        def neural_memory(x, Wq, Wk, Wv, Wg_w, Wg_b, Wout):
            B, S, D = x.shape
            q = x @ Wq.T
            k = x @ Wk.T
            v = x @ Wv.T
            g = jax.nn.sigmoid(x @ Wg_w.T + Wg_b)
            nC = S // STRIDE
            qc = q.reshape(B, nC, STRIDE, D).transpose(1, 0, 2, 3)
            kc = k.reshape(B, nC, STRIDE, D).transpose(1, 0, 2, 3)
            vc = v.reshape(B, nC, STRIDE, MEM_DIM).transpose(1, 0, 2, 3)
            gc = g.reshape(B, nC, STRIDE, 1).transpose(1, 0, 2, 3)

            def step(M, inp):
                qi, ki, vi, gi = inp
                reads = jnp.einsum('bsd,bdm->bsm', qi, M)
                write = jnp.einsum('bsd,bsm->bdm', ki * gi, vi)
                avg_gate = gi.mean(axis=1, keepdims=True)
                return ((1.0 - avg_gate) * M + write, reads)
            M0 = jnp.zeros((B, D, MEM_DIM), x.dtype)
            _, reads = jax.lax.scan(step, M0, (qc, kc, vc, gc))
            reads = reads.transpose(1, 0, 2, 3).reshape(B, S, MEM_DIM)
            return reads @ Wout.T
        B, S, H = x.shape
        head_weights = jax.nn.sigmoid(x @ router_w.T + router_b)
        gp = x @ gate_w.T
        x_gated, gate = jnp.split(gp, 2, axis=-1)
        x_gated = x_gated * jax.nn.sigmoid(gate)
        xh = x_gated.reshape(B, S, NUM_HEADS, HEAD_DIM)
        mem_idx = {h: i for i, h in enumerate(MEM_HEADS)}
        outs = []
        for i in range(NUM_HEADS):
            h = xh[:, :, i, :].transpose(0, 2, 1)
            for j, d in enumerate(DILATIONS[i]):
                h = h + causal_dconv(h, conv_w[i, j], conv_b[i, j], d)
            h = h.transpose(0, 2, 1)
            if i in mem_idx:
                m = mem_idx[i]
                h = h + neural_memory(xh[:, :, i, :], mem_Wq[m], mem_Wk[m], mem_Wv[m], mem_Wg_w[m], mem_Wg_b[m], mem_Wout[m])
            h = h * head_weights[:, :, i:i + 1]
            outs.append(h)
        out = jnp.concatenate(outs, axis=-1)
        out = out * jax.nn.sigmoid(out @ mixg_w.T + mixg_b)
        return out @ mix_w.T + mix_b

    def _L0_ffn_ref(x, w_fc, b_fc, w_proj, b_proj, alpha_e, alpha_r):
        import math
        import jax, jax.numpy as jnp
        import numpy as np
        EMBED_CHOICES = [96, 144, 192]
        RATIO_CHOICES = [2, 3, 4]
        E_MAX = 192
        H_MAX = 768

        def new_gelu(x):
            c = math.sqrt(2.0 / math.pi)
            return 0.5 * x * (1.0 + jnp.tanh(c * (x + 0.044715 * x * x * x)))

        def _mixed_coeffs(alpha_e, alpha_r):
            h_idx = jnp.arange(H_MAX)
            d_idx = jnp.arange(E_MAX)
            C0 = jnp.zeros((H_MAX, E_MAX), jnp.float32)
            c0b = jnp.zeros((H_MAX,), jnp.float32)
            C1 = jnp.zeros((E_MAX, H_MAX), jnp.float32)
            c1b = jnp.zeros((E_MAX,), jnp.float32)
            for i, e in enumerate(EMBED_CHOICES):
                m_in = (d_idx < e).astype(jnp.float32)
                for j, r in enumerate(RATIO_CHOICES):
                    a = alpha_e[i] * alpha_r[j]
                    m_out = (h_idx < r * e).astype(jnp.float32)
                    C0 = C0 + a * (m_out[:, None] * m_in[None, :])
                    c0b = c0b + a * m_out
                    C1 = C1 + a * (m_in[:, None] * m_out[None, :])
                    c1b = c1b + a * m_in
            return (C0, c0b, C1, c1b)
        C0, c0b, C1, c1b = _mixed_coeffs(alpha_e, alpha_r)
        W0 = w_fc * C0
        b0 = b_fc * c0b
        h = jnp.einsum('bte,he->bth', x, W0) + b0
        h = new_gelu(h)
        W1 = w_proj * C1
        b1 = b_proj * c1b
        out = jnp.einsum('bth,eh->bte', h, W1) + b1
        return out

    def _L1_attn_ref(x, w_qkv, w_proj, b_proj):
        import jax, jax.numpy as jnp
        import numpy as np
        NUM_HEADS = 12
        NUM_LANDMARKS = 64

        def iterative_inv(K, n_iter=6):
            I = jnp.eye(K.shape[-1], dtype=K.dtype)
            denom = jnp.max(jnp.sum(K, axis=-2), axis=-1)[..., None, None]
            V = jnp.swapaxes(K, -1, -2) / denom
            for _ in range(n_iter):
                KV = K @ V
                V = 0.25 * V @ (13.0 * I - KV @ (15.0 * I - KV @ (7.0 * I - KV)))
            return V
        B, N, C = x.shape
        H, L = (NUM_HEADS, NUM_LANDMARKS)
        D = C // H
        scale = D ** 0.5
        qkv = (x @ w_qkv).reshape(B, N, 3, H, D)
        qkv = jnp.transpose(qkv, (2, 0, 3, 1, 4))
        Q, K, V = (qkv[0] / scale, qkv[1], qkv[2])
        segs = N // L
        K_lm = K.reshape(B, H, L, segs, D).mean(axis=-2)
        Q_lm = Q.reshape(B, H, L, segs, D).mean(axis=-2)
        kernel1 = jax.nn.softmax(jnp.einsum('bhnd,bhld->bhnl', Q, K_lm), axis=-1)
        kernel2 = jax.nn.softmax(jnp.einsum('bhld,bhmd->bhlm', Q_lm, K_lm), axis=-1)
        kernel3 = jax.nn.softmax(jnp.einsum('bhld,bhnd->bhln', Q_lm, K), axis=-1)
        SV = kernel1 @ iterative_inv(kernel2) @ (kernel3 @ V)
        SV = jnp.transpose(SV, (0, 2, 1, 3)).reshape(B, N, C)
        out = SV @ w_proj + b_proj
        out = out + jnp.transpose(V, (0, 2, 1, 3)).reshape(B, N, C)
        return out

    def _L1_ffn_ref(x, gate_w, w1, b1, w2, b2):
        import jax, jax.numpy as jnp
        import numpy as np
        TOP_K = 2
        B, S, D = x.shape
        E, _, H = w1.shape
        T = B * S
        K = TOP_K
        xf = x.reshape(T, D)
        logits = xf @ gate_w.T
        probs = jax.nn.softmax(logits, axis=-1)
        top_w, top_i = jax.lax.top_k(probs, K)
        top_w = top_w / (jnp.sum(top_w, axis=-1, keepdims=True) + 1e-09)
        flat_e = top_i.reshape(-1)
        flat_w = top_w.reshape(-1)
        tok_idx = jnp.repeat(jnp.arange(T), K)
        order = jnp.argsort(flat_e)
        se = flat_e[order]
        pt = tok_idx[order]
        pw = flat_w[order]
        counts = jax.ops.segment_sum(jnp.ones(T * K, jnp.int32), se, num_segments=E)
        starts = jnp.concatenate([jnp.zeros((1,), jnp.int32), jnp.cumsum(counts)[:-1]])
        pos = jnp.arange(T * K) - starts[se]
        cap = T * K
        padded = jnp.zeros((E, cap, D), x.dtype).at[se, pos].set(xf[pt])
        hidden = jax.nn.gelu(jnp.einsum('ecd,edh->ech', padded, w1) + b1[:, None, :], approximate=False)
        out = jnp.einsum('ech,ehd->ecd', hidden, w2) + b2[:, None, :]
        expert_out = out[se, pos] * pw[:, None]
        final = jnp.zeros((T, D), x.dtype).at[pt].add(expert_out)
        return final.reshape(B, S, D)

    def _L2_attn_ref(x, w0, w1, w2):
        import jax, jax.numpy as jnp
        import numpy as np
        HIDDEN = 192
        TTT_HIDDEN = 512
        CHUNK = 128
        SEQ = 2048
        BATCH = 4
        LR = 0.01

        def _fast_weight(xc, w0, w1, w2):
            return jax.nn.silu(xc @ w0) * (xc @ w2) @ w1

        def _reference_tuple_inner(x, w0, w1, w2):
            b, s, h = x.shape
            num_chunks = s // CHUNK
            x_chunks = x.reshape(b, num_chunks, CHUNK, h).transpose(1, 0, 2, 3)

            def process_chunk(carry, x_chunk):
                cw0, cw1, cw2, acc_loss = carry
                chunk_output = _fast_weight(x_chunk, cw0, cw1, cw2)

                def loss_fn(a0, a1, a2):
                    out = _fast_weight(x_chunk, a0, a1, a2)
                    return jnp.mean((out - x_chunk) ** 2)
                chunk_loss, (g0, g1, g2) = jax.value_and_grad(loss_fn, argnums=(0, 1, 2))(cw0, cw1, cw2)
                new_carry = (cw0 - LR * g0, cw1 - LR * g1, cw2 - LR * g2, acc_loss + chunk_loss)
                return (new_carry, chunk_output)
            init = (w0, w1, w2, jnp.float32(0.0))
            (_, _, _, total_loss), ys = jax.lax.scan(process_chunk, init, x_chunks)
            output = ys.transpose(1, 0, 2, 3).reshape(b, s, h)
            ttt_loss = total_loss / num_chunks
            return (output, ttt_loss)
        return _reference_tuple_inner(x, w0, w1, w2)[0]

    def _L2_ffn_ref(x, ln_w, w_router, wi, wo):
        import jax, jax.numpy as jnp
        import numpy as np
        B, S, D, F, E = (8, 512, 192, 768, 16)
        CAP = 64
        EPS = 1e-06

        def _switch_moe_block(x, ln_w, w_router, wi, wo):
            var = jnp.mean(jnp.square(x.astype(jnp.float32)), axis=-1, keepdims=True)
            normed = (x * jax.lax.rsqrt(var + EPS)).astype(x.dtype) * ln_w
            logits = jnp.einsum('bsd,de->bse', normed.astype(jnp.float32), w_router.astype(jnp.float32))
            probs = jax.nn.softmax(logits, axis=-1)
            expert_idx = jnp.argmax(probs, axis=-1)
            onehot = jax.nn.one_hot(expert_idx, E, dtype=jnp.float32)
            priority = jnp.cumsum(onehot, axis=1)
            keep = onehot * (priority <= CAP)
            pos = (priority - 1.0).astype(jnp.int32)
            dispatch = keep[..., None] * jax.nn.one_hot(pos, CAP, dtype=jnp.float32)
            expert_in = jnp.einsum('bsec,bsd->becd', dispatch, normed)
            h = jax.nn.relu(jnp.einsum('becd,edf->becf', expert_in, wi))
            expert_out = jnp.einsum('becf,efd->becd', h, wo)
            combined = jnp.einsum('bsec,becd->bsd', dispatch, expert_out)
            routed = jnp.sum(dispatch, axis=(2, 3)) > 0
            next_states = jnp.where(routed[..., None], combined.astype(x.dtype), normed)
            router_prob = jnp.max(probs, axis=-1, keepdims=True).astype(x.dtype)
            return x + router_prob * next_states
        return _switch_moe_block(x, ln_w, w_router, wi, wo)

    def _L3_attn_ref(x_q, w_qkv, b_qkv, w_out, b_out):
        import jax, jax.numpy as jnp
        import numpy as np
        EMBED_DIM = 192
        NUM_HEADS = 12
        HEAD_DIM = EMBED_DIM // NUM_HEADS
        SCALING = HEAD_DIM ** (-0.5)
        B, N = (4, 512)
        b_sz, n, _ = x_q.shape
        qkv = jnp.einsum('bne,fe->bnf', x_q, w_qkv) + b_qkv
        qkv = qkv.reshape(b_sz, n, 3, NUM_HEADS, HEAD_DIM).transpose(0, 3, 2, 1, 4)
        q, k, v = (qkv[:, :, 0], qkv[:, :, 1], qkv[:, :, 2])
        q = q * SCALING
        attn = jnp.einsum('bhqd,bhkd->bhqk', q, k) + 1.0
        attn = jax.nn.softmax(attn, axis=-1)
        out = jnp.einsum('bhqk,bhkd->bhqd', attn, v)
        out = out.transpose(0, 2, 1, 3).reshape(b_sz, n, EMBED_DIM)
        return jnp.einsum('bne,fe->bnf', out, w_out) + b_out

    def _L3_ffn_ref(hidden_states, ln_gamma, ln_beta, router_w, w1, w2):
        import jax, jax.numpy as jnp
        import numpy as np
        D_MODEL, D_FF, N_EXPERTS, TOP_K = (192, 768, 8, 2)
        B, S = (2, 256)
        LN_EPS = 1e-05

        def _layernorm(x, gamma, beta):
            mu = jnp.mean(x, axis=-1, keepdims=True)
            var = jnp.mean(jnp.square(x - mu), axis=-1, keepdims=True)
            return (x - mu) * jax.lax.rsqrt(var + LN_EPS) * gamma + beta
        Bz, Sz, D = hidden_states.shape
        residual = hidden_states
        x = _layernorm(hidden_states, ln_gamma, ln_beta)
        tokens = x.reshape(-1, D)
        T = tokens.shape[0]
        logits = tokens @ router_w
        probs = jax.nn.softmax(logits, axis=-1)
        topw, topi = jax.lax.top_k(probs, TOP_K)
        topw = topw / jnp.sum(topw, axis=-1, keepdims=True)
        gates = jnp.zeros((T, N_EXPERTS), dtype=tokens.dtype)
        gates = gates.at[jnp.arange(T)[:, None], topi].set(topw)
        h = jnp.einsum('td,edf->etf', tokens, w1)
        h = jax.nn.silu(h)
        y = jnp.einsum('etf,efd->etd', h, w2)
        out = jnp.einsum('te,etd->td', gates, y)
        return residual + out.reshape(Bz, Sz, D)
    h = _L0_tok_ref(x, L0_tok_conv_w, L0_tok_conv_b, L0_tok_ln1_g, L0_tok_ln1_b, L0_tok_qkv_w, L0_tok_out_w, L0_tok_out_b, L0_tok_ln2_g, L0_tok_ln2_b, L0_tok_ff1_w, L0_tok_ff1_b, L0_tok_ff2_w, L0_tok_ff2_b, L0_tok_lnf_g, L0_tok_lnf_b, L0_tok_head_w, L0_tok_head_b)
    h = h + _L0_attn_ref(_layernorm(h, axis=-1), L0_attn_conv_w, L0_attn_conv_b, L0_attn_mem_Wq, L0_attn_mem_Wk, L0_attn_mem_Wv, L0_attn_mem_Wg_w, L0_attn_mem_Wg_b, L0_attn_mem_Wout, L0_attn_gate_w, L0_attn_router_w, L0_attn_router_b, L0_attn_mixg_w, L0_attn_mixg_b, L0_attn_mix_w, L0_attn_mix_b)
    h = h + _L0_ffn_ref(_layernorm(h, axis=-1), L0_ffn_w_fc, L0_ffn_b_fc, L0_ffn_w_proj, L0_ffn_b_proj, L0_ffn_alpha_e, L0_ffn_alpha_r)
    h = h + _L1_attn_ref(_layernorm(h, axis=-1), L1_attn_w_qkv, L1_attn_w_proj, L1_attn_b_proj)
    h = h + _L1_ffn_ref(_layernorm(h, axis=-1), L1_ffn_gate_w, L1_ffn_w1, L1_ffn_b1, L1_ffn_w2, L1_ffn_b2)
    h = h + _L2_attn_ref(_layernorm(h, axis=-1), L2_attn_w0, L2_attn_w1, L2_attn_w2)
    h = h + _L2_ffn_ref(_layernorm(h, axis=-1), L2_ffn_ln_w, L2_ffn_w_router, L2_ffn_wi, L2_ffn_wo)
    h = h + _L3_attn_ref(_layernorm(h, axis=-1), L3_attn_w_qkv, L3_attn_b_qkv, L3_attn_w_out, L3_attn_b_out)
    h = h + _L3_ffn_ref(_layernorm(h, axis=-1), L3_ffn_ln_gamma, L3_ffn_ln_beta, L3_ffn_router_w, L3_ffn_w1, L3_ffn_w2)
    return h

_drawn_inputs = setup_inputs


def setup_inputs(seed=0):
    import zlib

    import numpy as np

    out = dict(_drawn_inputs(seed))
    spreads = {'L0_tok_conv_b': (0.0, 0.1),
     'L0_tok_ln1_g': (1.0, 0.6),
     'L0_tok_ln1_b': (0.0, 0.76),
     'L0_tok_out_b': (0.0, 0.1),
     'L0_tok_ln2_g': (1.0, 0.587),
     'L0_tok_ln2_b': (0.0, 0.454),
     'L0_tok_ff1_b': (0.0, 0.1),
     'L0_tok_ff2_b': (0.0, 0.1),
     'L0_tok_lnf_g': (1.0, 0.2),
     'L0_tok_lnf_b': (0.0, 0.1),
     'L0_tok_head_b': (0.0, 0.1),
     'L0_attn_mem_Wg_b': (-2.0, 0.6),
     'L0_attn_router_b': (0.0, 0.629),
     'L0_attn_mixg_b': (2.0, 0.6),
     'L0_attn_mix_b': (0.0, 0.1),
     'L0_ffn_b_fc': (0.0, 0.1),
     'L0_ffn_b_proj': (0.0, 0.1),
     'L1_ffn_b1': (0.0, 0.1),
     'L1_ffn_b2': (0.0, 0.1),
     'L2_ffn_ln_w': (1.0, 0.557),
     'L3_ffn_ln_gamma': (1.0, 0.6),
     'L3_ffn_ln_beta': (0.0, 0.8)}
    factors = {'L0_tok_qkv_w': 5.927,
     'L0_tok_out_w': 5.432,
     'L0_attn_conv_b': 2.976,
     'L0_attn_mem_Wq': 64.0,
     'L0_attn_mem_Wk': 64.0,
     'L0_attn_mem_Wv': 64.0,
     'L0_attn_mem_Wg_w': 64.0,
     'L0_attn_mem_Wout': 64.0,
     'L0_attn_router_w': 3.095,
     'L0_attn_mixg_w': 47.56,
     'L3_ffn_router_w': 2.787}
    for name, (base, spread) in spreads.items():
        noise = np.random.default_rng([zlib.crc32(name.encode()), seed]).standard_normal(out[name].shape)
        drawn = base * np.exp(spread * noise) if base else spread * noise
        out[name] = jnp.asarray(drawn.astype(out[name].dtype))
    for name, factor in factors.items():
        out[name] = (out[name] * factor).astype(out[name].dtype)
    return out
```

```python
from contextlib import ExitStack, contextmanager

import numpy as np

import concourse.bass as bass
from concourse import mybir
from concourse.alu_op_type import AluOpType as ALU

F32 = mybir.dt.float32
ACT = mybir.ActivationFunctionType
AX = mybir.AxisListType

P = 128
B, N = 4, 256
T = B * N
NT = T // P
TPB = N // P
D = 192
HF = D // 2
DT = 128
HD = 16
NH = 12
SLOT = 32
HG = 3
LM = 64
FF = 768
FT = FF // P
BANK = 512
NB = 8


class Steps:

    def __init__(self, eng, sem):
        self.eng, self.sem, self.n = eng, sem, 0

    def mark(self, ins):
        ins.then_inc(self.sem, 1)
        self.n += 1
        return self.n

    def then(self, ins):
        self.eng.wait_ge(self.sem, self.mark(ins))


class Jobs:

    def __init__(self, core, sems, order, banks=None):
        self.core, self.sems, self.order = core, sems, order
        self.banks = banks or list(range(NB))
        self.index = {key: k for k, (key, _) in enumerate(order)}
        assert len(self.index) == len(order)

    def bank(self, key):
        return self.core.bank[self.banks[self.index[key] % len(self.banks)]]

    def taken(self, key):
        k = self.index[key]
        who = self.order[k][1]
        count = sum(1 for _, w in self.order[:k + 1] if w == who)
        return (self.sems["vector_took"] if who == "v" else self.sems["scalar_took"]), count

    def bank_free(self, pe, key):
        k = self.index[key] - len(self.banks)
        if k >= 0:
            pe.wait_ge(*self.taken(self.order[k][0]))

    def ready(self, key):
        return self.sems["product_ready"], self.index[key] + 1

    def by(self, who):
        return [key for key, w in self.order if w == who]


@contextmanager
def stage(nc, names):
    with ExitStack() as ctx:
        made = {n: ctx.enter_context(nc.semaphore(n + f"_{nc.get_next_instruction_name()}")) for n in names.split()}
        with nc.Block(no_gpsimd_drain=True) as block:
            yield block, made
        nc.gpsimd.drain()
        for n in names.split():
            nc.gpsimd.sem_clear(made[n])
        nc.all_engine_barrier()


JOB_SEMS = "product_ready vector_took scalar_took vector_step scalar_step "
PATCH_SEMS = " ".join(f"patch{k}" for k in range(16))


class Core:

    def __init__(self, nc, ctx):
        self.nc, self.ctx = nc, ctx
        self.psum = ctx.enter_context(nc.psum_tensor("psum", [P, NB, BANK], F32))
        self.bank = [self.psum[:, i, :] for i in range(NB)]

        self.counter = 0

    def uid(self):
        self.counter += 1
        return self.counter

    def sb(self, name, shape, scope=None):
        return (scope or self.ctx).enter_context(self.nc.sbuf_tensor(name, shape, F32))

    def allocate(self):
        self.H = self.sb("residual", [P, NT, D])
        self.XN = self.sb("normed", [P, NT, D])
        self.XT = self.sb("normedT", [HF, 2, T])
        self.ident = self.sb("ident", [P, P])
        self.eps = self.sb("eps", [P, 2])
        self.eps5, self.eps6 = self.eps[:, 0:1], self.eps[:, 1:2]
        self.rows = self.sb("rows", [P, ROW_LEN])
        self.cols = self.sb("cols", [P, COL_LEN])
        self.ffn_b0 = self.sb("ffn_b0", [P, FT])
        self.ffn_b1 = self.sb("ffn_b1", [P, D])
        self.pick_top = self.sb("pick_top", [P, NT])
        self.rank = self.sb("rank", [P, 16])
        self.rows_in = self.ctx.enter_context(self.nc.semaphore("rows_in"))
        self.cols_in = self.ctx.enter_context(self.nc.semaphore("cols_in"))
        self.weights_in, self.tile = {}, {}

    def allocate_weights(self, names, scope):
        for name in names:
            self.tile[name] = self.sb(name, list(self.w[name].shape), scope)
            self.weights_in[name] = self.ctx.enter_context(self.nc.semaphore(name + "_in"))

    def load_weights(self, sp, names):
        for name in names:
            tile, src = self.tile[name], self.w[name]
            sp.dma_start(tile[tuple(slice(None) for _ in src.shape)], src).then_inc(self.weights_in[name], 16)

    def row(self, name):
        at, n = ROW_AT[name]
        return self.rows[:, at:at + n]

    def col(self, name):
        at, n = COL_AT[name]
        return self.cols[:, at:at + n]


def halves(width):
    return [(0, DT)] if width == DT else [(0, HF), (HF, HF)]


def norm_and_turn(c, X, XN, XT, width, eps, gain=None, shift=None, sync=None):
    nc = c.nc
    parts = halves(width)
    HT = NT // 2
    with ExitStack() as mem:
        stats = mem.enter_context(nc.sbuf_tensor(f"stats{c.uid()}", [P, NT, 6], F32))
        mv = mem.enter_context(nc.sbuf_tensor(f"mv{c.uid()}", [P, NT, 2], F32))
        rstd = mem.enter_context(nc.sbuf_tensor(f"rstd{c.uid()}", [P, 2, NT], F32))
        with stage(nc, JOB_SEMS + "stats_done moments_done std_ready row_normed") as (block, s):
            order = [((g, p), "sv"[p]) for g in range(2) for p in range(len(parts))]
            jobs = Jobs(c, s, order)
            if sync:
                block.sync(sync)

            @block.vector
            def _(dve):
                step = Steps(dve, s["vector_step"])
                for t in range(NT):
                    nc.vector.bn_stats(stats[:, t, :], X[:, t, 0:width]).then_inc(s["stats_done"], 1)
                for t in range(NT):
                    dve.wait_ge(s["stats_done"], t + 1)
                    nc.vector.bn_aggr(mv[:, t, :], stats[:, t, :]).then_inc(s["moments_done"], 1)
                dve.wait_ge(s["std_ready"], 1)
                step.then(nc.vector.reciprocal(rstd[:, 1, :], rstd[:, 0, :]))
                for t in range(NT):
                    nc.vector.tensor_scalar(XN[:, t, 0:width], X[:, t, 0:width], mv[:, t, 0:1], rstd[:, 1, t:t + 1],
                                            ALU.subtract, ALU.mult).then_inc(s["row_normed"], 1)
                for g, p in jobs.by("v"):
                    n = parts[p][1]
                    dve.wait_ge(*jobs.ready((g, p)))
                    dst, src = XT[0:n, p, g * BANK:(g + 1) * BANK], jobs.bank((g, p))[0:n, :]
                    if gain is None:
                        nc.vector.tensor_copy(dst, src).then_inc(s["vector_took"], 1)
                    else:
                        nc.vector.tensor_scalar(dst, src, gain[0:n, p:p + 1], shift[0:n, p:p + 1],
                                                ALU.mult, ALU.add).then_inc(s["vector_took"], 1)

            @block.scalar
            def _(act):
                act.wait_ge(s["moments_done"], NT)
                nc.scalar.activation(rstd[:, 0, :], mv[:, :, 1], ACT.Sqrt, bias=eps).then_inc(s["std_ready"], 1)
                for g, p in jobs.by("s"):
                    n = parts[p][1]
                    act.wait_ge(*jobs.ready((g, p)))
                    dst, src = XT[0:n, p, g * BANK:(g + 1) * BANK], jobs.bank((g, p))[0:n, :]
                    if gain is None:
                        nc.scalar.copy(dst, src).then_inc(s["scalar_took"], 1)
                    else:
                        nc.scalar.activation(dst, src, ACT.Identity, bias=shift[0:n, p:p + 1],
                                             scale=gain[0:n, p:p + 1]).then_inc(s["scalar_took"], 1)

            @block.tensor
            def _(pe):
                for g, p in [key for key, _ in order]:
                    lo, n = parts[p]
                    pe.wait_ge(s["row_normed"], HT * (g + 1))
                    for i in range(HT):
                        last = pe.transpose(jobs.bank((g, p))[0:n, i * P:(i + 1) * P],
                                            XN[:, HT * g + i, lo:lo + n], c.ident[:, :])
                    last.then_inc(s["product_ready"], 1)


def tokenizer_patches(c, w):
    nc = c.nc
    STEPS = 16
    with ExitStack() as mem:
        patches = mem.enter_context(nc.sbuf_tensor("patches", [P, STEPS, T], F32))
        convw = mem.enter_context(nc.sbuf_tensor("convw", [P, STEPS, DT], F32))
        xT = mem.enter_context(nc.sbuf_tensor("patchT", [P, T], F32))
        c.choice = c.sb("choice", [P, 9], mem)
        c.coef_in, c.coef_hid = c.sb("coef_in", [HF, 2, FF], mem), c.sb("coef_hid", [P, FT, D], mem)
        with stage(nc, JOB_SEMS + "convw_in pool_step " + PATCH_SEMS) as (block, s):
            arrived = [s["patch0"], s["patch1"], s["patch2"], s["patch3"], s["patch4"], s["patch5"], s["patch6"], s["patch7"], s["patch8"], s["patch9"],
                       s["patch10"], s["patch11"], s["patch12"], s["patch13"], s["patch14"], s["patch15"]]
            order = [(("conv", g), "vs"[g]) for g in range(2)] + [(("turn", g), "v") for g in range(2)]
            jobs = Jobs(c, s, order)

            @block.gpsimd
            def _(pool):
                pool.wait_ge(c.rows_in, 16)
                mask_entangled_ffn(c, pool, Steps(pool, s["pool_step"]))

            @block.sync
            def _(sp):
                sp.dma_start(convw[:, :, :], w["conv_w"]).then_inc(s["convw_in"], 16)
                for k in range(0, STEPS, 2):
                    sp.dma_start(patches[:, k, :], w["patches"][:, k, :]).then_inc(arrived[k], 16)
                c.load_weights(sp, TOK + EARLY)

            @block.scalar
            def _(act):
                for k in range(1, STEPS, 2):
                    act.dma_start(patches[:, k, :], w["patches"][:, k, :]).then_inc(arrived[k], 16)
                act.wait_ge(*jobs.ready(("conv", 1)))
                nc.scalar.copy(xT[:, BANK:], jobs.bank(("conv", 1))).then_inc(s["scalar_took"], 1)

            @block.tensor
            def _(pe):
                pe.wait_ge(s["convw_in"], 16)
                for k in range(STEPS):
                    pe.wait_ge(arrived[k], 16)
                    for g in range(2):
                        last = pe.matmul(jobs.bank(("conv", g)), convw[:, k, :],
                                         patches[:, k, g * BANK:(g + 1) * BANK],
                                         start=(k == 0), stop=(k == STEPS - 1))
                        if k == STEPS - 1:
                            last.then_inc(s["product_ready"], 1)
                for g in range(2):
                    pe.wait_ge(*jobs.taken(("conv", g)))
                    for i in range(4):
                        last = pe.transpose(jobs.bank(("turn", g))[:, i * P:(i + 1) * P],
                                            xT[:, g * BANK + i * P:g * BANK + (i + 1) * P], c.ident[:, :])
                    last.then_inc(s["product_ready"], 1)

            @block.vector
            def _(dve):
                dve.wait_ge(*jobs.ready(("conv", 0)))
                nc.vector.tensor_copy(xT[:, 0:BANK], jobs.bank(("conv", 0))).then_inc(s["vector_took"], 1)
                dve.wait_ge(c.rows_in, 16)
                for g in range(2):
                    dve.wait_ge(*jobs.ready(("turn", g)))
                    nc.vector.tensor_tensor(
                        c.X[:, 4 * g:4 * g + 4, 0:DT], jobs.bank(("turn", g)).rearrange("p (t d) -> p t d", d=DT),
                        c.row("conv_b").unsqueeze(1).to_broadcast([P, 4, DT]), ALU.add).then_inc(s["vector_took"], 1)


def tokenizer_attention(c, layer):
    nc = c.nc
    DH, M4 = 64, 4
    INNER = 512
    qkv, out_w = c.tile["tok_qkv"][:, layer, :], c.tile["tok_out"][:, layer]
    with ExitStack() as mem:
        def sb(name, shape):
            return mem.enter_context(nc.sbuf_tensor(name + str(layer), shape, F32))
        qshift, qexp = sb("qshift", [P, 2, INNER]), sb("qexp", [P, 2, INNER])
        qmax, qsum, qinv = sb("qmax", [P, NT, 8]), sb("qsum", [P, NT, 8]), sb("qinv", [P, NT, 8])
        kmax, ksum, kinv = sb("kmax", [P, M4, B]), sb("ksum", [P, M4, B]), sb("kinv", [P, M4, B])
        kexp = sb("kexp", [P, M4, T])
        ktok = sb("ktok", [P, NT, INNER])
        vtok = sb("vtok", [P, NT, INNER])
        qT = sb("qT", [P, M4, T])
        ctx = sb("ctxbd", [P, B, M4, P])
        qprob = sb("qprob", [P, NT, INNER])
        attT = kexp
        ks = [("k", m, g) for m in range(M4) for g in range(2)]
        order = [(k, "s") for k in ks]
        for t in range(NT):
            order += [(("q", t), "v"), (("v", t), "s")]
        order += [(("kt", t), "s") for t in range(NT)]
        order += [(("qt", t), "v") for t in range(NT)]
        order += [(("ctx", b), "v") for b in range(B)]
        order += [(("att", b, h), "sv"[h]) for b in range(B) for h in range(2)]
        order += [(("out", g), "v") for g in range(2)]
        with stage(nc, JOB_SEMS + "kmax_ready ctx_zero q_exped q_normed") as (block, s):
            jobs = Jobs(c, s, order)

            @block.gpsimd
            def _(pool):
                nc.gpsimd.memset(ctx[:, :, :, :], 0.0).then_inc(s["ctx_zero"], 1)

            @block.tensor
            def _(pe):
                if layer == 0:
                    for name in TOK:
                        pe.wait_ge(c.weights_in[name], 16)
                for key, _ in order:
                    kind, bank = key[0], jobs.bank(key)
                    jobs.bank_free(pe, key)
                    if kind == "k":
                        _, m, g = key
                        last = pe.matmul(bank, qkv[:, INNER + m * P:INNER + (m + 1) * P],
                                         c.YT[:, 0, g * BANK:(g + 1) * BANK], start=True, stop=True)
                    elif kind in "qv":
                        t = key[1]
                        lo = 0 if kind == "q" else 2 * INNER
                        last = pe.matmul(bank, c.YT[:, 0, t * P:(t + 1) * P], qkv[:, lo:lo + INNER],
                                         start=True, stop=True)
                    elif kind == "kt":
                        t = key[1]
                        pe.wait_ge(s["scalar_took"], 8)
                        for m in range(M4):
                            last = pe.transpose(bank[:, m * P:(m + 1) * P], kexp[:, m, t * P:(t + 1) * P],
                                                c.ident[:, :])
                    elif kind == "qt":
                        t = key[1]
                        pe.wait_ge(s["q_normed"], t + 1)
                        for m in range(M4):
                            last = pe.transpose(bank[:, m * P:(m + 1) * P], qprob[:, t, m * P:(m + 1) * P],
                                                c.ident[:, :])
                    elif kind == "ctx":
                        b = key[1]
                        pe.wait_ge(*jobs.taken(("kt", TPB * b + 1)))
                        for m in range(M4):
                            for i in range(TPB):
                                t = TPB * b + i
                                last = pe.matmul(bank[:, m * P:(m + 1) * P], ktok[:, t, m * P:(m + 1) * P],
                                                 vtok[:, t, m * P:(m + 1) * P], start=(i == 0), stop=(i == TPB - 1))
                    elif kind == "att":
                        _, b, h = key
                        pe.wait_ge(*jobs.taken(("ctx", b)))
                        for i in range(2):
                            m = 2 * h + i
                            last = pe.matmul(bank[:, i * N:(i + 1) * N], ctx[:, b, m, :],
                                             qT[:, m, b * N:(b + 1) * N], start=True, stop=True)
                    else:
                        g = key[1]
                        pe.wait_ge(*jobs.taken(("att", 2 * g + 1, 0)))
                        pe.wait_ge(*jobs.taken(("att", 2 * g + 1, 1)))
                        for i in range(4):
                            t = 4 * g + i
                            for m in range(M4):
                                last = pe.matmul(bank[:, i * P:(i + 1) * P], attT[:, m, t * P:(t + 1) * P],
                                                 out_w[:, m, :], start=(m == 0), stop=(m == M4 - 1))
                    last.then_inc(s["product_ready"], 1)

            @block.scalar
            def _(act):
                for n, key in enumerate(ks):
                    _, m, g = key
                    act.wait_ge(s["kmax_ready"], n + 1)
                    for i in range(2):
                        b = 2 * g + i
                        last = nc.scalar.activation(kexp[:, m, b * N:(b + 1) * N], jobs.bank(key)[:, i * N:(i + 1) * N],
                                                    ACT.Exp, bias=kmax[:, m, b:b + 1], accum_out=ksum[:, m, b:b + 1])
                    last.then_inc(s["scalar_took"], 1)
                for t in range(NT):
                    act.wait_ge(*jobs.taken(("q", t)))
                    if t >= 2:
                        act.wait_ge(s["q_normed"], t - 1)
                    nc.scalar.activation(qexp[:, t % 2, :], qshift[:, t % 2, :], ACT.Exp).then_inc(s["q_exped"], 1)
                    act.wait_ge(*jobs.ready(("v", t)))
                    nc.scalar.copy(vtok[:, t, :], jobs.bank(("v", t))).then_inc(s["scalar_took"], 1)
                for t in range(NT):
                    act.wait_ge(*jobs.ready(("kt", t)))
                    nc.scalar.copy(ktok[:, t, :], jobs.bank(("kt", t))).then_inc(s["scalar_took"], 1)
                for b in range(B):
                    act.wait_ge(*jobs.ready(("att", b, 0)))
                    nc.scalar.copy(attT[:, 0:2, b * N:(b + 1) * N],
                                   jobs.bank(("att", b, 0)).rearrange("p (m n) -> p m n", m=2)).then_inc(s["scalar_took"], 1)

            @block.vector
            def _(dve):
                step = Steps(dve, s["vector_step"])
                for key in ks:
                    _, m, g = key
                    dve.wait_ge(*jobs.ready(key))
                    nc.vector.tensor_reduce(kmax[:, m, 2 * g:2 * g + 2],
                                            jobs.bank(key).rearrange("p (b n) -> p b n", b=2), AX.X, ALU.max,
                                            negate=True).then_inc(s["kmax_ready"], 1)

                def normalise_q(t):
                    dve.wait_ge(s["q_exped"], t + 1)
                    e = qexp[:, t % 2, :].rearrange("p (h d) -> p h d", d=DH)
                    step.then(nc.vector.tensor_reduce(qsum[:, t, :], e, AX.X, ALU.add))
                    step.then(nc.vector.reciprocal(qinv[:, t, :], qsum[:, t, :]))
                    nc.vector.scalar_tensor_tensor(
                        qprob[:, t, :].rearrange("p (h d) -> p h d", d=DH), e, DH ** -0.5,
                        qinv[:, t, :].unsqueeze(2).to_broadcast([P, 8, DH]), ALU.mult, ALU.mult).then_inc(s["q_normed"], 1)

                for t in range(NT):
                    dve.wait_ge(*jobs.ready(("q", t)))
                    q = jobs.bank(("q", t)).rearrange("p (h d) -> p h d", d=DH)
                    step.then(nc.vector.tensor_reduce(qmax[:, t, :], q, AX.X, ALU.max))
                    if t >= 2:
                        dve.wait_ge(s["q_exped"], t - 1)
                    nc.vector.tensor_tensor(qshift[:, t % 2, :].rearrange("p (h d) -> p h d", d=DH), q,
                                            qmax[:, t, :].unsqueeze(2).to_broadcast([P, 8, DH]),
                                            ALU.subtract).then_inc(s["vector_took"], 1)
                    if t >= 1:
                        normalise_q(t - 1)
                normalise_q(NT - 1)
                for t in range(NT):
                    dve.wait_ge(*jobs.ready(("qt", t)))
                    nc.vector.tensor_copy(qT[:, :, t * P:(t + 1) * P],
                                          jobs.bank(("qt", t)).rearrange("p (m n) -> p m n", m=M4)).then_inc(s["vector_took"], 1)
                dve.wait_ge(s["scalar_took"], 8)
                dve.wait_ge(s["ctx_zero"], 1)
                step.then(nc.vector.reciprocal(kinv[:, :, :], ksum[:, :, :]))
                for b in range(B):
                    dve.wait_ge(*jobs.ready(("ctx", b)))
                    for h in range(2):
                        r = slice(h * DH, (h + 1) * DH)
                        last = nc.vector.tensor_tensor(
                            ctx[r, b, :, r], jobs.bank(("ctx", b)).rearrange("p (m d) -> p m d", m=M4)[r, :, r],
                            kinv[r, :, b:b + 1].to_broadcast([DH, M4, DH]), ALU.mult)
                        if h == 1:
                            last.then_inc(s["vector_took"], 1)
                for b in range(B):
                    dve.wait_ge(*jobs.ready(("att", b, 1)))
                    nc.vector.tensor_copy(attT[:, 2:4, b * N:(b + 1) * N],
                                          jobs.bank(("att", b, 1)).rearrange("p (m n) -> p m n", m=2)).then_inc(s["vector_took"], 1)
                add_product_and_bias(c, dve, step, jobs, s, c.row(f"tok_out_b{layer}"))


def add_product_and_bias(c, dve, step, jobs, s, bias):
    nc = c.nc
    for g in range(2):
        dve.wait_ge(*jobs.ready(("out", g)))
        xs = c.X[:, 4 * g:4 * g + 4, 0:DT]
        step.then(nc.vector.tensor_tensor(xs, xs, jobs.bank(("out", g)).rearrange("p (t d) -> p t d", d=DT), ALU.add))
        nc.vector.tensor_tensor(xs, xs, bias.unsqueeze(1).to_broadcast([P, 4, DT]), ALU.add).then_inc(s["vector_took"], 1)


def tokenizer_ffn(c, layer):
    nc = c.nc
    M4 = 4
    ff1, ff2 = c.tile["tok_ff1"][:, layer, :], c.tile["tok_ff2"][:, layer]
    with ExitStack() as mem:
        hid = mem.enter_context(nc.sbuf_tensor(f"tokhid{layer}", [P, M4, T], F32))
        order = [(("h", m, g), "s") for g in range(2) for m in range(M4)] + [(("out", g), "v") for g in range(2)]
        with stage(nc, JOB_SEMS) as (block, s):
            jobs = Jobs(c, s, order)

            @block.tensor
            def _(pe):
                for key, _ in order:
                    bank = jobs.bank(key)
                    jobs.bank_free(pe, key)
                    if key[0] == "h":
                        _, m, g = key
                        last = pe.matmul(bank, ff1[:, m * P:(m + 1) * P], c.YT[:, 0, g * BANK:(g + 1) * BANK],
                                         start=True, stop=True)
                    else:
                        g = key[1]
                        pe.wait_ge(*jobs.taken(("h", M4 - 1, g)))
                        for i in range(4):
                            t = 4 * g + i
                            for m in range(M4):
                                last = pe.matmul(bank[:, i * P:(i + 1) * P], hid[:, m, t * P:(t + 1) * P], ff2[:, m, :],
                                                 start=(m == 0), stop=(m == M4 - 1))
                    last.then_inc(s["product_ready"], 1)

            @block.scalar
            def _(act):
                for key in jobs.by("s"):
                    _, m, g = key
                    act.wait_ge(*jobs.ready(key))
                    b = c.col(f"tok_ff1_b{layer}")[:, m:m + 1]
                    nc.scalar.activation(hid[:, m, g * BANK:(g + 1) * BANK], jobs.bank(key), ACT.Gelu,
                                         bias=b).then_inc(s["scalar_took"], 1)

            @block.vector
            def _(dve):
                step = Steps(dve, s["vector_step"])
                add_product_and_bias(c, dve, step, jobs, s, c.row(f"tok_ff2_b{layer}"))


def tokenizer_head(c):
    nc = c.nc
    order = [(("head", t), "v") for t in range(0, NT, 2)]
    with stage(nc, JOB_SEMS) as (block, s):
        jobs = Jobs(c, s, order)

        @block.tensor
        def _(pe):
            for key, _ in order:
                for i in range(2):
                    t = key[1] + i
                    last = pe.matmul(jobs.bank(key)[:, i * D:(i + 1) * D], c.YT[:, 0, t * P:(t + 1) * P], c.tile["head_w"][:, :],
                                     start=True, stop=True)
                last.then_inc(s["product_ready"], 1)

        @block.vector
        def _(dve):
            for key in jobs.by("v"):
                t = key[1]
                dve.wait_ge(*jobs.ready(key))
                nc.vector.tensor_tensor(c.H[:, t:t + 2, :], jobs.bank(key)[:, 0:2 * D].rearrange("p (t d) -> p t d", t=2),
                                        c.row("head_b").unsqueeze(1).to_broadcast([P, 2, D]),
                                        ALU.add).then_inc(s["vector_took"], 1)


def prepare(c):
    nc = c.nc
    with stage(nc, "ident_zero ident_ready") as (block, s):
        @block.sync
        def _(sp):
            sp.dma_start(c.cols[:, :], c.w["cols"]).then_inc(c.cols_in, 16)
            sp.dma_start(c.rows[:, :], c.w["rows"].broadcast_to([P, ROW_LEN])).then_inc(c.rows_in, 16)
            sp.wait_ge(c.cols_in, 16)
            sp.wait_ge(c.rows_in, 16)

        @block.vector
        def _(dve):
            nc.vector.memset(c.eps5, 1e-5)
            nc.vector.memset(c.eps6, 1e-6)

        @block.gpsimd
        def _(pool):
            nc.gpsimd.iota(c.rank[:, :], pattern=[[-1, 16]], base=16, channel_multiplier=0,
                           allow_small_or_imprecise_dtypes=True)
            nc.gpsimd.memset(c.ident[:, :], 0.0).then_inc(s["ident_zero"], 1)
            pool.wait_ge(s["ident_zero"], 1)
            nc.gpsimd.affine_select(out=c.ident[:, :], in_=c.ident[:, :], compare_op=ALU.not_equal, fill=1.0, base=0,
                                    pattern=[[-1, P]], channel_multiplier=1).then_inc(s["ident_ready"], 1)


DILATIONS = [(1, 2, 4), (1, 1, 1), (4, 8, 16), (8, 16, 32), (32, 64, 128), (64, 128, 64), (64, 128, 256), (1, 100, 200),
             (1, 125, 250), (1, 256, 512), (3, 9, 27), (5, 25, 125)]
TAPS = 4
PAIRS = NH // 2
MD = 64
CHUNK = 64


def add_rows(c, dve, step, jobs, s, name, bias=None):
    nc = c.nc
    for t in range(0, NT, 2):
        dve.wait_ge(*jobs.ready((name, t)))
        h, p = c.H[:, t:t + 2, :], jobs.bank((name, t))[:, 0:2 * D].rearrange("p (t d) -> p t d", t=2)
        if bias is None:
            nc.vector.tensor_tensor(h, h, p, ALU.add).then_inc(s["vector_took"], 1)
        else:
            step.then(nc.vector.tensor_tensor(h, h, p, ALU.add))
            nc.vector.tensor_tensor(h, h, bias.unsqueeze(1).to_broadcast([P, 2, D]), ALU.add).then_inc(s["vector_took"], 1)


def gated_convolutions(c):
    nc = c.nc
    with ExitStack() as mem:
        def sb(name, shape):
            return mem.enter_context(nc.sbuf_tensor(name, shape, F32))
        gateT, valueT, headT = sb("gateT", [HF, 2, T]), sb("valueT", [HF, 2, T]), sb("headT", [HF, 2, T])
        memT = sb("memT", [MD, T])
        channels_out = nc.dram_tensor("gated_channels", (D, T), F32, kind="Internal").ap()
        channels_back = nc.dram_tensor("convolved_channels", (D, T), F32, kind="Internal").ap()
        convolve_and_remember(c, gateT, valueT, headT, memT, channels_out, channels_back)
        mix_channels(c, headT, memT, channels_back)


def convolve_and_remember(c, gateT, valueT, headT, memT, channels_out, channels_back):
    nc = c.nc
    KG = MD + 4
    MV = KG + MD
    with ExitStack() as mem:
        def sb(name, shape):
            return mem.enter_context(nc.sbuf_tensor(name, shape, F32))
        conv = [sb("conv_a", [P, PAIRS, N]), sb("conv_b_", [P, PAIRS, N])]
        tap_one = sb("tap_one", [P, PAIRS * 3])
        mem_v, mem_out = sb("mem_v", [P, MD]), sb("mem_out", [P, MD])
        mask = sb("head_mask", [MD, 4, HD])
        uv = sb("mem_uv", [MD, MD])
        qT = sb("mem_qT", [MD, T])
        kv = sb("mem_kv", [P, NT, MV])
        gate = sb("mem_gate", [P, NT, 4])
        gate16 = sb("mem_gate16", [P, NT, 4, HD])
        kg = sb("mem_kg", [P, NT, 4, HD])
        ones = sb("ones_col", [P, 1])
        writes = sb("mem_writes", [MD, B, 3, MD])
        gsum = sb("mem_gsum", [MD, B, 3])
        decay = sb("mem_decay", [MD, B, 3])
        state = sb("mem_state", [MD, 3, B, MD])
        order = []
        for m, g in ((1, 0), (1, 1), (0, 0), (0, 1)):
            order += [(("gate", m, g), "s"), (("value", m, g), "v")]
        order += [(("uv",), "v")]
        order += [(("mq", g), "s") for g in range(2)]
        order += [(("kv", t), "s") for t in range(NT)]
        order += [(("head", m, g), "s") for m in range(2) for g in range(2)]
        order += [((kind, odd), "s") for odd in range(2) for kind in ("write", "gsum")]
        order += [(("read", b2), "s") for b2 in range(2)]
        names = JOB_SEMS + ("mem_w_in mask_step gates_in pool_step gate_ready kg_ready states_ready stored loaded "
                            "convolved returned ones_ready logits_ready zeroed")
        with stage(nc, names) as (block, s):
            jobs = Jobs(c, s, order)

            @block.sync
            def _(sp):
                sp.dma_start(mem_v[:, :], c.w["mem_v"]).then_inc(s["mem_w_in"], 16)
                sp.dma_start(mem_out[:, :], c.w["mem_out"]).then_inc(s["mem_w_in"], 16)
                for m in (1, 0):
                    for g in range(2):
                        sp.wait_ge(*jobs.taken(("value", m, g)))
                    sp.dma_start(channels_out[m * HF:(m + 1) * HF, :], valueT[:, m, :]).then_inc(s["stored"], 16)
                sp.wait_ge(s["stored"], 32)
                for hh in range(2):
                    for b in range(B):
                        lo = hh * 64 + b * HD
                        src = channels_out.rearrange("(q h d) n -> h d q n", q=PAIRS, h=2)[hh][:, :, b * N:(b + 1) * N]
                        sp.dma_start(conv[0][lo:lo + HD, :, :], src).then_inc(s["loaded"], 16)
                sp.wait_ge(s["convolved"], 1)
                for hh in range(2):
                    for b in range(B):
                        lo = hh * 64 + b * HD
                        dst = channels_back.rearrange("(q h d) n -> h d q n", q=PAIRS, h=2)[hh][:, :, b * N:(b + 1) * N]
                        sp.dma_start(dst, conv[1][lo:lo + HD, :, :]).then_inc(s["returned"], 16)
                sp.wait_ge(s["returned"], 16 * 8)

            @block.tensor
            def _(pe):
                for name in EARLY:
                    pe.wait_ge(c.weights_in[name], 16)
                for key, _ in order:
                    kind, bank = key[0], jobs.bank(key)
                    jobs.bank_free(pe, key)
                    if kind in ("gate", "value", "head"):
                        _, m, g = key
                        w = c.tile["router_wT"] if kind == "head" else c.tile["gate_wT"]
                        lo = m * HF + (D if kind == "gate" else 0)
                        for k in range(2):
                            last = pe.matmul(bank[0:HF, :], w[:, k, lo:lo + HF], c.XT[:, k, g * BANK:(g + 1) * BANK],
                                             start=(k == 0), stop=(k == 1))
                    elif kind == "uv":
                        pe.wait_ge(s["mem_w_in"], 32)
                        last = pe.matmul(bank[0:MD, 0:MD], mem_v[:, :], mem_out[:, :], start=True, stop=True)
                    elif kind == "mq":
                        g = key[1]
                        pe.wait_ge(*jobs.taken(("value", 1, g)))
                        last = pe.matmul(bank[0:MD, :], c.tile["mem_qk"][:, 0:MD], valueT[0:MD, 1, g * BANK:(g + 1) * BANK],
                                         start=True, stop=True)
                    elif kind == "kv":
                        t = key[1]
                        pe.wait_ge(*jobs.taken(("uv",)))
                        x = valueT[0:MD, 1, t * P:(t + 1) * P]
                        pe.matmul(bank[:, 0:KG], x, c.tile["mem_qk"][:, MD:MD + KG], start=True, stop=True)
                        last = pe.matmul(bank[:, KG:MV], x, uv[:, :], start=True, stop=True)
                    elif kind in ("write", "gsum"):
                        pe.wait_ge(s["kg_ready"], 1)
                        pe.wait_ge(s["ones_ready"], 1)
                        odd = key[1]
                        chunks = [(b, i) for b in range(B) for i in ((1,) if odd else (0, 2))]
                        r = slice(64 * odd, 64 * odd + 64)
                        for n, (b, i) in enumerate(chunks):
                            t = TPB * b + i // 2
                            if kind == "write":
                                last = pe.matmul(bank[0:MD, n * MD:(n + 1) * MD], kg[r, t].rearrange("p m d -> p (m d)"),
                                                 kv[r, t, KG:MV], start=True, stop=True)
                            else:
                                last = pe.matmul(bank[0:MD, n:n + 1], gate16[r, t].rearrange("p m d -> p (m d)"),
                                                 ones[r, :], start=True, stop=True)
                    else:
                        pe.wait_ge(s["states_ready"], 1)
                        for n in range(6):
                            b, i = 2 * key[1] + n // 3, n % 3
                            at = b * N + (i + 1) * CHUNK
                            last = pe.matmul(bank[0:MD, n * CHUNK:(n + 1) * CHUNK], state[:, i, b, :],
                                             qT[:, at:at + CHUNK], start=True, stop=True)
                    last.then_inc(s["product_ready"], 1)

            @block.scalar
            def _(act):
                def sigmoid_gate(m, g):
                    act.wait_ge(*jobs.ready(("gate", m, g)))
                    nc.scalar.activation(gateT[:, m, g * BANK:(g + 1) * BANK], jobs.bank(("gate", m, g))[0:HF, :],
                                         ACT.Sigmoid).then_inc(s["scalar_took"], 1)
                for m, g in ((1, 0), (1, 1), (0, 0), (0, 1)):
                    sigmoid_gate(m, g)
                for g in range(2):
                    act.wait_ge(*jobs.ready(("mq", g)))
                    nc.scalar.copy(qT[:, g * BANK:(g + 1) * BANK], jobs.bank(("mq", g))[0:MD, :]).then_inc(s["scalar_took"], 1)
                for t in range(NT):
                    act.wait_ge(*jobs.ready(("kv", t)))
                    nc.scalar.copy(kv[:, t, :], jobs.bank(("kv", t))[:, 0:MV]).then_inc(s["scalar_took"], 1)
                for m in range(2):
                    for g in range(2):
                        act.wait_ge(*jobs.ready(("head", m, g)))
                        nc.scalar.activation(headT[:, m, g * BANK:(g + 1) * BANK], jobs.bank(("head", m, g))[0:HF, :],
                                             ACT.Sigmoid, bias=c.col("router_b")[0:HF, m:m + 1]).then_inc(s["scalar_took"], 1)
                act.wait_ge(s["logits_ready"], 1)
                nc.scalar.activation(gate[:, :, :], gate[:, :, :], ACT.Sigmoid).then_inc(s["gate_ready"], 1)
                for odd in range(2):
                    z = slice(1, 2) if odd else slice(0, 3, 2)
                    n = B * (1 if odd else 2)
                    act.wait_ge(*jobs.ready(("write", odd)))
                    nc.scalar.copy(writes[:, :, z, :], jobs.bank(("write", odd))[0:MD, 0:n * MD].rearrange(
                        "p (b i d) -> p b i d", b=B, d=MD)).then_inc(s["scalar_took"], 1)
                    act.wait_ge(*jobs.ready(("gsum", odd)))
                    nc.scalar.copy(gsum[:, :, z], jobs.bank(("gsum", odd))[0:MD, 0:n].rearrange(
                        "p (b i) -> p b i", b=B)).then_inc(s["scalar_took"], 1)
                for b2 in range(2):
                    act.wait_ge(*jobs.ready(("read", b2)))
                    nc.scalar.copy(memT.rearrange("p (b n) -> p b n", b=B)[:, 2 * b2:2 * b2 + 2, CHUNK:N],
                                   jobs.bank(("read", b2))[0:MD, 0:6 * CHUNK].rearrange("p (b n) -> p b n", b=2)
                                   ).then_inc(s["scalar_took"], 1)

            @block.gpsimd
            def _(pool):
                step = Steps(pool, s["pool_step"])
                nc.gpsimd.memset(memT.rearrange("p (b n) -> p b n", b=B)[:, :, 0:CHUNK], 0.0).then_inc(s["zeroed"], 1)
                nc.gpsimd.memset(ones[:, :], 1.0).then_inc(s["ones_ready"], 1)
                step.then(nc.gpsimd.memset(mask[:, :, :], 1.0))
                step.then(nc.gpsimd.affine_select(out=mask[:, :, :], in_=mask[:, :, :], compare_op=ALU.is_ge, fill=0.0,
                                                  base=0, pattern=[[-HD, 4], [0, HD]], channel_multiplier=1))
                nc.gpsimd.affine_select(out=mask[:, :, :], in_=mask[:, :, :], compare_op=ALU.is_ge, fill=0.0,
                                        base=HD - 1, pattern=[[HD, 4], [0, HD]],
                                        channel_multiplier=-1).then_inc(s["mask_step"], 1)
                pool.wait_ge(*jobs.taken(("kv", NT - 1)))
                nc.gpsimd.tensor_tensor(gate[:, :, :], kv[:, :, MD:KG],
                                        c.row("mem_Wg_b").unsqueeze(1).to_broadcast([P, NT, 4]),
                                        ALU.add).then_inc(s["logits_ready"], 1)
                pool.wait_ge(s["gate_ready"], 1)
                g16 = gate[:, :, :].unsqueeze(3).to_broadcast([P, NT, 4, HD])
                step.then(nc.gpsimd.tensor_copy(gate16[:, :, :, :], g16))
                for t in range(NT):
                    last = nc.gpsimd.tensor_tensor(kg[:, t, :, :], kv[:, t, 0:MD].rearrange("p (m d) -> p m d", d=HD),
                                                   gate16[:, t, :, :], ALU.mult)
                last.then_inc(s["kg_ready"], 1)
                pool.wait_ge(*jobs.taken(("gsum", 1)))
                pool.wait_ge(s["mask_step"], 1)
                step.then(nc.gpsimd.tensor_scalar(decay[:, :, :], gsum[:, :, :], -1.0 / CHUNK, 1.0, ALU.mult, ALU.add))
                m3 = mask.rearrange("p m d -> p (m d)").unsqueeze(1).to_broadcast([MD, B, MD])
                for i in range(3):
                    step.then(nc.gpsimd.tensor_tensor(writes[:, :, i, :], writes[:, :, i, :], m3, ALU.mult))
                step.then(nc.gpsimd.tensor_copy(state[:, 0, :, :], writes[:, :, 0, :]))
                for i in (1, 2):
                    d = decay[:, :, i:i + 1].to_broadcast([MD, B, MD])
                    step.then(nc.gpsimd.tensor_tensor(state[:, i, :, :], state[:, i - 1, :, :], d, ALU.mult))
                    ins = nc.gpsimd.tensor_tensor(state[:, i, :, :], state[:, i, :, :], writes[:, :, i, :], ALU.add)
                    if i == 1:
                        step.then(ins)
                    else:
                        ins.then_inc(s["states_ready"], 1)

            @block.vector
            def _(dve):
                step = Steps(dve, s["vector_step"])
                dve.wait_ge(c.cols_in, 16)
                taps = c.col("conv_taps").rearrange("p (q j k) -> p q j k", q=PAIRS, j=3)
                bias = c.col("conv_bias").rearrange("p (q j) -> p q j", q=PAIRS)
                step.then(nc.vector.tensor_scalar(tap_one.rearrange("p (q j) -> p q j", q=PAIRS), taps[:, :, :, TAPS - 1],
                                                  1.0, None, ALU.add))
                for m, g in ((1, 0), (1, 1), (0, 0), (0, 1)):
                    dve.wait_ge(*jobs.ready(("value", m, g)))
                    dve.wait_ge(*jobs.taken(("gate", m, g)))
                    nc.vector.tensor_tensor(valueT[:, m, g * BANK:(g + 1) * BANK], jobs.bank(("value", m, g))[0:HF, :],
                                            gateT[:, m, g * BANK:(g + 1) * BANK], ALU.mult).then_inc(s["vector_took"], 1)
                dve.wait_ge(*jobs.ready(("uv",)))
                dve.wait_ge(s["mask_step"], 1)
                nc.vector.tensor_tensor(uv[:, :], jobs.bank(("uv",))[0:MD, 0:MD], mask.rearrange("p m d -> p (m d)"),
                                        ALU.mult).then_inc(s["vector_took"], 1)
                dve.wait_ge(s["loaded"], 16 * 8)
                done = {}
                src, dst = conv
                for j in range(3):
                    chains = []
                    for q in range(PAIRS):
                        ops = [(slice(0, P), 0, None)]
                        for k in range(TAPS - 1):
                            for hh in range(2):
                                shift = (TAPS - 1 - k) * DILATIONS[2 * q + hh][j]
                                if shift < N:
                                    ops.append((slice(64 * hh, 64 * hh + 64), shift, k))
                        chains.append(ops)
                    for n in range(max(map(len, chains))):
                        for q in range(PAIRS):
                            if n >= len(chains[q]):
                                continue
                            r, shift, k = chains[q][n]
                            if q in done:
                                dve.wait_ge(s["vector_step"], done[q])
                            if k is None:
                                ins = nc.vector.tensor_scalar(dst[:, q, :], src[:, q, :], tap_one[:, 3 * q + j:3 * q + j + 1],
                                                              bias[:, q, j:j + 1], ALU.mult, ALU.add)
                            else:
                                ins = nc.vector.scalar_tensor_tensor(dst[r, q, shift:N], src[r, q, 0:N - shift],
                                                                     taps[r, q, j, k:k + 1], dst[r, q, shift:N],
                                                                     ALU.mult, ALU.add)
                            done[q] = step.mark(ins)
                    src, dst = dst, src
                dve.wait_ge(s["vector_step"], step.n)
                nc.vector.engine_nop().then_inc(s["convolved"], 1)


def mix_channels(c, headT, memT, channels_back):
    nc = c.nc
    with ExitStack() as mem:
        convT = mem.enter_context(nc.sbuf_tensor("convT", [HF, 2, T], F32))
        gateT = mem.enter_context(nc.sbuf_tensor("mixgT", [HF, 2, T], F32))
        order = [(("mg", m, g), "s") for g in range(2) for m in range(2)] + [(("mix", t), "v") for t in range(0, NT, 2)]
        with stage(nc, JOB_SEMS + "channels_in weighted gated") as (block, s):
            jobs = Jobs(c, s, order)

            @block.sync
            def _(sp):
                sp.dma_start(convT[:, :, :], channels_back.rearrange("(m p) n -> p m n", m=2)).then_inc(s["channels_in"], 16)

            @block.tensor
            def _(pe):
                for key, _ in order:
                    bank = jobs.bank(key)
                    jobs.bank_free(pe, key)
                    if key[0] == "mg":
                        _, m, g = key
                        pe.wait_ge(s["weighted"], g + 1)
                        for k in range(2):
                            last = pe.matmul(bank[0:HF, :], c.tile["mixg_wT"][:, k, m * HF:(m + 1) * HF],
                                             convT[:, k, g * BANK:(g + 1) * BANK], start=(k == 0), stop=(k == 1))
                    else:
                        pe.wait_ge(s["gated"], key[1] // 4 + 1)
                        for i in range(2):
                            t = key[1] + i
                            for k in range(2):
                                last = pe.matmul(bank[:, i * D:(i + 1) * D], gateT[:, k, t * P:(t + 1) * P],
                                                 c.tile["mix_wT"][:, k, :], start=(k == 0), stop=(k == 1))
                    last.then_inc(s["product_ready"], 1)

            @block.scalar
            def _(act):
                for key in jobs.by("s"):
                    _, m, g = key
                    act.wait_ge(*jobs.ready(key))
                    nc.scalar.activation(gateT[:, m, g * BANK:(g + 1) * BANK], jobs.bank(key)[0:HF, :], ACT.Sigmoid,
                                         bias=c.col("mixg_b")[0:HF, m:m + 1]).then_inc(s["scalar_took"], 1)

            @block.vector
            def _(dve):
                step = Steps(dve, s["vector_step"])
                dve.wait_ge(s["channels_in"], 16)
                step.then(nc.vector.tensor_tensor(convT[0:MD, 1, :], convT[0:MD, 1, :], memT[:, :], ALU.add))
                for g in range(2):
                    z = slice(g * BANK, (g + 1) * BANK)
                    nc.vector.tensor_tensor(convT[:, :, z], convT[:, :, z], headT[:, :, z], ALU.mult).then_inc(s["weighted"], 1)
                for g in range(2):
                    z = slice(g * BANK, (g + 1) * BANK)
                    dve.wait_ge(*jobs.taken(("mg", 1, g)))
                    dve.wait_ge(s["weighted"], g + 1)
                    nc.vector.tensor_tensor(gateT[:, :, z], gateT[:, :, z], convT[:, :, z], ALU.mult).then_inc(s["gated"], 1)
                add_rows(c, dve, step, jobs, s, "mix", c.row("mix_b"))


EMBEDS, RATIOS = (96, 144, 192), (2, 3, 4)


def mask_entangled_ffn(c, pool, step):
    nc = c.nc
    for name in ("ffn_fcT", "ffn_proj"):
        pool.wait_ge(c.weights_in[name], 16)
    alpha = c.row("alpha")
    for i in range(3):
        step.then(nc.gpsimd.tensor_scalar(c.choice[:, 3 * i:3 * i + 3], alpha[:, 3:6], alpha[:, i:i + 1], None, ALU.mult))
    step.mark(nc.gpsimd.memset(c.coef_in[:, :, :], 0.0))
    step.then(nc.gpsimd.memset(c.coef_hid[:, :, :], 0.0))

    def add_choice(region, a):
        step.then(nc.gpsimd.tensor_scalar(region, region, a, None, ALU.add))

    for i, e in enumerate(EMBEDS):
        for j, r in enumerate(RATIOS):
            a, wide = c.choice[:, 3 * i + j:3 * i + j + 1], r * e
            add_choice(c.coef_in[:, 0, 0:wide], a[0:HF])
            if e > HF:
                add_choice(c.coef_in[0:e - HF, 1, 0:wide], a[0:e - HF])
            add_choice(c.coef_hid[:, 0:wide // P, 0:e], a)
            if wide % P:
                add_choice(c.coef_hid[0:wide % P, wide // P, 0:e], a[0:wide % P])
    step.mark(nc.gpsimd.tensor_tensor(c.ffn_b0[:, :], c.col("ffn_b_fc"), c.coef_hid[:, :, 0], ALU.mult))
    step.mark(nc.gpsimd.tensor_tensor(c.ffn_b1[:, :], c.row("ffn_b_proj"), c.coef_hid[:, 0, :], ALU.mult))
    step.mark(nc.gpsimd.tensor_tensor(c.tile["ffn_fcT"][:, :, :], c.tile["ffn_fcT"][:, :, :], c.coef_in[:, :, :], ALU.mult))
    step.then(nc.gpsimd.tensor_tensor(c.tile["ffn_proj"][:, :, :], c.tile["ffn_proj"][:, :, :], c.coef_hid[:, :, :], ALU.mult))


def entangled_ffn(c):
    nc = c.nc
    with ExitStack() as mem:
        hid = mem.enter_context(nc.sbuf_tensor("ffn_hidden", [P, FT, T], F32))
        order = [(("h", m, g), "s") for g in range(2) for m in range(FT)] + [(("out", t), "v") for t in range(0, NT, 2)]
        with stage(nc, JOB_SEMS) as (block, s):
            jobs = Jobs(c, s, order)

            @block.tensor
            def _(pe):
                for key, _ in order:
                    bank = jobs.bank(key)
                    jobs.bank_free(pe, key)
                    if key[0] == "h":
                        _, m, g = key
                        for k in range(2):
                            last = pe.matmul(bank, c.tile["ffn_fcT"][:, k, m * P:(m + 1) * P], c.XT[:, k, g * BANK:(g + 1) * BANK],
                                             start=(k == 0), stop=(k == 1))
                    else:
                        pe.wait_ge(*jobs.taken(("h", FT - 1, key[1] // 4)))
                        for i in range(2):
                            t = key[1] + i
                            for m in range(FT):
                                last = pe.matmul(bank[:, i * D:(i + 1) * D], hid[:, m, t * P:(t + 1) * P],
                                                 c.tile["ffn_proj"][:, m, :], start=(m == 0), stop=(m == FT - 1))
                    last.then_inc(s["product_ready"], 1)

            @block.scalar
            def _(act):
                for key in jobs.by("s"):
                    _, m, g = key
                    act.wait_ge(*jobs.ready(key))
                    nc.scalar.activation(hid[:, m, g * BANK:(g + 1) * BANK], jobs.bank(key), ACT.Gelu_apprx_tanh,
                                         bias=c.ffn_b0[:, m:m + 1]).then_inc(s["scalar_took"], 1)

            @block.vector
            def _(dve):
                add_rows(c, dve, Steps(dve, s["vector_step"]), jobs, s, "out", c.ffn_b1[:, :])


COMBOS = B * PAIRS
ORDER_RP = [(b, hg) for b in range(B) for hg in range(HG)]


def combo(b, p):
    return b * PAIRS + p


def nystrom_attention(c):
    nc = c.nc
    with ExitStack() as mem:
        def sb(name, shape):
            return mem.enter_context(nc.sbuf_tensor(name, shape, F32))
        c.Vtok = sb("nys_Vtok", [P, NT, D])
        c.k1T = sb("nys_k1T", [P, PAIRS, T])
        c.W = sb("nys_W", [P, COMBOS, HD])
        c.V, c.VT = sb("nys_inv", [P, COMBOS, LM]), sb("nys_invT", [P, COMBOS, LM])
        c.KT = sb("nys_KT", [P, COMBOS, LM])
        with ExitStack() as early:
            def sb2(name, shape):
                return early.enter_context(nc.sbuf_tensor(name, shape, F32))
            c.QT, c.KTok = sb2("nys_QT", [P, HG, T]), sb2("nys_KT_feat", [P, HG, T])
            c.QL, c.KL = sb2("nys_QL", [P, HG, B * LM]), sb2("nys_KL", [P, HG, B * LM])
            nystrom_project(c)
            nystrom_landmark_kernel(c)
            nystrom_token_kernels(c)
        nystrom_invert(c)
        nystrom_apply(c)


def nystrom_project(c):
    nc = c.nc
    order = [(("qk", m, g), "s") for m in range(2 * HG) for g in range(2)] + [(("v", t), "v") for t in range(0, NT, 2)]
    with stage(nc, JOB_SEMS) as (block, s):
        jobs = Jobs(c, s, order)

        @block.tensor
        def _(pe):
            for key, _ in order:
                bank = jobs.bank(key)
                jobs.bank_free(pe, key)
                if key[0] == "qk":
                    _, m, g = key
                    for k in range(2):
                        last = pe.matmul(bank, c.tile["nys_qk"][:, k, m * P:(m + 1) * P], c.XT[:, k, g * BANK:(g + 1) * BANK],
                                         start=(k == 0), stop=(k == 1))
                else:
                    for i in range(2):
                        t = key[1] + i
                        for k in range(2):
                            last = pe.matmul(bank[:, i * D:(i + 1) * D], c.XT[:, k, t * P:(t + 1) * P], c.tile["nys_v"][:, k, :],
                                             start=(k == 0), stop=(k == 1))
                last.then_inc(s["product_ready"], 1)

        @block.scalar
        def _(act):
            for key in jobs.by("s"):
                _, m, g = key
                act.wait_ge(*jobs.ready(key))
                dst, scale = (c.QT, 1.0 / HD ** 0.5) if m < HG else (c.KTok, 1.0)
                nc.scalar.mul(dst[:, m % HG, g * BANK:(g + 1) * BANK], jobs.bank(key), scale).then_inc(s["scalar_took"], 1)

        @block.vector
        def _(dve):
            step = Steps(dve, s["vector_step"])
            for key in jobs.by("v"):
                t = key[1]
                dve.wait_ge(*jobs.ready(key))
                nc.vector.tensor_copy(c.Vtok[:, t:t + 2, :], jobs.bank(key)[:, 0:2 * D].rearrange(
                    "p (t d) -> p t d", t=2)).then_inc(s["vector_took"], 1)
            for m in range(2 * HG):
                src, dst = (c.QT, c.QL) if m < HG else (c.KTok, c.KL)
                dve.wait_ge(*jobs.taken(("qk", m, 1)))
                step.then(nc.vector.tensor_reduce(dst[:, m % HG, :], src[:, m % HG, :].rearrange(
                    "p (l s) -> p l s", s=N // LM), AX.X, ALU.add))
                step.mark(nc.vector.tensor_scalar(dst[:, m % HG, :], dst[:, m % HG, :], 1.0 / (N // LM), None, ALU.mult))


def head_rows(h):
    return slice(SLOT * (h % 4), SLOT * (h % 4) + SLOT)


def nystrom_landmark_kernel(c):
    nc = c.nc
    with ExitStack() as mem:
        def sb(name, shape):
            return mem.enter_context(nc.sbuf_tensor(name, shape, F32))
        shifted = sb("k2_shifted", [P, COMBOS, LM])
        kexp = sb("k2_exp", [P, COMBOS, LM])
        K = sb("k2", [P, COMBOS, LM])
        Kdiag = sb("k2_diag", [P, COMBOS, P])
        kmax, ksum, kinv = sb("k2_max", [P, COMBOS]), sb("k2_sum", [P, COMBOS]), sb("k2_inv", [P, COMBOS])
        colsum, dinv = sb("k2_colsum", [P, COMBOS]), sb("k2_dinv", [P, COMBOS])
        best = sb("k2_best", [COMBOS, 2])
        spread = sb("k2_spread", [COMBOS, P])
        order = [(("k2", rp, n), "v") for rp in range(2) for n in range(2)]
        order += [(("turn", n), "v") for n in range(6)] + [(("sums",), "v"), (("inv",), "v")]
        with stage(nc, JOB_SEMS + "exped diag_zero diag_ready colsum_ready spread_ready") as (block, s):
            jobs = Jobs(c, s, order)

            def members(rp, n):
                return [(b, 2 * hg + rp) for b, hg in ORDER_RP[6 * n:6 * n + 6]]

            @block.gpsimd
            def _(pool):
                nc.gpsimd.memset(Kdiag[:, :, :], 0.0).then_inc(s["diag_zero"], 1)

            @block.tensor
            def _(pe):
                for key, _ in order:
                    kind, bank = key[0], jobs.bank(key)
                    jobs.bank_free(pe, key)
                    if kind == "k2":
                        for i, (b, p) in enumerate(members(key[1], key[2])):
                            for half in range(2):
                                h = 2 * p + half
                                r, z = head_rows(h), slice(b * LM, (b + 1) * LM)
                                last = pe.matmul(bank[64 * half:64 * half + 64, i * LM:(i + 1) * LM],
                                                 c.QL[r, h // 4, z], c.KL[r, h // 4, z], start=True, stop=True,
                                                 tile_position=(SLOT * (h % 4), 64 * half))
                    elif kind == "turn":
                        pe.wait_ge(s["diag_ready"], 1)
                        for i in range(4):
                            last = pe.transpose(bank[:, i * P:(i + 1) * P], Kdiag[:, 4 * key[1] + i, :], c.ident[:, :])
                    elif kind == "sums":
                        pe.wait_ge(s["colsum_ready"], 1)
                        last = pe.transpose(bank[0:COMBOS, 0:P], colsum[:, :], c.ident[:, :])
                    else:
                        pe.wait_ge(s["spread_ready"], 1)
                        last = pe.transpose(bank[:, 0:COMBOS], spread[:, :], c.ident[0:COMBOS, 0:COMBOS])
                    last.then_inc(s["product_ready"], 1)

            @block.scalar
            def _(act):
                act.wait_ge(*jobs.taken(("k2", 1, 1)))
                nc.scalar.activation(kexp[:, :, :], shifted[:, :, :], ACT.Exp).then_inc(s["exped"], 1)

            @block.vector
            def _(dve):
                step = Steps(dve, s["vector_step"])
                for key in [k for k in jobs.by("v") if k[0] == "k2"]:
                    _, rp, n = key
                    dve.wait_ge(*jobs.ready(key))
                    src = jobs.bank(key)[:, 0:6 * LM].rearrange("p (b g l) -> p b g l", b=2, g=HG)
                    view = lambda m: m.rearrange("p (b g r) -> p b g r", b=B, g=HG)[:, 2 * n:2 * n + 2, :, rp]
                    step.then(nc.vector.tensor_reduce(view(kmax), src, AX.X, ALU.max))
                    dst = shifted.rearrange("p (b g r) l -> p b g r l", b=B, g=HG)
                    for b in range(2):
                        last = nc.vector.tensor_tensor(dst[:, 2 * n + b, :, rp, :], src[:, b], view(kmax)[:, b].unsqueeze(
                            2).to_broadcast([P, HG, LM]), ALU.subtract)
                    last.then_inc(s["vector_took"], 1)
                dve.wait_ge(s["exped"], 1)
                step.then(nc.vector.tensor_reduce(ksum[:, :], kexp[:, :, :], AX.X, ALU.add))
                step.then(nc.vector.reciprocal(kinv[:, :], ksum[:, :]))
                step.then(nc.vector.tensor_tensor(K[:, :, :], kexp[:, :, :], kinv[:, :].unsqueeze(2).to_broadcast(
                    [P, COMBOS, LM]), ALU.mult))
                dve.wait_ge(s["diag_zero"], 1)
                nc.vector.tensor_copy(Kdiag[0:64, :, 0:LM], K[0:64, :, :])
                nc.vector.tensor_copy(Kdiag[64:P, :, LM:P], K[64:P, :, :]).then_inc(s["diag_ready"], 1)
                for n in range(6):
                    dve.wait_ge(*jobs.ready(("turn", n)))
                    src = jobs.bank(("turn", n)).rearrange("p (c l) -> p c l", c=4)
                    nc.vector.tensor_copy(c.KT[0:64, 4 * n:4 * n + 4, :], src[0:64, :, 0:LM])
                    nc.vector.tensor_copy(c.KT[64:P, 4 * n:4 * n + 4, :], src[64:P, :, LM:P]).then_inc(s["vector_took"], 1)
                dve.wait_ge(*jobs.taken(("turn", 5)))
                nc.vector.tensor_reduce(colsum[:, :], c.KT[:, :, :], AX.X, ALU.add).then_inc(s["colsum_ready"], 1)
                dve.wait_ge(*jobs.ready(("sums",)))
                nc.vector.tensor_reduce(best[:, :], jobs.bank(("sums",))[0:COMBOS, 0:P].rearrange("p (h l) -> p h l", h=2),
                                        AX.X, ALU.max).then_inc(s["vector_took"], 1)
                dve.wait_ge(*jobs.taken(("sums",)))
                step.then(nc.vector.reciprocal(best[:, :], best[:, :]))
                nc.vector.tensor_copy(spread.rearrange("p (h l) -> p h l", h=2), best[:, :].unsqueeze(2).to_broadcast(
                    [COMBOS, 2, LM])).then_inc(s["spread_ready"], 1)
                dve.wait_ge(*jobs.ready(("inv",)))
                nc.vector.tensor_copy(dinv[:, :], jobs.bank(("inv",))[:, 0:COMBOS]).then_inc(s["vector_took"], 1)
                dve.wait_ge(*jobs.taken(("inv",)))
                d = dinv[:, :].unsqueeze(2).to_broadcast([P, COMBOS, LM])
                nc.vector.tensor_tensor(c.V[:, :, :], c.KT[:, :, :], d, ALU.mult)
                step.then(nc.vector.tensor_tensor(c.VT[:, :, :], K[:, :, :], d, ALU.mult))


def nystrom_token_kernels(c):
    nc = c.nc
    with ExitStack() as mem:
        def sb(name, shape):
            return mem.enter_context(nc.sbuf_tensor(name, shape, F32))
        k1 = sb("k1", [P, NT, NH, LM])
        shifted, exped = sb("k1_shifted", [P, 2, TPB, HG, LM]), sb("k1_exped", [P, 2, TPB, HG, LM])
        kmax, ksum, kinv = sb("k1_max", [P, 16, TPB, HG]), sb("k1_sum", [P, 16, TPB, HG]), sb("k1_inv", [P, 16, TPB, HG])
        k3 = sb("k3", [P, COMBOS, N])
        k3T = c.k1T.rearrange("p q t -> p (q t)").rearrange("p (c j l) -> p c j l", c=COMBOS, j=TPB)
        k3max, k3sum, k3inv = sb("k3_max", [P, COMBOS]), sb("k3_sum", [P, COMBOS]), sb("k3_inv", [P, COMBOS])
        k3jobs = [("k3", rp, n) for rp in range(2) for n in range(6)]
        k1jobs = [("k1", r, b) for b in range(B) for r in range(4)]
        order = [(k, "s") for k in k3jobs] + [(k, "v") for k in k1jobs]
        order += [(("k3T", n), "s") for n in range(12)]
        order += [(("W", n), "v") for n in range(2)]
        order += [(("k1T", p, g), "vs"[g]) for p in range(PAIRS) for g in range(2)]
        with stage(nc, JOB_SEMS + "k3max_ready k1_exped k1_normed") as (block, s):
            jobs = Jobs(c, s, order)

            def members(rp, n):
                return [(b, 2 * hg + rp) for b, hg in ORDER_RP[2 * n:2 * n + 2]]

            @block.tensor
            def _(pe):
                for key, _ in order:
                    kind, bank = key[0], jobs.bank(key)
                    jobs.bank_free(pe, key)
                    if kind == "k3":
                        for i, (b, p) in enumerate(members(key[1], key[2])):
                            for half in range(2):
                                h = 2 * p + half
                                r = head_rows(h)
                                last = pe.matmul(bank[64 * half:64 * half + 64, i * N:(i + 1) * N],
                                                 c.QL[r, h // 4, b * LM:(b + 1) * LM], c.KTok[r, h // 4, b * N:(b + 1) * N],
                                                 start=True, stop=True, tile_position=(SLOT * (h % 4), 64 * half))
                    elif kind == "k1":
                        _, r, b = key
                        for i in range(TPB):
                            t = TPB * b + i
                            for hg in range(HG):
                                at = (i * HG + hg) * LM
                                last = pe.matmul(bank[:, at:at + LM], c.QT[head_rows(r), hg, t * P:(t + 1) * P],
                                                 c.KL[head_rows(r), hg, b * LM:(b + 1) * LM], start=True, stop=True,
                                                 tile_position=(SLOT * r, 0))
                    elif kind == "k3T":
                        n = key[1]
                        pe.wait_ge(*jobs.taken(k3jobs[-1]))
                        for i in range(4):
                            last = pe.transpose(bank[:, i * P:(i + 1) * P], k3[:, 2 * n + i // 2, (i % 2) * P:(i % 2 + 1) * P],
                                                c.ident[:, :])
                    elif kind == "W":
                        for i in range(12):
                            co = 12 * key[1] + i
                            b, p = co // PAIRS, co % PAIRS
                            pe.wait_ge(*jobs.taken(("k3T", co // 2)))
                            for j in range(TPB):
                                last = pe.matmul(bank[:, i * 32:(i + 1) * 32], k3T[:, co, j, :],
                                                 c.Vtok[:, TPB * b + j, 32 * p:32 * p + 32], start=(j == 0), stop=(j == 1))
                    else:
                        _, p, g = key
                        pe.wait_ge(s["k1_normed"], 8 * (g + 1))
                        for i in range(4):
                            last = pe.transpose(bank[:, i * P:(i + 1) * P],
                                                k1[:, 4 * g + i, 2 * p:2 * p + 2, :].rearrange("p h l -> p (h l)"),
                                                c.ident[:, :])
                    last.then_inc(s["product_ready"], 1)

            @block.scalar
            def _(act):
                for n, key in enumerate(k3jobs):
                    act.wait_ge(s["k3max_ready"], n + 1)
                    for i, (b, p) in enumerate(members(key[1], key[2])):
                        co = combo(b, p)
                        last = nc.scalar.activation(k3[:, co, :], jobs.bank(key)[:, i * N:(i + 1) * N], ACT.Exp,
                                                    bias=k3max[:, co:co + 1], accum_out=k3sum[:, co:co + 1])
                    last.then_inc(s["scalar_took"], 1)
                for n, key in enumerate(k1jobs):
                    act.wait_ge(*jobs.taken(key))
                    if n >= 2:
                        act.wait_ge(s["k1_normed"], n - 1)
                    nc.scalar.activation(exped[:, n % 2], shifted[:, n % 2], ACT.Exp).then_inc(s["k1_exped"], 1)
                for n in range(12):
                    act.wait_ge(*jobs.ready(("k3T", n)))
                    nc.scalar.copy(k3T[:, 2 * n:2 * n + 2, :, :].rearrange("p c j l -> p (c j l)"),
                                   jobs.bank(("k3T", n))).then_inc(s["scalar_took"], 1)
                for p in range(PAIRS):
                    act.wait_ge(*jobs.ready(("k1T", p, 1)))
                    nc.scalar.copy(c.k1T[:, p, BANK:T], jobs.bank(("k1T", p, 1))).then_inc(s["scalar_took"], 1)

            @block.vector
            def _(dve):
                step = Steps(dve, s["vector_step"])
                for key in k3jobs:
                    _, rp, n = key
                    dve.wait_ge(*jobs.ready(key))
                    for i, (b, p) in enumerate(members(rp, n)):
                        co = combo(b, p)
                        last = nc.vector.tensor_reduce(k3max[:, co:co + 1], jobs.bank(key)[:, i * N:(i + 1) * N], AX.X,
                                                       ALU.max, negate=True)
                    last.then_inc(s["k3max_ready"], 1)

                def normalise(n):
                    _, r, b = k1jobs[n]
                    dve.wait_ge(s["k1_exped"], n + 1)
                    e = exped[:, n % 2]
                    step.then(nc.vector.tensor_reduce(ksum[:, n], e, AX.X, ALU.add))
                    step.then(nc.vector.reciprocal(kinv[:, n], ksum[:, n]))
                    for i in range(TPB):
                        dst = k1[:, TPB * b + i].rearrange("p (g r) l -> p g r l", g=HG)[:, :, r, :]
                        last = nc.vector.tensor_tensor(dst, e[:, i], kinv[:, n, i].unsqueeze(2).to_broadcast([P, HG, LM]),
                                                       ALU.mult)
                    last.then_inc(s["k1_normed"], 1)

                for n, key in enumerate(k1jobs):
                    dve.wait_ge(*jobs.ready(key))
                    src = jobs.bank(key)[:, 0:6 * LM].rearrange("p (a l) -> p a l", l=LM)
                    mx = kmax[:, n].rearrange("p i g -> p (i g)")
                    step.then(nc.vector.tensor_reduce(mx, src, AX.X, ALU.max))
                    if n >= 2:
                        dve.wait_ge(s["k1_exped"], n - 1)
                    nc.vector.tensor_tensor(shifted[:, n % 2].rearrange("p i g l -> p (i g) l"), src,
                                            mx.unsqueeze(2).to_broadcast([P, 6, LM]), ALU.subtract).then_inc(s["vector_took"], 1)
                    if n:
                        normalise(n - 1)
                normalise(len(k1jobs) - 1)
                dve.wait_ge(*jobs.taken(k3jobs[-1]))
                step.then(nc.vector.reciprocal(k3inv[:, :], k3sum[:, :]))
                for n in range(2):
                    dve.wait_ge(*jobs.ready(("W", n)))
                    z = slice(12 * n, 12 * n + 12)
                    src = jobs.bank(("W", n))[:, 0:12 * 32].rearrange("p (c x) -> p c x", x=32)
                    for half in range(2):
                        r = slice(64 * half, 64 * half + 64)
                        last = nc.vector.tensor_tensor(c.W[r, z, :], src[r, :, HD * half:HD * half + HD],
                                                       k3inv[r, z].unsqueeze(2).to_broadcast([64, 12, HD]), ALU.mult)
                    last.then_inc(s["vector_took"], 1)
                for p in range(PAIRS):
                    dve.wait_ge(*jobs.ready(("k1T", p, 0)))
                    nc.vector.tensor_copy(c.k1T[:, p, 0:BANK], jobs.bank(("k1T", p, 0))).then_inc(s["vector_took"], 1)


def nystrom_invert(c):
    nc = c.nc
    G, ITERS = 6, 6
    with ExitStack() as mem:
        def sb(name, shape):
            return mem.enter_context(nc.sbuf_tensor(name, shape, F32))
        AT = sb("inv_AT", [P, COMBOS, LM])
        R = sb("inv_rest", [P, COMBOS, LM])
        eyes = sb("inv_eyes", [P, 3, LM])
        products = [("AT", c.V, c.KT, "s"), ("A", c.KT, c.V, "v"), ("C", AT, R, "v"), ("E", AT, R, "v"),
                    ("V", c.VT, R, "s"), ("VT", R, c.VT, "s")]
        order = []
        for a, b_ in ((0, 2), (2, 3), (3, 4), (4, 6)):
            order += [((products[i][0], g), products[i][3]) for g in range(G) for i in range(a, b_)]
        with stage(nc, JOB_SEMS + "eye_ready") as (block, s):
            jobs = Jobs(c, s, order)
            per_iter = {"v": len(jobs.by("v")), "s": len(jobs.by("s"))}
            table = {n: (lhsT, rhs) for n, lhsT, rhs, _ in products}

            def group(m, g):
                return m[:, 4 * g:4 * g + 4, :]

            def taken(key, it):
                sem, n = jobs.taken(key)
                return sem, it * per_iter[dict(order)[key]] + n

            @block.tensor
            def _(pe):
                def iterate(it, before, last_one=False):
                    for k, (key, _) in enumerate(order):
                        name, g = key
                        if last_one and name == "V":
                            continue
                        pe.wait_ge(s["vector_step"], 6)
                        if k >= NB:
                            j = k - NB
                            while last_one and order[j][0][0] == "V":
                                j -= NB
                            pe.wait_ge(*taken(order[j][0], it))
                        elif before is not None:
                            pe.wait_ge(*taken(order[(len(order) - 1 - k) // NB * NB + k][0], before))
                        if name in ("AT", "A") and before is not None:
                            pe.wait_ge(*taken(("VT", g), before))
                            pe.wait_ge(*taken(("V", g), before))
                        if name == "C":
                            pe.wait_ge(*taken(("A", g), it))
                            pe.wait_ge(*taken(("AT", g), it))
                        if name in ("E", "V", "VT"):
                            pe.wait_ge(*taken(("C" if name == "E" else "E", g), it))
                        bank = c.bank[k % NB]
                        lhsT, rhs = table[name]
                        for i in range(4):
                            for half in range(2):
                                r = slice(64 * half, 64 * half + 64)
                                last = pe.matmul(bank[r, i * LM:(i + 1) * LM], lhsT[r, 4 * g + i, :], rhs[r, 4 * g + i, :],
                                                 start=True, stop=True, tile_position=(64 * half, 64 * half))
                        last.then_inc(s["product_ready"], 1)

                iterate(0, None)
                for it in range(1, ITERS - 1):
                    iterate(it, it - 1)
                iterate(ITERS - 1, ITERS - 2, last_one=True)

            def ready(key, it, last_one=False):
                k = jobs.index[key]
                if last_one:
                    k -= sum(1 for x, _ in order[:k] if x[0] == "V")
                return s["product_ready"], it * len(order) + k + 1

            def out_of_bank(key):
                return c.bank[jobs.index[key] % NB][:, 0:4 * LM].rearrange("p (c l) -> p c l", c=4)

            @block.scalar
            def _(act):
                def iterate(it, last_one=False):
                    for key in jobs.by("s"):
                        name, g = key
                        if last_one and name == "V":
                            continue
                        act.wait_ge(*ready(key, it, last_one))
                        dst, scale = {"AT": (AT, 1.0), "V": (c.V, 0.25), "VT": (c.VT, 0.25)}[name]
                        if name == "V":
                            act.wait_ge(*ready(("VT", g), it))
                        nc.scalar.mul(group(dst, g), out_of_bank(key), scale).then_inc(s["scalar_took"], 1)

                iterate(0)
                for it in range(1, ITERS - 1):
                    iterate(it)
                iterate(ITERS - 1, last_one=True)

            @block.vector
            def _(dve):
                step = Steps(dve, s["vector_step"])
                for i, a in enumerate((7.0, 15.0, 13.0)):
                    for half in range(2):
                        r = slice(64 * half, 64 * half + 64)
                        step.mark(nc.vector.tensor_scalar(eyes[r, i, :], c.ident[r, r], a, None, ALU.mult))
                dve.wait_ge(s["vector_step"], step.n)

                def iterate(it, last_one=False):
                    for key in jobs.by("v"):
                        name, g = key
                        dve.wait_ge(*ready(key, it, last_one))
                        eye = eyes[:, {"A": 0, "C": 1, "E": 2}[name], :].unsqueeze(1).to_broadcast([P, 4, LM])
                        nc.vector.scalar_tensor_tensor(group(R, g), out_of_bank(key), -1.0, eye, ALU.mult,
                                                       ALU.add).then_inc(s["vector_took"], 1)

                iterate(0)
                for it in range(1, ITERS - 1):
                    iterate(it)
                iterate(ITERS - 1, last_one=True)


def nystrom_apply(c):
    nc = c.nc
    with ExitStack() as mem:
        Zdiag = mem.enter_context(nc.sbuf_tensor("nys_Z", [P, COMBOS, 32], F32))
        SVT = mem.enter_context(nc.sbuf_tensor("nys_SVT", [HF, 2, T], F32))
        order = [(("Z",), "v")] + [(("sv", hh, g), "sv"[hh]) for g in range(2) for hh in range(2)]
        order += [(("out", t), "v") for t in range(0, NT, 2)]
        with stage(nc, JOB_SEMS + "z_zero") as (block, s):
            jobs = Jobs(c, s, order)

            @block.gpsimd
            def _(pool):
                nc.gpsimd.memset(Zdiag[:, :, :], 0.0).then_inc(s["z_zero"], 1)

            @block.tensor
            def _(pe):
                for key, _ in order:
                    kind, bank = key[0], jobs.bank(key)
                    jobs.bank_free(pe, key)
                    if kind == "Z":
                        for co in range(COMBOS):
                            for half in range(2):
                                r = slice(64 * half, 64 * half + 64)
                                last = pe.matmul(bank[r, co * HD:(co + 1) * HD], c.VT[r, co, :], c.W[r, co, :], start=True,
                                                 stop=True, tile_position=(64 * half, 64 * half))
                    elif kind == "sv":
                        _, hh, g = key
                        pe.wait_ge(*jobs.taken(("Z",)))
                        for j in range(3):
                            p = 3 * hh + j
                            for b2 in range(2):
                                b = 2 * g + b2
                                last = pe.matmul(bank[32 * j:32 * j + 32, b2 * N:(b2 + 1) * N], Zdiag[:, combo(b, p), :],
                                                 c.k1T[:, p, b * N:(b + 1) * N], start=True, stop=True,
                                                 tile_position=(0, 32 * j))
                    else:
                        t0 = key[1]
                        for hh in range(2):
                            pe.wait_ge(*jobs.taken(("sv", hh, t0 // 4)))
                        for i in range(2):
                            t = t0 + i
                            for k in range(2):
                                last = pe.matmul(bank[:, i * D:(i + 1) * D], SVT[:, k, t * P:(t + 1) * P], c.tile["nys_proj"][:, k, :],
                                                 start=(k == 0), stop=(k == 1))
                    last.then_inc(s["product_ready"], 1)

            @block.scalar
            def _(act):
                for key in jobs.by("s"):
                    g = key[2]
                    act.wait_ge(*jobs.ready(key))
                    nc.scalar.copy(SVT[:, 0, g * BANK:(g + 1) * BANK], jobs.bank(key)[0:HF, :]).then_inc(s["scalar_took"], 1)

            @block.vector
            def _(dve):
                step = Steps(dve, s["vector_step"])
                step.then(nc.vector.tensor_tensor(c.H[:, :, :], c.H[:, :, :], c.Vtok[:, :, :], ALU.add))
                dve.wait_ge(*jobs.ready(("Z",)))
                dve.wait_ge(s["z_zero"], 1)
                src = jobs.bank(("Z",))[:, 0:COMBOS * HD].rearrange("p (c d) -> p c d", c=COMBOS)
                nc.vector.tensor_copy(Zdiag[0:64, :, 0:HD], src[0:64])
                nc.vector.tensor_copy(Zdiag[64:P, :, HD:32], src[64:P]).then_inc(s["vector_took"], 1)
                for g in range(2):
                    dve.wait_ge(*jobs.ready(("sv", 1, g)))
                    nc.vector.tensor_copy(SVT[:, 1, g * BANK:(g + 1) * BANK], jobs.bank(("sv", 1, g))[0:HF, :]
                                          ).then_inc(s["vector_took"], 1)
                add_rows(c, dve, step, jobs, s, "out", c.row("nys_b_proj"))


class ExpertRing:

    def __init__(self, c, scope):
        self.w1 = [c.sb(f"expert_w1_{i}", [HF, 2, FF], scope) for i in range(2)]
        self.w2 = [c.sb(f"expert_w2_{i}", [P, FT, D], scope) for i in range(2)]
        self.b1 = [c.sb(f"expert_b1_{i}", [P, FT], scope) for i in range(2)]
        self.landed = [c.ctx.enter_context(c.nc.semaphore(f"expert_landed{i}")) for i in range(2)]
        self.base = 0

    def prefetch(self, sp, w1, w2, b1=None):
        for e in range(2):
            sp.dma_start(self.w1[e][:, :, :], w1[e]).then_inc(self.landed[e], 16)
            sp.dma_start(self.w2[e][:, :, :], w2[e]).then_inc(self.landed[e], 16)
            if b1 is not None:
                sp.dma_start(self.b1[e][:, :], b1[e]).then_inc(self.landed[e], 16)


def pairs_of(w):
    return w.rearrange("(n two) p m -> n two p m" if len(w.shape) == 3 else "(n two) p k f -> n two p k f", two=2)


def softmax_rows(c, dve, step, s, logits, work, shape):
    nc = c.nc
    mx, sm = work
    step.then(nc.vector.tensor_reduce(mx, logits, AX.X, ALU.max))
    nc.vector.tensor_tensor(logits, logits, mx.unsqueeze(2).to_broadcast(shape), ALU.subtract).then_inc(s["shifted"], 1)
    dve.wait_ge(s["exped"], 1)
    step.then(nc.vector.tensor_reduce(sm, logits, AX.X, ALU.add))
    step.then(nc.vector.reciprocal(sm, sm))
    step.then(nc.vector.tensor_tensor(logits, logits, sm.unsqueeze(2).to_broadcast(shape), ALU.mult))


def pick_first_best(c, step, probs, best, eq, onehot, rank, shape):
    nc = c.nc
    bc = lambda m: m.unsqueeze(2).to_broadcast(shape)
    step.then(nc.vector.tensor_reduce(best, probs, AX.X, ALU.max))
    step.then(nc.vector.tensor_tensor(eq, probs, bc(best), ALU.is_equal))
    step.then(nc.vector.tensor_tensor(eq, eq, rank.unsqueeze(1).to_broadcast(shape), ALU.mult))
    step.then(nc.vector.tensor_reduce(c.pick_top[:, :], eq, AX.X, ALU.max))
    step.then(nc.vector.tensor_tensor(onehot, eq, bc(c.pick_top[:, :]), ALU.is_equal))


def route_top2(c, router, gates, eps, b2=None):
    nc = c.nc
    E = 8
    shape = [P, NT, E]
    with ExitStack() as mem:
        def sb(name, shape_):
            return mem.enter_context(nc.sbuf_tensor(name + str(c.uid()), shape_, F32))
        probs, eq, one1, one2 = sb("probs", shape), sb("eq", shape), sb("first", shape), sb("second", shape)
        mx, sm, m1, m2, tot = (sb(n, [P, NT]) for n in ("mx", "sm", "m1", "m2", "tot"))
        gatesT = sb("gatesT", [E, T])
        order = [(("logits",), "v")]
        if b2 is not None:
            order += [(("turn", g), "v") for g in range(2)] + [(("out", t), "v") for t in range(0, NT, 2)]
        with stage(nc, JOB_SEMS + "shifted exped gates_ready") as (block, s):
            jobs = Jobs(c, s, order)

            @block.tensor
            def _(pe):
                for name in ("moe1_gate", "moe1_b2"):
                    pe.wait_ge(c.weights_in[name], 16)
                for key, _ in order:
                    bank = jobs.bank(key)
                    if key[0] == "logits":
                        for t in range(NT):
                            for k in range(2):
                                last = pe.matmul(bank[:, t * E:(t + 1) * E], c.XT[:, k, t * P:(t + 1) * P], router[:, k, :],
                                                 start=(k == 0), stop=(k == 1))
                    elif key[0] == "turn":
                        pe.wait_ge(s["gates_ready"], 1)
                        for i in range(4):
                            last = pe.transpose(bank[0:E, i * P:(i + 1) * P], gates[:, 4 * key[1] + i, :], c.ident[:, :])
                    else:
                        pe.wait_ge(*jobs.taken(("turn", 1)))
                        for i in range(2):
                            t = key[1] + i
                            last = pe.matmul(bank[:, i * D:(i + 1) * D], gatesT[:, t * P:(t + 1) * P], b2[:, :],
                                             start=True, stop=True)
                    last.then_inc(s["product_ready"], 1)

            @block.scalar
            def _(act):
                act.wait_ge(s["shifted"], 1)
                nc.scalar.activation(probs[:, :, :], probs[:, :, :], ACT.Exp).then_inc(s["exped"], 1)

            @block.vector
            def _(dve):
                step = Steps(dve, s["vector_step"])
                dve.wait_ge(*jobs.ready(("logits",)))
                nc.vector.tensor_copy(probs[:, :, :], jobs.bank(("logits",))[:, 0:NT * E].rearrange(
                    "p (t e) -> p t e", e=E)).then_inc(s["vector_took"], 1)
                dve.wait_ge(*jobs.taken(("logits",)))
                softmax_rows(c, dve, step, s, probs[:, :, :], (mx[:, :], sm[:, :]), shape)
                rank = c.rank[:, 0:E]
                pick_first_best(c, step, probs[:, :, :], m1[:, :], eq[:, :, :], one1[:, :, :], rank, shape)
                step.then(nc.vector.scalar_tensor_tensor(probs[:, :, :], one1[:, :, :], -2.0, probs[:, :, :], ALU.mult,
                                                         ALU.add))
                pick_first_best(c, step, probs[:, :, :], m2[:, :], eq[:, :, :], one2[:, :, :], rank, shape)
                step.then(nc.vector.tensor_tensor(tot[:, :], m1[:, :], m2[:, :], ALU.add))
                if eps:
                    step.then(nc.vector.tensor_scalar(tot[:, :], tot[:, :], eps, None, ALU.add))
                step.then(nc.vector.reciprocal(tot[:, :], tot[:, :]))
                for one, m in ((one1, m1), (one2, m2)):
                    step.then(nc.vector.tensor_tensor(m[:, :], m[:, :], tot[:, :], ALU.mult))
                    step.then(nc.vector.tensor_tensor(one[:, :, :], one[:, :, :], m[:, :].unsqueeze(2).to_broadcast(shape),
                                                      ALU.mult))
                nc.vector.tensor_tensor(gates[:, :, :], one1[:, :, :], one2[:, :, :], ALU.add).then_inc(s["gates_ready"], 1)
                if b2 is not None:
                    for g in range(2):
                        dve.wait_ge(*jobs.ready(("turn", g)))
                        nc.vector.tensor_copy(gatesT[:, g * BANK:(g + 1) * BANK], jobs.bank(("turn", g))[0:E, :]
                                              ).then_inc(s["vector_took"], 1)
                    add_rows(c, dve, step, jobs, s, "out")


def experts_top2(c, name, gates, func, b1=None):
    nc, ring = c.nc, c.ring
    E = 8
    w1, w2 = c.w[name + "_w1"], c.w[name + "_w2"]
    with ExitStack() as mem:
        hid = mem.enter_context(nc.sbuf_tensor(name + "_hidden", [P, FT, T], F32))
        order = [(("h", m, g), "s") for g in range(2) for m in range(FT)] + [(("out", t), "v") for t in range(0, NT, 2)]
        LOADS = 16 * (2 if b1 is None else 3)
        NJ, NS, NV = len(order), 2 * FT, NT // 2
        assert NJ % NB == 0
        with stage(nc, JOB_SEMS) as (block, s):
            jobs = Jobs(c, s, order)
            base = ring.base

            def in_expert(at, e):
                sem, n = at
                per = {id(s["product_ready"]): NJ, id(s["scalar_took"]): NS, id(s["vector_took"]): NV}[id(sem)]
                return sem, e * per + n

            @block.sync
            def _(sp):
                with sp.Fori(1, E // 2, 1) as i:
                    for u in range(2):
                        sp.wait_ge(s["product_ready"], (2 * i - 1 + u) * NJ)
                        sp.dma_start(ring.w1[u][:, :, :], pairs_of(w1)[i, u]).then_inc(ring.landed[u], 16)
                        sp.dma_start(ring.w2[u][:, :, :], pairs_of(w2)[i, u]).then_inc(ring.landed[u], 16)
                        if b1 is not None:
                            sp.dma_start(ring.b1[u][:, :], pairs_of(b1)[i, u]).then_inc(ring.landed[u], 16)

            @block.tensor
            def _(pe):
                def expert(e, i, u, first=False):
                    pe.wait_ge(ring.landed[u], base + LOADS * (i + 1))
                    for k_, (key, _) in enumerate(order):
                        bank = jobs.bank(key)
                        if k_ >= NB:
                            pe.wait_ge(*in_expert(jobs.taken(order[k_ - NB][0]), e))
                        elif not first:
                            pe.wait_ge(*in_expert(jobs.taken(order[k_ + NJ - NB][0]), e - 1))
                        if key[0] == "h":
                            _, m, g = key
                            for k in range(2):
                                last = pe.matmul(bank, ring.w1[u][:, k, m * P:(m + 1) * P],
                                                 c.XT[:, k, g * BANK:(g + 1) * BANK], start=(k == 0), stop=(k == 1))
                        else:
                            pe.wait_ge(*in_expert(jobs.taken(("h", FT - 1, key[1] // 4)), e))
                            for j in range(2):
                                t = key[1] + j
                                for m in range(FT):
                                    last = pe.matmul(bank[:, j * D:(j + 1) * D], hid[:, m, t * P:(t + 1) * P],
                                                     ring.w2[u][:, m, :], start=(m == 0), stop=(m == FT - 1))
                        last.then_inc(s["product_ready"], 1)

                expert(0, 0, 0, first=True)
                expert(1, 0, 1)
                with pe.Fori(1, E // 2, 1) as i:
                    for u in range(2):
                        expert(2 * i + u, i, u)

            @block.scalar
            def _(act):
                def expert(e, i, u):
                    for key in jobs.by("s"):
                        _, m, g = key
                        act.wait_ge(*in_expert(jobs.ready(key), e))
                        dst = hid[:, m, g * BANK:(g + 1) * BANK]
                        b = 0.0 if b1 is None else ring.b1[u][:, m:m + 1]
                        nc.scalar.activation(dst, jobs.bank(key), func, bias=b).then_inc(s["scalar_took"], 1)

                with act.Fori(0, E // 2, 1) as i:
                    for u in range(2):
                        expert(2 * i + u, i, u)

            @block.vector
            def _(dve):
                def expert(e, i, u, first=False):
                    for n, key in enumerate(jobs.by("v")):
                        if not (first and n == 0):
                            dve.wait_ge(s["vector_took"], e * NV + n)
                        dve.wait_ge(*in_expert(jobs.ready(key), e))
                        for j in range(2):
                            t = key[1] + j
                            gate = gates.rearrange("p t (n u) -> p t n u", u=2)[:, t, i, u:u + 1]
                            last = nc.vector.scalar_tensor_tensor(c.H[:, t, :], jobs.bank(key)[:, j * D:(j + 1) * D], gate,
                                                                  c.H[:, t, :], ALU.mult, ALU.add)
                        last.then_inc(s["vector_took"], 1)

                expert(0, 0, 0, first=True)
                expert(1, 0, 1)
                with dve.Fori(1, E // 2, 1) as i:
                    for u in range(2):
                        expert(2 * i + u, i, u)
            ring.base += LOADS * (E // 2)


def top2_ffn(c, name, router, func, eps, b1=None, b2=None):
    with ExitStack() as mem:
        gates = mem.enter_context(c.nc.sbuf_tensor(name + "_gates", [P, NT, 8], F32))
        route_top2(c, router, gates, eps, b2)
        experts_top2(c, name, gates, func, b1)


TTT = 512
TH = TTT // P
LR = 0.01


def test_time_training(c):
    nc = c.nc
    with ExitStack() as mem:
        def sb(name, shape):
            return mem.enter_context(nc.sbuf_tensor(name, shape, F32))
        U, S, V = sb("ttt_u", [P, B, TTT]), sb("ttt_s", [P, B, TTT]), sb("ttt_v", [P, B, TTT])
        SV, A, DU, DV = (sb("ttt_" + n, [P, B, TTT]) for n in ("sv", "a", "du", "dv"))
        AT = sb("ttt_aT", [P, TH, B * P])
        G, GT = sb("ttt_g", [P, B, D]), sb("ttt_gT", [HF, 2, B * P])
        gate = sb("ttt_gate", [P, TH, B * P])
        order = []
        for b in range(B):
            order += [(("u", b), "s"), (("v", b), "v")]
        order += [(("aT", m), "s") for m in range(TH)]
        order += [(("o", b), "v") for b in range(B)]
        order += [(("gT", k), "s") for k in range(2)]
        order += [(("da", b), "v") for b in range(B)]
        order += [(("g1", m2), "v") for m2 in range(2)]
        order += [(("g2", k), "v") for k in range(2)] + [(("g0", k), "v") for k in range(2)]
        for m in range(TH):
            order += [(("u1", m), "s"), (("v1", m), "v")]
        order += [(("o1", b2), "v") for b2 in range(2)]
        with stage(nc, JOB_SEMS + "u_copied hidden_ready g_ready") as (block, s):
            jobs = Jobs(c, s, order)
            tok = lambda b, chunk: slice((TPB * b + chunk) * P, (TPB * b + chunk + 1) * P)
            chunk1 = lambda k: c.XT[:, k, :].rearrange("p (b i n) -> p b i n", b=B, i=TPB)[:, :, 1, :]

            @block.tensor
            def _(pe):
                for name in ("ttt_w0", "ttt_w1", "ttt_w2", "ttt_w1T"):
                    pe.wait_ge(c.weights_in[name], 16)
                for key, _ in order:
                    kind, n, bank = key[0], key[1], jobs.bank(key)
                    jobs.bank_free(pe, key)
                    if kind in "uv":
                        w = c.tile["ttt_w0"] if kind == "u" else c.tile["ttt_w2"]
                        for k in range(2):
                            last = pe.matmul(bank, c.XT[:, k, tok(n, 0)], w[:, k, :], start=(k == 0), stop=(k == 1))
                    elif kind == "aT":
                        pe.wait_ge(s["hidden_ready"], B)
                        for b in range(B):
                            last = pe.transpose(bank[:, b * P:(b + 1) * P], A[:, b, n * P:(n + 1) * P], c.ident[:, :])
                    elif kind == "o":
                        pe.wait_ge(*jobs.taken(("aT", TH - 1)))
                        for m in range(TH):
                            last = pe.matmul(bank[:, 0:D], AT[:, m, n * P:(n + 1) * P], c.tile["ttt_w1"][:, m, :],
                                             start=(m == 0), stop=(m == TH - 1))
                    elif kind == "gT":
                        pe.wait_ge(s["g_ready"], B)
                        for b in range(B):
                            last = pe.transpose(bank[0:HF, b * P:(b + 1) * P], G[:, b, n * HF:(n + 1) * HF], c.ident[:, :])
                    elif kind == "da":
                        for k in range(2):
                            pe.wait_ge(*jobs.taken(("gT", k)))
                            last = pe.matmul(bank, GT[:, k, n * P:(n + 1) * P], c.tile["ttt_w1T"][:, k, :],
                                             start=(k == 0), stop=(k == 1))
                    elif kind == "g1":
                        for i in range(2):
                            for b in range(B):
                                last = pe.matmul(bank[:, i * D:(i + 1) * D], A[:, b, (2 * n + i) * P:(2 * n + i + 1) * P],
                                                 G[:, b, :], start=(b == 0), stop=(b == B - 1))
                    elif kind in ("g0", "g2"):
                        src = DU if kind == "g0" else DV
                        pe.wait_ge(*jobs.taken(("da", B - 1)))
                        for b in range(B):
                            last = pe.matmul(bank[0:HF, :], c.XN[:, TPB * b, n * HF:(n + 1) * HF], src[:, b, :],
                                             start=(b == 0), stop=(b == B - 1))
                    elif kind in ("u1", "v1"):
                        w = c.tile["ttt_w0"] if kind == "u1" else c.tile["ttt_w2"]
                        for k in range(2):
                            pe.wait_ge(*jobs.taken(("g0", k)))
                            last = pe.matmul(bank.rearrange("p (b n) -> p b n", b=B), w[:, k, n * P:(n + 1) * P], chunk1(k),
                                             start=(k == 0), stop=(k == 1))
                    else:
                        pe.wait_ge(*jobs.taken(("v1", TH - 1)))
                        for i in range(2):
                            b = 2 * n + i
                            for m in range(TH):
                                last = pe.matmul(bank[:, i * D:(i + 1) * D], AT[:, m, b * P:(b + 1) * P], c.tile["ttt_w1"][:, m, :],
                                                 start=(m == 0), stop=(m == TH - 1))
                    last.then_inc(s["product_ready"], 1)

            @block.scalar
            def _(act):
                for b in range(B):
                    act.wait_ge(*jobs.ready(("u", b)))
                    nc.scalar.copy(U[:, b, :], jobs.bank(("u", b))).then_inc(s["scalar_step"], 1)
                    nc.scalar.activation(S[:, b, :], jobs.bank(("u", b)), ACT.Sigmoid).then_inc(s["scalar_took"], 1)
                for m in range(TH):
                    act.wait_ge(*jobs.ready(("aT", m)))
                    nc.scalar.copy(AT[:, m, :], jobs.bank(("aT", m))).then_inc(s["scalar_took"], 1)
                for k in range(2):
                    act.wait_ge(*jobs.ready(("gT", k)))
                    nc.scalar.copy(GT[:, k, :], jobs.bank(("gT", k))[0:HF, :]).then_inc(s["scalar_took"], 1)
                for m in range(TH):
                    act.wait_ge(*jobs.ready(("u1", m)))
                    nc.scalar.activation(gate[:, m, :], jobs.bank(("u1", m)), ACT.Silu).then_inc(s["scalar_took"], 1)

            @block.vector
            def _(dve):
                step = Steps(dve, s["vector_step"])
                for b in range(B):
                    dve.wait_ge(*jobs.ready(("v", b)))
                    nc.vector.tensor_copy(V[:, b, :], jobs.bank(("v", b))).then_inc(s["vector_took"], 1)
                    dve.wait_ge(*jobs.taken(("u", b)))
                    dve.wait_ge(*jobs.taken(("v", b)))
                    step.then(nc.vector.tensor_tensor(SV[:, b, :], S[:, b, :], V[:, b, :], ALU.mult))
                    nc.vector.tensor_tensor(A[:, b, :], U[:, b, :], SV[:, b, :], ALU.mult).then_inc(s["hidden_ready"], 1)
                for b in range(B):
                    step.mark(nc.vector.tensor_tensor(V[:, b, :], U[:, b, :], S[:, b, :], ALU.mult))
                for b in range(B):
                    dve.wait_ge(s["vector_step"], step.n - B + 1 if b == 0 else step.n)
                    step.then(nc.vector.tensor_tensor(U[:, b, :], U[:, b, :], V[:, b, :], ALU.subtract))
                    step.mark(nc.vector.scalar_tensor_tensor(SV[:, b, :], U[:, b, :], 1.0, SV[:, b, :], ALU.add, ALU.mult))
                for b in range(B):
                    dve.wait_ge(*jobs.ready(("o", b)))
                    o = jobs.bank(("o", b))[:, 0:D]
                    step.then(nc.vector.tensor_tensor(G[:, b, :], o, c.XN[:, TPB * b, :], ALU.subtract))
                    nc.vector.tensor_scalar(G[:, b, :], G[:, b, :], 2.0 / (B * P * D), None, ALU.mult).then_inc(s["g_ready"], 1)
                    nc.vector.tensor_tensor(c.H[:, TPB * b, :], c.H[:, TPB * b, :], o, ALU.add).then_inc(s["vector_took"], 1)
                for b in range(B):
                    dve.wait_ge(*jobs.ready(("da", b)))
                    nc.vector.tensor_tensor(DV[:, b, :], jobs.bank(("da", b)), V[:, b, :], ALU.mult)
                    nc.vector.tensor_tensor(DU[:, b, :], jobs.bank(("da", b)), SV[:, b, :], ALU.mult).then_inc(s["vector_took"], 1)
                for m2 in range(2):
                    dve.wait_ge(*jobs.ready(("g1", m2)))
                    w = c.tile["ttt_w1"][:, 2 * m2:2 * m2 + 2, :]
                    nc.vector.scalar_tensor_tensor(w, jobs.bank(("g1", m2))[:, 0:2 * D].rearrange("p (i d) -> p i d", i=2),
                                                   -LR, w, ALU.mult, ALU.add).then_inc(s["vector_took"], 1)
                for kind, w in (("g2", c.tile["ttt_w2"]), ("g0", c.tile["ttt_w0"])):
                    for k in range(2):
                        dve.wait_ge(*jobs.ready((kind, k)))
                        nc.vector.scalar_tensor_tensor(w[:, k, :], jobs.bank((kind, k))[0:HF, :], -LR, w[:, k, :], ALU.mult,
                                                       ALU.add).then_inc(s["vector_took"], 1)
                for m in range(TH):
                    dve.wait_ge(*jobs.ready(("v1", m)))
                    dve.wait_ge(*jobs.taken(("u1", m)))
                    nc.vector.tensor_tensor(AT[:, m, :], gate[:, m, :], jobs.bank(("v1", m)), ALU.mult
                                            ).then_inc(s["vector_took"], 1)
                for b2 in range(2):
                    dve.wait_ge(*jobs.ready(("o1", b2)))
                    h = c.H.rearrange("p (b i) d -> p b i d", b=B)[:, 2 * b2:2 * b2 + 2, 1, :]
                    nc.vector.tensor_tensor(h, h, jobs.bank(("o1", b2))[:, 0:2 * D].rearrange("p (i d) -> p i d", i=2),
                                            ALU.add).then_inc(s["vector_took"], 1)


SE = 16
CAP = 64
SLOTS = SE * CAP
EP = SE // 2


def switch_ffn(c):
    nc = c.nc
    with ExitStack() as mem:
        def sb(name, shape):
            return mem.enter_context(nc.sbuf_tensor(name, shape, F32))
        NM = sb("sw_normed", [P, NT, D])
        best, drop, slot = sb("sw_best", [P, NT]), sb("sw_drop", [P, NT]), sb("sw_slot", [P, NT])
        DIS = sb("sw_dispatch", [P, NT * SLOTS])
        DT_ = sb("sw_dispatchT", [P, NT, EP, P])
        XE = sb("sw_inputs", [HF, 2, EP, 2, 2, 2, CAP])
        EO = DIS.rearrange("p x -> p x")[:, 0:EP * B * D].rearrange("p (e b d) -> p e b d", e=EP, b=B)
        DIS = DIS.rearrange("p (t x) -> p t x", t=NT)
        switch_route(c, NM, best, drop, slot)
        switch_dispatch(c, NM, slot, DIS, DT_, XE)
        switch_experts(c, XE, EO)
        switch_combine(c, NM, best, drop, DT_, EO)


def switch_route(c, NM, best, drop, slot):
    nc = c.nc
    E = SE
    shape = [P, NT, E]
    with ExitStack() as mem:
        def sb(name, shape_):
            return mem.enter_context(nc.sbuf_tensor(name, shape_, F32))
        square = sb("sw_square", [P, 2, D])
        ss, rms = sb("sw_ss", [P, NT]), sb("sw_rms", [P, NT])
        probs, eq, one, work = sb("sw_probs", shape), sb("sw_eq", shape), sb("sw_one", shape), sb("sw_work", shape)
        mx, sm = sb("sw_mx", [P, NT]), sb("sw_sm", [P, NT])
        tri, full = sb("sw_tri", [P, P]), sb("sw_full", [P, P])
        names = sb("sw_names", [P, B, TPB, E])
        place = sb("sw_place", [P, NT])
        order = [(("turn", g, k), "sv"[k]) for g in range(2) for k in range(2)]
        order += [(("logits",), "v"), (("count",), "v")]
        with stage(nc, JOB_SEMS + "squared rms_ready normed pool_step shifted exped chosen") as (block, s):
            jobs = Jobs(c, s, order)

            @block.gpsimd
            def _(pool):
                step = Steps(pool, s["pool_step"])
                step.mark(nc.gpsimd.memset(full[:, :], 1.0))
                step.then(nc.gpsimd.memset(tri[:, :], 1.0))
                step.mark(nc.gpsimd.affine_select(out=tri[:, :], in_=tri[:, :], compare_op=ALU.is_ge, fill=0.0, base=0,
                                                  pattern=[[1, P]], channel_multiplier=-1))
                for b in range(B):
                    for i in range(TPB):
                        pattern = [[1, E]] if b % 2 == 0 else [[2, EP], [-1, 2]]
                        step.mark(nc.gpsimd.iota(names[:, b, i, :], pattern=pattern, base=b % 2, channel_multiplier=0,
                                                 allow_small_or_imprecise_dtypes=True))

            @block.scalar
            def _(act):
                for t in range(NT):
                    if t >= 2:
                        act.wait_ge(s["squared"], t - 1)
                    nc.scalar.activation(square[:, t % 2, :], c.XN[:, t, :], ACT.Square,
                                         accum_out=ss[:, t:t + 1]).then_inc(s["squared"], 1)
                act.wait_ge(s["squared"], NT)
                nc.scalar.activation(rms[:, :], ss[:, :], ACT.Sqrt, bias=c.eps6, scale=1.0 / D).then_inc(s["rms_ready"], 1)
                for g in range(2):
                    act.wait_ge(*jobs.ready(("turn", g, 0)))
                    nc.scalar.copy(c.XT[:, 0, g * BANK:(g + 1) * BANK], jobs.bank(("turn", g, 0))[0:HF, :]
                                   ).then_inc(s["scalar_took"], 1)
                act.wait_ge(s["shifted"], 1)
                nc.scalar.activation(probs[:, :, :], probs[:, :, :], ACT.Exp).then_inc(s["exped"], 1)

            @block.tensor
            def _(pe):
                pe.wait_ge(c.weights_in["switch_router"], 16)
                for key, _ in order:
                    kind, bank = key[0], jobs.bank(key)
                    if kind == "turn":
                        _, g, k = key
                        pe.wait_ge(s["normed"], 4 * (g + 1))
                        for i in range(4):
                            last = pe.transpose(bank[0:HF, i * P:(i + 1) * P], NM[:, 4 * g + i, k * HF:(k + 1) * HF],
                                                c.ident[:, :])
                    elif kind == "logits":
                        for k in range(2):
                            pe.wait_ge(*jobs.taken(("turn", 1, k)))
                        for t in range(NT):
                            for k in range(2):
                                last = pe.matmul(bank[:, t * E:(t + 1) * E], c.XT[:, k, t * P:(t + 1) * P],
                                                 c.tile["switch_router"][:, k, :], start=(k == 0), stop=(k == 1))
                    else:
                        pe.wait_ge(s["chosen"], 1)
                        pe.wait_ge(s["pool_step"], 3 + NT)
                        o = one.rearrange("p (b i) e -> p b i e", b=B)
                        dst = bank[:, 0:2 * B * E].rearrange("p (i b e) -> p i b e", i=2, b=B)
                        pe.matmul(dst[:, 0], tri[:, :], o[:, :, 0, :], start=True, stop=True)
                        pe.matmul(dst[:, 1], full[:, :], o[:, :, 0, :], start=True, stop=False)
                        last = pe.matmul(dst[:, 1], tri[:, :], o[:, :, 1, :], start=False, stop=True)
                    last.then_inc(s["product_ready"], 1)

            @block.vector
            def _(dve):
                step = Steps(dve, s["vector_step"])
                dve.wait_ge(s["rms_ready"], 1)
                step.then(nc.vector.reciprocal(rms[:, :], rms[:, :]))
                for t in range(NT):
                    nc.vector.scalar_tensor_tensor(NM[:, t, :], c.XN[:, t, :], rms[:, t:t + 1], c.row("switch_ln_w"),
                                                   ALU.mult, ALU.mult).then_inc(s["normed"], 1)
                for g in range(2):
                    dve.wait_ge(*jobs.ready(("turn", g, 1)))
                    nc.vector.tensor_copy(c.XT[:, 1, g * BANK:(g + 1) * BANK], jobs.bank(("turn", g, 1))[0:HF, :]
                                          ).then_inc(s["vector_took"], 1)
                dve.wait_ge(*jobs.ready(("logits",)))
                nc.vector.tensor_copy(probs[:, :, :], jobs.bank(("logits",))[:, 0:NT * E].rearrange(
                    "p (t e) -> p t e", e=E)).then_inc(s["vector_took"], 1)
                dve.wait_ge(*jobs.taken(("logits",)))
                softmax_rows(c, dve, step, s, probs[:, :, :], (mx[:, :], sm[:, :]), shape)
                pick_first_best(c, step, probs[:, :, :], best[:, :], eq[:, :, :], one[:, :, :], c.rank[:, 0:E], shape)
                nc.vector.tensor_copy(work[:, :, :], one[:, :, :]).then_inc(s["chosen"], 1)
                dve.wait_ge(s["chosen"], 1)
                dve.wait_ge(s["pool_step"], 3 + NT)
                step.then(nc.vector.tensor_tensor(eq[:, :, :], one[:, :, :], names.rearrange("p b i e -> p (b i) e"), ALU.mult))
                step.then(nc.vector.tensor_reduce(place[:, :], eq[:, :, :], AX.X, ALU.add))
                dve.wait_ge(*jobs.ready(("count",)))
                src = jobs.bank(("count",))[:, 0:2 * B * E].rearrange("p (i b e) -> p b i e", i=2, b=B)
                w4 = work.rearrange("p (b i) e -> p b i e", b=B)
                nc.vector.tensor_tensor(w4, w4, src, ALU.mult).then_inc(s["vector_took"], 1)
                dve.wait_ge(*jobs.taken(("count",)))
                step.then(nc.vector.tensor_reduce(slot[:, :], work[:, :, :], AX.X, ALU.add))
                step.then(nc.vector.tensor_scalar(drop[:, :], slot[:, :], float(CAP), None, ALU.is_gt))
                step.then(nc.vector.scalar_tensor_tensor(slot[:, :], place[:, :], float(CAP), slot[:, :], ALU.mult, ALU.add))
                step.then(nc.vector.tensor_scalar(slot[:, :], slot[:, :], -1.0, None, ALU.add))
                step.then(nc.vector.scalar_tensor_tensor(slot[:, :], drop[:, :], float(4 * SLOTS), slot[:, :], ALU.mult,
                                                         ALU.add))


def switch_dispatch(c, NM, slot, DIS, DT_, XE):
    nc = c.nc
    with ExitStack() as mem:
        numbers = mem.enter_context(nc.sbuf_tensor("sw_numbers", [P, SLOTS], F32))
        order = []
        for b in range(B):
            for sh in range(2):
                order += [(("xe", b, sh, k), "sv"[k]) for k in range(2)]
            for i in range(TPB):
                order += [(("turn", TPB * b + i, q), "sv"[q]) for q in range(2)]
        with stage(nc, JOB_SEMS + "numbered dispatched") as (block, s):
            jobs = Jobs(c, s, order)

            @block.gpsimd
            def _(pool):
                nc.gpsimd.iota(numbers[:, :], pattern=[[1, SLOTS]], base=0, channel_multiplier=0,
                               allow_small_or_imprecise_dtypes=True).then_inc(s["numbered"], 1)

            @block.tensor
            def _(pe):
                for key, _ in order:
                    bank = jobs.bank(key)
                    jobs.bank_free(pe, key)
                    if key[0] == "xe":
                        _, b, sh, k = key
                        pe.wait_ge(s["dispatched"], TPB * (b + 1))
                        for i in range(TPB):
                            t = TPB * b + i
                            last = pe.matmul(bank[0:HF, :], NM[:, t, k * HF:(k + 1) * HF],
                                             DIS[:, t, sh * BANK:(sh + 1) * BANK], start=(i == 0), stop=(i == TPB - 1))
                    else:
                        _, t, q = key
                        for i in range(4):
                            at = (4 * q + i) * P
                            last = pe.transpose(bank[:, i * P:(i + 1) * P], DIS[:, t, at:at + P], c.ident[:, :])
                    last.then_inc(s["product_ready"], 1)

            def take(eng, copy, took, who):
                for key in jobs.by(who):
                    eng.wait_ge(*jobs.ready(key))
                    bank = jobs.bank(key)
                    if key[0] == "xe":
                        _, b, sh, k = key
                        src = bank[0:HF, :].rearrange("p (e u c) -> p e u c", e=4, u=2)
                        for u in range(2):
                            last = copy(XE[:, k, 4 * sh:4 * sh + 4, u ^ (b % 2), b // 2, u, :], src[:, :, u, :])
                    else:
                        _, t, q = key
                        last = copy(DT_[:, t, 4 * q:4 * q + 4, :].rearrange("p e n -> p (e n)"), bank)
                    last.then_inc(took, 1)

            @block.scalar
            def _(act):
                take(act, nc.scalar.copy, s["scalar_took"], "s")

            @block.vector
            def _(dve):
                dve.wait_ge(s["numbered"], 1)
                for t in range(NT):
                    nc.vector.tensor_scalar(DIS[:, t, :], numbers[:, :], slot[:, t:t + 1], None,
                                            ALU.is_equal).then_inc(s["dispatched"], 1)
                take(dve, nc.vector.tensor_copy, s["vector_took"], "v")


def switch_experts(c, XE, EO):
    nc, ring = c.nc, c.ring
    w1, w2 = c.w["switch_w1"], c.w["switch_w2"]
    with ExitStack() as mem:
        hid = [mem.enter_context(nc.sbuf_tensor(f"sw_hidden{u}", [P, FT, 4 * CAP], F32)) for u in range(2)]
        order = []
        for u in range(2):
            order += [(("h", u, m2), "s") for m2 in range(FT // 2)]
        order += [(("out", u), "v") for u in range(2)]
        NJ, NS, NV = len(order), 2 * (FT // 2), 2
        assert NJ == NB
        with stage(nc, JOB_SEMS) as (block, s):
            jobs = Jobs(c, s, order)
            base = ring.base

            def in_pair(at, i):
                sem, n = at
                per = {id(s["product_ready"]): NJ, id(s["scalar_took"]): NS, id(s["vector_took"]): NV}[id(sem)]
                return sem, i * per + n

            inputs = XE.rearrange("p k n u s r c -> p k n u (s r c)")

            @block.sync
            def _(sp):
                with sp.Fori(1, EP, 1) as i:
                    for u in range(2):
                        sp.wait_ge(*in_pair(jobs.ready(("out", u)), i - 1))
                        sp.dma_start(ring.w1[u][:, :, :], pairs_of(w1)[i, u]).then_inc(ring.landed[u], 16)
                        sp.dma_start(ring.w2[u][:, :, :], pairs_of(w2)[i, u]).then_inc(ring.landed[u], 16)

            @block.tensor
            def _(pe):
                def pair(i, first=False):
                    for key, _ in order:
                        kind, u = key[0], key[1]
                        bank = jobs.bank(key)
                        if not first:
                            pe.wait_ge(*in_pair(jobs.taken(key), i - 1))
                        if kind == "h":
                            if key[2] == 0:
                                pe.wait_ge(ring.landed[u], base + 32 * (i + 1))
                            for j in range(2):
                                m = 2 * key[2] + j
                                for k in range(2):
                                    last = pe.matmul(bank[:, j * 256:(j + 1) * 256], ring.w1[u][:, k, m * P:(m + 1) * P],
                                                     inputs[:, k, i, u, :], start=(k == 0), stop=(k == 1))
                        else:
                            pe.wait_ge(*in_pair(jobs.taken(("h", u, FT // 2 - 1)), i))
                            for j in range(2):
                                for m in range(FT):
                                    last = pe.matmul(bank[:, j * D:(j + 1) * D], hid[u][:, m, j * P:(j + 1) * P],
                                                     ring.w2[u][:, m, :], start=(m == 0), stop=(m == FT - 1))
                        last.then_inc(s["product_ready"], 1)

                pair(0, first=True)
                with pe.Fori(1, EP, 1) as i:
                    pair(i)

            @block.scalar
            def _(act):
                with act.Fori(0, EP, 1) as i:
                    for key in jobs.by("s"):
                        _, u, m2 = key
                        act.wait_ge(*in_pair(jobs.ready(key), i))
                        nc.scalar.activation(hid[u][:, 2 * m2:2 * m2 + 2, :].rearrange("p m n -> p (m n)"), jobs.bank(key),
                                             ACT.Relu).then_inc(s["scalar_took"], 1)

            @block.vector
            def _(dve):
                with dve.Fori(0, EP, 1) as i:
                    for u in range(2):
                        dve.wait_ge(*in_pair(jobs.ready(("out", u)), i))
                        src = jobs.bank(("out", u))[:, 0:2 * D].rearrange("p (s d) -> p s d", s=2)
                        for half in range(2):
                            r, par = slice(64 * half, 64 * half + 64), u ^ half
                            dst = EO.rearrange("p e (s r) d -> p e s r d", r=2)[r, i, :, par, :]
                            last = nc.vector.tensor_scalar(dst, src[r], 1.0, None, ALU.mult)
                        last.then_inc(s["vector_took"], 1)
            ring.base += 32 * EP


def switch_combine(c, NM, best, drop, DT_, EO):
    nc = c.nc
    with ExitStack() as mem:
        mixed = mem.enter_context(nc.sbuf_tensor("sw_mixed", [P, NT, D], F32))
        order = [(("out", t), "v") for t in range(0, NT, 2)]
        with stage(nc, JOB_SEMS) as (block, s):
            jobs = Jobs(c, s, order)

            @block.tensor
            def _(pe):
                for key, _ in order:
                    for i in range(2):
                        t = key[1] + i
                        for e in range(EP):
                            last = pe.matmul(jobs.bank(key)[:, i * D:(i + 1) * D], DT_[:, t, e, :], EO[:, e, t // TPB, :],
                                             start=(e == 0), stop=(e == EP - 1))
                    last.then_inc(s["product_ready"], 1)

            @block.vector
            def _(dve):
                step = Steps(dve, s["vector_step"])
                step.then(nc.vector.tensor_tensor(c.H[:, :, :], c.H[:, :, :], c.XN[:, :, :], ALU.add))
                for key in jobs.by("v"):
                    dve.wait_ge(*jobs.ready(key))
                    for i in range(2):
                        t = key[1] + i
                        last = nc.vector.scalar_tensor_tensor(mixed[:, t, :], NM[:, t, :], drop[:, t:t + 1],
                                                              jobs.bank(key)[:, i * D:(i + 1) * D], ALU.mult, ALU.add)
                    last.then_inc(s["vector_took"], 1)
                    dve.wait_ge(*jobs.taken(key))
                    for i in range(2):
                        t = key[1] + i
                        step.mark(nc.vector.scalar_tensor_tensor(c.H[:, t, :], mixed[:, t, :], best[:, t:t + 1],
                                                                 c.H[:, t, :], ALU.mult, ALU.add))


def softmax_attention(c):
    nc = c.nc
    with ExitStack() as mem:
        def sb(name, shape):
            return mem.enter_context(nc.sbuf_tensor(name, shape, F32))
        QT, KT, V = sb("att_QT", [P, HG, T]), sb("att_KT", [P, HG, T]), sb("att_V", [P, NT, D])
        AO = sb("att_rows", [P, NT, D])
        attention_project(c, QT, KT, V)
        attention_heads(c, QT, KT, V, AO)
        attention_out(c, AO)


def attention_project(c, QT, KT, V):
    nc = c.nc
    order = [(("qk", m, g), "s") for m in range(2 * HG) for g in range(2)] + [(("v", t), "v") for t in range(0, NT, 2)]
    with stage(nc, JOB_SEMS) as (block, s):
        jobs = Jobs(c, s, order)

        @block.tensor
        def _(pe):
            for name in ("att_qk", "att_v"):
                pe.wait_ge(c.weights_in[name], 16)
            for key, _ in order:
                bank = jobs.bank(key)
                jobs.bank_free(pe, key)
                if key[0] == "qk":
                    _, m, g = key
                    for k in range(2):
                        last = pe.matmul(bank, c.tile["att_qk"][:, k, m * P:(m + 1) * P], c.XT[:, k, g * BANK:(g + 1) * BANK],
                                         start=(k == 0), stop=(k == 1))
                else:
                    for i in range(2):
                        t = key[1] + i
                        for k in range(2):
                            last = pe.matmul(bank[:, i * D:(i + 1) * D], c.XT[:, k, t * P:(t + 1) * P], c.tile["att_v"][:, k, :],
                                             start=(k == 0), stop=(k == 1))
                last.then_inc(s["product_ready"], 1)

        @block.scalar
        def _(act):
            for key in jobs.by("s"):
                _, m, g = key
                act.wait_ge(*jobs.ready(key))
                dst = QT if m < HG else KT
                nc.scalar.activation(dst[:, m % HG, g * BANK:(g + 1) * BANK], jobs.bank(key), ACT.Identity,
                                     bias=c.col("att_b_qk")[:, m:m + 1]).then_inc(s["scalar_took"], 1)

        @block.vector
        def _(dve):
            for key in jobs.by("v"):
                t = key[1]
                dve.wait_ge(*jobs.ready(key))
                nc.vector.tensor_tensor(V[:, t:t + 2, :], jobs.bank(key)[:, 0:2 * D].rearrange("p (t d) -> p t d", t=2),
                                        c.row("att_b_v").unsqueeze(1).to_broadcast([P, 2, D]),
                                        ALU.add).then_inc(s["vector_took"], 1)


def attention_heads(c, QT, KT, V, AO):
    nc = c.nc
    LAG, RINGP = 3, 4
    SCALE = HD ** -0.5
    with ExitStack() as mem:
        def sb(name, shape):
            return mem.enter_context(nc.sbuf_tensor(name, shape, F32))
        prob = sb("att_prob", [P, RINGP, 2, N])
        probT = sb("att_probT", [P, 2, TPB, NH, TPB, P])
        negmax = sb("att_negmax", [P, 48, 2])
        sums, inv = sb("att_sums", [P, NT, NH]), sb("att_inv", [P, NT, NH])
        units = [(b, r, n) for b in range(B) for r in range(4) for n in range(3)]

        def members(u):
            _, r, n = u
            pairs = [(i, hg) for i in range(TPB) for hg in range(HG)]
            return [(i, 4 * hg + r) for i, hg in pairs[2 * n:2 * n + 2]]

        order = []
        for j in range(len(units) + LAG + 2):
            if j < len(units):
                order.append((("s", j), "s"))
            if 0 <= j - LAG < len(units):
                order.append((("t", j - LAG), "s" if j % 4 == 0 else "v"))
            if j >= 12 + LAG + 1 and (j - LAG - 1) % 12 == 0:
                order += [(("o", (j - LAG - 1) // 12 - 1, i), "v") for i in range(TPB)]
        assert len(order) == 2 * len(units) + NT
        with stage(nc, JOB_SEMS + "max_ready exped") as (block, s):
            jobs = Jobs(c, s, order)

            @block.tensor
            def _(pe):
                for key, _ in order:
                    kind, bank = key[0], jobs.bank(key)
                    jobs.bank_free(pe, key)
                    if kind == "s":
                        b = units[key[1]][0]
                        for x, (i, h) in enumerate(members(units[key[1]])):
                            r, t = head_rows(h), TPB * b + i
                            last = pe.matmul(bank[:, x * N:(x + 1) * N], QT[r, h // 4, t * P:(t + 1) * P],
                                             KT[r, h // 4, b * N:(b + 1) * N], start=True, stop=True,
                                             tile_position=(SLOT * (h % 4), 0))
                    elif kind == "t":
                        j = key[1]
                        pe.wait_ge(*jobs.taken(("s", j)))
                        for x in range(2):
                            for kt in range(TPB):
                                at = (2 * x + kt) * P
                                last = pe.transpose(bank[:, at:at + P], prob[:, j % RINGP, x, kt * P:(kt + 1) * P],
                                                    c.ident[:, :])
                    else:
                        _, b, i = key
                        for j in range(12 * b + 8, 12 * b + 12):
                            pe.wait_ge(*jobs.taken(("t", j)))
                        for h in range(NH):
                            for kt in range(TPB):
                                last = pe.matmul(bank[:, h * HD:(h + 1) * HD], probT[:, b % 2, i, h, kt, :],
                                                 V[:, TPB * b + kt, h * HD:(h + 1) * HD], start=(kt == 0), stop=(kt == 1))
                    last.then_inc(s["product_ready"], 1)

            def turned(copy, took, eng, j):
                b = units[j][0]
                eng.wait_ge(*jobs.ready(("t", j)))
                if b >= 2:
                    eng.wait_ge(*jobs.ready(("o", b - 2, TPB - 1)))
                src = jobs.bank(("t", j))
                for x, (i, h) in enumerate(members(units[j])):
                    last = copy(probT[:, b % 2, i, h, :, :].rearrange("p k q -> p (k q)"), src[:, 2 * x * P:2 * (x + 1) * P])
                last.then_inc(took, 1)

            @block.scalar
            def _(act):
                for key, who in order:
                    if who != "s":
                        continue
                    kind, j = key
                    if kind == "t":
                        turned(nc.scalar.copy, s["scalar_took"], act, j)
                        continue
                    act.wait_ge(s["max_ready"], j + 1)
                    if j >= RINGP:
                        act.wait_ge(*jobs.ready(("t", j - RINGP)))
                    b = units[j][0]
                    for x, (i, h) in enumerate(members(units[j])):
                        last = nc.scalar.activation(prob[:, j % RINGP, x, :], jobs.bank(key)[:, x * N:(x + 1) * N], ACT.Exp,
                                                    bias=negmax[:, j, x:x + 1], scale=SCALE,
                                                    accum_out=sums[:, TPB * b + i, h:h + 1])
                    last.then_inc(s["scalar_took"], 1)

            @block.vector
            def _(dve):
                step = Steps(dve, s["vector_step"])
                for key, who in order:
                    if key[0] == "s":
                        j = key[1]
                        dve.wait_ge(*jobs.ready(key))
                        step.then(nc.vector.tensor_reduce(negmax[:, j, :], jobs.bank(key).rearrange("p (x k) -> p x k", x=2),
                                                          AX.X, ALU.max, negate=True))
                        nc.vector.tensor_scalar(negmax[:, j, :], negmax[:, j, :], SCALE, None,
                                                ALU.mult).then_inc(s["max_ready"], 1)
                    elif who == "v" and key[0] == "t":
                        turned(nc.vector.tensor_copy, s["vector_took"], dve, key[1])
                    elif who == "v":
                        _, b, i = key
                        t = TPB * b + i
                        dve.wait_ge(*jobs.ready(key))
                        dve.wait_ge(*jobs.taken(("s", 12 * b + 11)))
                        step.then(nc.vector.reciprocal(inv[:, t, :], sums[:, t, :]))
                        nc.vector.tensor_tensor(AO[:, t, :].rearrange("p (h d) -> p h d", h=NH),
                                                jobs.bank(key)[:, 0:D].rearrange("p (h d) -> p h d", h=NH),
                                                inv[:, t, :].unsqueeze(2).to_broadcast([P, NH, HD]),
                                                ALU.mult).then_inc(s["vector_took"], 1)


def attention_out(c, AO):
    nc = c.nc
    with ExitStack() as mem:
        AOT = mem.enter_context(nc.sbuf_tensor("att_rowsT", [HF, 2, T], F32))
        order = [(("turn", g, k), "sv"[k]) for g in range(2) for k in range(2)] + [(("out", t), "v") for t in range(0, NT, 2)]
        with stage(nc, JOB_SEMS) as (block, s):
            jobs = Jobs(c, s, order)

            @block.tensor
            def _(pe):
                pe.wait_ge(c.weights_in["att_out"], 16)
                for key, _ in order:
                    bank = jobs.bank(key)
                    jobs.bank_free(pe, key)
                    if key[0] == "turn":
                        _, g, k = key
                        for i in range(4):
                            last = pe.transpose(bank[0:HF, i * P:(i + 1) * P], AO[:, 4 * g + i, k * HF:(k + 1) * HF],
                                                c.ident[:, :])
                    else:
                        for k in range(2):
                            pe.wait_ge(*jobs.taken(("turn", key[1] // 4, k)))
                        for i in range(2):
                            t = key[1] + i
                            for k in range(2):
                                last = pe.matmul(bank[:, i * D:(i + 1) * D], AOT[:, k, t * P:(t + 1) * P], c.tile["att_out"][:, k, :],
                                                 start=(k == 0), stop=(k == 1))
                    last.then_inc(s["product_ready"], 1)

            @block.scalar
            def _(act):
                for _, g, k in jobs.by("s"):
                    act.wait_ge(*jobs.ready(("turn", g, 0)))
                    nc.scalar.copy(AOT[:, 0, g * BANK:(g + 1) * BANK], jobs.bank(("turn", g, 0))[0:HF, :]
                                   ).then_inc(s["scalar_took"], 1)

            @block.vector
            def _(dve):
                for g in range(2):
                    dve.wait_ge(*jobs.ready(("turn", g, 1)))
                    nc.vector.tensor_copy(AOT[:, 1, g * BANK:(g + 1) * BANK], jobs.bank(("turn", g, 1))[0:HF, :]
                                          ).then_inc(s["vector_took"], 1)
                add_rows(c, dve, Steps(dve, s["vector_step"]), jobs, s, "out", c.row("att_b_out"))


def keep_rows(c):
    with stage(c.nc, "") as (block, s):
        @block.vector
        def _(dve):
            c.nc.vector.tensor_tensor(c.H[:, :, :], c.H[:, :, :], c.XN[:, :, :], ALU.add)


def first_layers(c):
    norm_and_turn(c, c.H, c.XN, c.XT, D, c.eps5)
    gated_convolutions(c)
    norm_and_turn(c, c.H, c.XN, c.XT, D, c.eps5)
    entangled_ffn(c)
    norm_and_turn(c, c.H, c.XN, c.XT, D, c.eps5)
    nystrom_attention(c)


def later_layers(c):
    c.ring = ExpertRing(c, c.ctx)
    c.allocate_weights(LATE, c.ctx)

    def load_late(sp):
        c.load_weights(sp, LATE)
        c.ring.prefetch(sp, c.w["moe1_w1"], c.w["moe1_w2"], c.w["moe1_b1"])

    norm_and_turn(c, c.H, c.XN, c.XT, D, c.eps5, sync=load_late)
    top2_ffn(c, "moe1", c.tile["moe1_gate"], ACT.Gelu, 1e-9, c.w["moe1_b1"], c.tile["moe1_b2"])
    norm_and_turn(c, c.H, c.XN, c.XT, D, c.eps5, sync=lambda sp: c.ring.prefetch(sp, c.w["switch_w1"], c.w["switch_w2"]))
    test_time_training(c)
    norm_and_turn(c, c.H, c.XN, c.XT, D, c.eps5)
    switch_ffn(c)
    norm_and_turn(c, c.H, c.XN, c.XT, D, c.eps5, sync=lambda sp: c.ring.prefetch(sp, c.w["moe3_w1"], c.w["moe3_w2"]))
    softmax_attention(c)
    norm_and_turn(c, c.H, c.XN, c.XT, D, c.eps5)
    keep_rows(c)
    norm_and_turn(c, c.XN, c.XN, c.XT, D, c.eps5, c.col("moe3_gamma"), c.col("moe3_beta"))
    top2_ffn(c, "moe3", c.tile["moe3_router"], ACT.Silu, 0.0)


ROWS = [("conv_b", DT), ("tok_out_b0", DT), ("tok_out_b1", DT), ("tok_ff2_b0", DT), ("tok_ff2_b1", DT),
        ("head_b", D), ("mix_b", D), ("ffn_b_proj", D), ("nys_b_proj", D), ("att_b_v", D), ("att_b_out", D),
        ("switch_ln_w", D), ("alpha", 6), ("mem_Wg_b", 4)]
COLS = [("tok_ln1_g0", 1), ("tok_ln1_b0", 1), ("tok_ln1_g1", 1), ("tok_ln1_b1", 1),
        ("tok_ln2_g0", 1), ("tok_ln2_b0", 1), ("tok_ln2_g1", 1), ("tok_ln2_b1", 1), ("lnf_g", 1), ("lnf_b", 1),
        ("tok_ff1_b0", 4), ("tok_ff1_b1", 4), ("router_b", 2), ("mixg_b", 2), ("ffn_b_fc", 6),
        ("conv_taps", 6 * 3 * 4), ("conv_bias", 6 * 3), ("att_b_qk", 2 * HG),
        ("moe3_gamma", 2), ("moe3_beta", 2)]


def spans(table):
    at, out = 0, {}
    for name, width in table:
        out[name] = (at, width)
        at += width
    return out, at


ROW_AT, ROW_LEN = spans(ROWS)
COL_AT, COL_LEN = spans(COLS)

TOK = ("tok_qkv", "tok_out", "tok_ff1", "tok_ff2", "head_w")
EARLY = ("gate_wT", "router_wT", "mixg_wT", "mix_wT", "mem_qk", "ffn_fcT", "ffn_proj", "nys_qk", "nys_v", "nys_proj")
LATE = ("ttt_w0", "ttt_w2", "ttt_w1", "ttt_w1T", "att_qk", "att_v", "att_out", "moe1_b2", "moe1_gate", "switch_router",
        "moe3_router")


def tokenizer(c, scope):
    c.X = c.sb("tok_residual", [P, NT, DT], scope)
    c.YT = c.sb("tok_rowsT", [P, 1, T], scope)
    tokenizer_patches(c, c.w)
    for layer in range(2):
        norm_and_turn(c, c.X, c.XN, c.YT, DT, c.eps5, c.col(f"tok_ln1_g{layer}"), c.col(f"tok_ln1_b{layer}"))
        tokenizer_attention(c, layer)
        norm_and_turn(c, c.X, c.XN, c.YT, DT, c.eps5, c.col(f"tok_ln2_g{layer}"), c.col(f"tok_ln2_b{layer}"))
        tokenizer_ffn(c, layer)
    norm_and_turn(c, c.X, c.XN, c.YT, DT, c.eps5, c.col("lnf_g"), c.col("lnf_b"))
    tokenizer_head(c)


def tower(nc, w, out):
    with ExitStack() as ctx:
        c = Core(nc, ctx)
        c.w, c.stack = w, ctx
        out_done = ctx.enter_context(nc.semaphore("out_done"))
        c.allocate()
        prepare(c)
        with ExitStack() as early:
            c.allocate_weights(EARLY, early)
            with ExitStack() as tok:
                c.allocate_weights(TOK, tok)
                tokenizer(c, tok)
            first_layers(c)
        later_layers(c)
        with stage(nc, "") as (block, s):
            @block.sync
            def _(sp):
                sp.dma_start(out.rearrange("b (t p) d -> p (b t) d", p=P), c.H[:, :, :]).then_inc(out_done, 16)
                sp.wait_ge(out_done, 16)



def _layouts(a):
    f = np.ascontiguousarray
    o = {}
    o["patches"] = f(a["x"].reshape(B, 32, 16, 2, 4, 16, 8).transpose(1, 4, 3, 6, 0, 2, 5).reshape(P, 16, T))
    o["conv_w"] = f(a["L0_tok_conv_w"].reshape(P, 32, 2, 4, 8).transpose(1, 3, 2, 4, 0).reshape(P, 16, P))
    o["tok_qkv"] = f(a["L0_tok_qkv_w"].transpose(1, 0, 2))
    o["tok_out"] = f(a["L0_tok_out_w"].reshape(2, 4, P, DT).transpose(2, 0, 1, 3))
    o["tok_ff1"] = f(a["L0_tok_ff1_w"].transpose(1, 0, 2))
    o["tok_ff2"] = f(a["L0_tok_ff2_w"].reshape(2, 4, P, DT).transpose(2, 0, 1, 3))
    o["head_w"] = a["L0_tok_head_w"]

    def split(m):
        return f(m.reshape(2, HF, -1).transpose(1, 0, 2))

    def tiles(m, p=P):
        return f(m.reshape(-1, p, m.shape[-1]).transpose(1, 0, 2))

    def pad_heads(m):
        z = np.zeros((m.shape[0], NH, SLOT), m.dtype)
        z[:, :, :HD] = m.reshape(m.shape[0], NH, HD)
        return z.reshape(m.shape[0], NH * SLOT)

    o["gate_wT"] = split(a["L0_attn_gate_w"].T)
    o["router_wT"] = split(np.repeat(a["L0_attn_router_w"], HD, axis=0).T)
    o["mixg_wT"] = split(a["L0_attn_mixg_w"].T)
    o["mix_wT"] = split(a["L0_attn_mix_w"].T)
    m = np.zeros((64, 64 + 64 + 4), np.float32)
    for h in range(4):
        r = slice(16 * h, 16 * h + 16)
        m[r, 16 * h:16 * h + 16] = a["L0_attn_mem_Wq"][h].T
        m[r, 64 + 16 * h:64 + 16 * h + 16] = a["L0_attn_mem_Wk"][h].T
        m[r, 128 + h] = a["L0_attn_mem_Wg_w"][h, 0]
    o["mem_qk"] = m
    o["mem_v"] = f(a["L0_attn_mem_Wv"].transpose(1, 0, 2).reshape(P, 64))
    o["mem_out"] = f(a["L0_attn_mem_Wout"].transpose(2, 0, 1).reshape(P, 64))
    o["ffn_fcT"] = split(a["L0_ffn_w_fc"].T)
    o["ffn_proj"] = tiles(f(a["L0_ffn_w_proj"].T))
    q, k, v = (a["L1_attn_w_qkv"][:, i * D:(i + 1) * D] for i in range(3))
    o["nys_qk"] = split(np.concatenate([pad_heads(q), pad_heads(k)], 1))
    o["nys_v"] = split(v)
    o["nys_proj"] = split(a["L1_attn_w_proj"])
    o["moe1_w1"] = f(a["L1_ffn_w1"].reshape(8, 2, HF, FF).transpose(0, 2, 1, 3))
    o["moe1_w2"] = f(a["L1_ffn_w2"].reshape(8, FT, P, D).transpose(0, 2, 1, 3))
    o["moe1_b1"] = f(a["L1_ffn_b1"].reshape(8, FT, P).transpose(0, 2, 1))
    o["moe1_b2"] = a["L1_ffn_b2"]
    o["moe1_gate"] = split(a["L1_ffn_gate_w"].T)
    o["ttt_w0"], o["ttt_w2"] = split(a["L2_attn_w0"]), split(a["L2_attn_w2"])
    o["ttt_w1"], o["ttt_w1T"] = tiles(a["L2_attn_w1"]), split(f(a["L2_attn_w1"].T))
    o["switch_router"] = split(a["L2_ffn_w_router"])
    o["switch_w1"] = f(a["L2_ffn_wi"].reshape(16, 2, HF, FF).transpose(0, 2, 1, 3))
    o["switch_w2"] = f(a["L2_ffn_wo"].reshape(16, FT, P, D).transpose(0, 2, 1, 3))
    wq, wk, wv = (a["L3_attn_w_qkv"][i * D:(i + 1) * D].T for i in range(3))
    o["att_qk"] = split(np.concatenate([pad_heads(wq), pad_heads(wk)], 1))
    o["att_v"], o["att_out"] = split(f(wv)), split(f(a["L3_attn_w_out"].T))
    o["moe3_router"] = split(a["L3_ffn_router_w"])
    o["moe3_w1"] = f(a["L3_ffn_w1"].reshape(8, 2, HF, FF).transpose(0, 2, 1, 3))
    o["moe3_w2"] = f(a["L3_ffn_w2"].reshape(8, FT, P, D).transpose(0, 2, 1, 3))

    bqkv = a["L3_attn_b_qkv"]
    rows = {"conv_b": a["L0_tok_conv_b"], "head_b": a["L0_tok_head_b"], "mix_b": a["L0_attn_mix_b"],
            "ffn_b_proj": a["L0_ffn_b_proj"], "nys_b_proj": a["L1_attn_b_proj"], "att_b_v": bqkv[2 * D:],
            "att_b_out": a["L3_attn_b_out"], "switch_ln_w": a["L2_ffn_ln_w"],
            "alpha": np.concatenate([a["L0_ffn_alpha_e"], a["L0_ffn_alpha_r"]]), "mem_Wg_b": a["L0_attn_mem_Wg_b"][:, 0]}
    for i in range(2):
        rows[f"tok_out_b{i}"], rows[f"tok_ff2_b{i}"] = a["L0_tok_out_b"][i], a["L0_tok_ff2_b"][i]
    o["rows"] = np.concatenate([rows[n] for n, _ in ROWS])[None]
    cols = np.zeros((P, COL_LEN), np.float32)

    def col(name, m):
        at, n = COL_AT[name]
        m = m.reshape(n, -1)
        cols[:m.shape[1], at:at + n] = m.T

    for i in range(2):
        for n in ("ln1_g", "ln1_b", "ln2_g", "ln2_b"):
            col(f"tok_{n}{i}", a[f"L0_tok_{n}"][i])
        col(f"tok_ff1_b{i}", a["L0_tok_ff1_b"][i])
    col("lnf_g", a["L0_tok_lnf_g"])
    col("lnf_b", a["L0_tok_lnf_b"])
    col("router_b", np.repeat(a["L0_attn_router_b"], HD))
    col("mixg_b", a["L0_attn_mixg_b"])
    col("ffn_b_fc", a["L0_ffn_b_fc"])
    cw = a["L0_attn_conv_w"].reshape(6, 2, 3, HD, 4)
    taps = np.broadcast_to(cw[:, :, None], (6, 2, B, 3, HD, 4)).transpose(1, 2, 4, 0, 3, 5).reshape(P, 72)
    cb = a["L0_attn_conv_b"].reshape(6, 2, 3, HD)
    bias = np.broadcast_to(cb[:, :, None], (6, 2, B, 3, HD)).transpose(1, 2, 4, 0, 3).reshape(P, 18)
    cols[:, COL_AT["conv_taps"][0]:][:, :72] = taps
    cols[:, COL_AT["conv_bias"][0]:][:, :18] = bias
    bq, bk = pad_heads(bqkv[None, :D])[0], pad_heads(bqkv[None, D:2 * D])[0]
    col("att_b_qk", np.concatenate([bq, bk]))
    col("moe3_gamma", a["L3_ffn_ln_gamma"])
    col("moe3_beta", a["L3_ffn_ln_beta"])
    o["cols"] = cols
    return {k: f(v) for k, v in o.items()}


def kernel(**inputs):
    import concourse.bacc as _bacc
    from concourse.bass_utils import run_bass_kernel_spmd as _run

    nc = _bacc.Bacc("TRN2", target_bir_lowering=False, num_devices=1)
    arrays = _layouts({k: np.asarray(v) for k, v in inputs.items()})
    w = {}
    for name, a in arrays.items():
        w[name] = nc.dram_tensor(name + "_dram", a.shape, mybir.dt.from_np(a.dtype), kind="ExternalInput").ap()
    out = nc.dram_tensor("out_0_dram", (B, N, D), F32, kind="ExternalOutput").ap()
    tower(nc, w, out)
    r = _run(nc, [{name + "_dram": a for name, a in arrays.items()}], core_ids=[0])
    return r.results[0]["out_0_dram"]
```

```python
from contextlib import ExitStack, contextmanager

import numpy as np

import concourse.bass as bass
from concourse import mybir
from concourse.alu_op_type import AluOpType as ALU

F32 = mybir.dt.float32
U32, I32 = mybir.dt.uint32, mybir.dt.int32
ACT = mybir.ActivationFunctionType
AX = mybir.AxisListType

P = 128
B, N = 4, 256
T = B * N
NT = T // P
TPB = N // P
D = 192
HF = D // 2
DT = 128
HD = 16
NH = 12
SLOT = 32
HG = 3
LM = 64
FF = 768
FT = FF // P
BLOCKS = (2 * T + 8 * (P - 1)) // P
assert BLOCKS >= (T + 16 * (P - 1)) // P
BANK = 512
NB = 8


class Steps:

    def __init__(self, eng, sem):
        self.eng, self.sem, self.n = eng, sem, 0

    def mark(self, ins):
        ins.then_inc(self.sem, 1)
        self.n += 1
        return self.n

    def then(self, ins):
        self.eng.wait_ge(self.sem, self.mark(ins))


class Jobs:

    def __init__(self, core, sems, order, banks=None):
        self.core, self.sems, self.order = core, sems, order
        self.banks = banks or list(range(NB))
        self.index = {key: k for k, (key, _) in enumerate(order)}
        assert len(self.index) == len(order)

    def bank(self, key):
        return self.core.bank[self.banks[self.index[key] % len(self.banks)]]

    def taken(self, key):
        k = self.index[key]
        who = self.order[k][1]
        count = sum(1 for _, w in self.order[:k + 1] if w == who)
        return (self.sems["vector_took"] if who == "v" else self.sems["scalar_took"]), count

    def bank_free(self, pe, key):
        k = self.index[key] - len(self.banks)
        if k >= 0:
            pe.wait_ge(*self.taken(self.order[k][0]))

    def ready(self, key):
        return self.sems["product_ready"], self.index[key] + 1

    def by(self, who):
        return [key for key, w in self.order if w == who]


@contextmanager
def stage(nc, names):
    with ExitStack() as ctx:
        made = {n: ctx.enter_context(nc.semaphore(n + f"_{nc.get_next_instruction_name()}")) for n in names.split()}
        with nc.Block(no_gpsimd_drain=True) as block:
            yield block, made
        nc.gpsimd.drain()
        for n in names.split():
            nc.gpsimd.sem_clear(made[n])
        nc.all_engine_barrier()


JOB_SEMS = "product_ready vector_took scalar_took vector_step scalar_step "
PATCH_SEMS = " ".join(f"patch{k}" for k in range(16))


class Core:

    def __init__(self, nc, ctx):
        self.nc, self.ctx = nc, ctx
        self.psum = ctx.enter_context(nc.psum_tensor("psum", [P, NB, BANK], F32))
        self.bank = [self.psum[:, i, :] for i in range(NB)]

        self.counter = 0

    def uid(self):
        self.counter += 1
        return self.counter

    def sb(self, name, shape, scope=None):
        return (scope or self.ctx).enter_context(self.nc.sbuf_tensor(name, shape, F32))

    def allocate(self):
        self.H = self.sb("residual", [P, NT, D])
        self.XN = self.sb("normed", [P, NT, D])
        self.XT = self.sb("normedT", [HF, 2, T])
        self.ident = self.sb("ident", [P, P])
        self.eps = self.sb("eps", [P, 2])
        self.eps5, self.eps6 = self.eps[:, 0:1], self.eps[:, 1:2]
        self.rows = self.sb("rows", [P, ROW_LEN])
        self.cols = self.sb("cols", [P, COL_LEN])
        self.ffn_b0 = self.sb("ffn_b0", [P, FT])
        self.ffn_b1 = self.sb("ffn_b1", [P, D])
        self.pick_top = self.sb("pick_top", [P, NT])
        self.rank = self.sb("rank", [P, 16])
        self.zero_row, self.full, self.tri = self.sb("zero_row", [P, D]), self.sb("full", [P, P]), self.sb("tri", [P, P])
        self.before = self.sb("before", [P, 16, 16])
        self.multiples = self.sb("multiples", [P, BLOCKS])
        self.rows_zeroed = self.ctx.enter_context(self.nc.semaphore("rows_zeroed"))
        names = ["scattered"] + [f"stored{n}" for n in range(4)] + [f"back{n}" for n in range(4)]
        self.soft = {n: self.ctx.enter_context(self.nc.semaphore(n)) for n in names}
        self.soft_at = {n: 0 for n in names}
        self.block_rows = self.nc.dram_tensor("block_rows", (BLOCKS * P, D), F32, kind="Internal").ap()
        self.block_outs = self.nc.dram_tensor("block_outs", (BLOCKS * P, D), F32, kind="Internal").ap()
        self.rows_in = self.ctx.enter_context(self.nc.semaphore("rows_in"))
        self.cols_in = self.ctx.enter_context(self.nc.semaphore("cols_in"))
        self.weights_in, self.tile = {}, {}

    def allocate_weights(self, names, scope):
        for name in names:
            self.tile[name] = self.sb(name, list(self.w[name].shape), scope)
            self.weights_in[name] = self.ctx.enter_context(self.nc.semaphore(name + "_in"))

    def load_weights(self, sp, names):
        for name in names:
            tile, src = self.tile[name], self.w[name]
            sp.dma_start(tile[tuple(slice(None) for _ in src.shape)], src).then_inc(self.weights_in[name], 16)

    def row(self, name):
        at, n = ROW_AT[name]
        return self.rows[:, at:at + n]

    def col(self, name):
        at, n = COL_AT[name]
        return self.cols[:, at:at + n]


def halves(width):
    return [(0, DT)] if width == DT else [(0, HF), (HF, HF)]


def norm_and_turn(c, X, XN, XT, width, eps, gain=None, shift=None, sync=None):
    nc = c.nc
    parts = halves(width)
    HT = NT // 2
    with ExitStack() as mem:
        stats = mem.enter_context(nc.sbuf_tensor(f"stats{c.uid()}", [P, NT, 6], F32))
        mv = mem.enter_context(nc.sbuf_tensor(f"mv{c.uid()}", [P, NT, 2], F32))
        rstd = mem.enter_context(nc.sbuf_tensor(f"rstd{c.uid()}", [P, 2, NT], F32))
        with stage(nc, JOB_SEMS + "stats_done moments_done std_ready row_normed") as (block, s):
            order = [((g, p), "sv"[p]) for g in range(2) for p in range(len(parts))]
            jobs = Jobs(c, s, order)
            if sync:
                block.sync(sync)

            @block.vector
            def _(dve):
                step = Steps(dve, s["vector_step"])
                for t in range(NT):
                    nc.vector.bn_stats(stats[:, t, :], X[:, t, 0:width]).then_inc(s["stats_done"], 1)
                for t in range(NT):
                    dve.wait_ge(s["stats_done"], t + 1)
                    nc.vector.bn_aggr(mv[:, t, :], stats[:, t, :]).then_inc(s["moments_done"], 1)
                dve.wait_ge(s["std_ready"], 1)
                step.then(nc.vector.reciprocal(rstd[:, 1, :], rstd[:, 0, :]))
                for t in range(NT):
                    nc.vector.tensor_scalar(XN[:, t, 0:width], X[:, t, 0:width], mv[:, t, 0:1], rstd[:, 1, t:t + 1],
                                            ALU.subtract, ALU.mult).then_inc(s["row_normed"], 1)
                for g, p in jobs.by("v"):
                    n = parts[p][1]
                    dve.wait_ge(*jobs.ready((g, p)))
                    dst, src = XT[0:n, p, g * BANK:(g + 1) * BANK], jobs.bank((g, p))[0:n, :]
                    if gain is None:
                        nc.vector.tensor_copy(dst, src).then_inc(s["vector_took"], 1)
                    else:
                        nc.vector.tensor_scalar(dst, src, gain[0:n, p:p + 1], shift[0:n, p:p + 1],
                                                ALU.mult, ALU.add).then_inc(s["vector_took"], 1)

            @block.scalar
            def _(act):
                act.wait_ge(s["moments_done"], NT)
                nc.scalar.activation(rstd[:, 0, :], mv[:, :, 1], ACT.Sqrt, bias=eps).then_inc(s["std_ready"], 1)
                for g, p in jobs.by("s"):
                    n = parts[p][1]
                    act.wait_ge(*jobs.ready((g, p)))
                    dst, src = XT[0:n, p, g * BANK:(g + 1) * BANK], jobs.bank((g, p))[0:n, :]
                    if gain is None:
                        nc.scalar.copy(dst, src).then_inc(s["scalar_took"], 1)
                    else:
                        nc.scalar.activation(dst, src, ACT.Identity, bias=shift[0:n, p:p + 1],
                                             scale=gain[0:n, p:p + 1]).then_inc(s["scalar_took"], 1)

            @block.tensor
            def _(pe):
                for g, p in [key for key, _ in order]:
                    lo, n = parts[p]
                    pe.wait_ge(s["row_normed"], HT * (g + 1))
                    for i in range(HT):
                        last = pe.transpose(jobs.bank((g, p))[0:n, i * P:(i + 1) * P],
                                            XN[:, HT * g + i, lo:lo + n], c.ident[:, :])
                    last.then_inc(s["product_ready"], 1)


def tokenizer_patches(c, w):
    nc = c.nc
    STEPS = 16
    with ExitStack() as mem:
        patches = mem.enter_context(nc.sbuf_tensor("patches", [P, STEPS, T], F32))
        convw = mem.enter_context(nc.sbuf_tensor("convw", [P, STEPS, DT], F32))
        xT = mem.enter_context(nc.sbuf_tensor("patchT", [P, T], F32))
        with stage(nc, JOB_SEMS + "convw_in " + PATCH_SEMS) as (block, s):
            arrived = [s["patch0"], s["patch1"], s["patch2"], s["patch3"], s["patch4"], s["patch5"], s["patch6"], s["patch7"], s["patch8"], s["patch9"],
                       s["patch10"], s["patch11"], s["patch12"], s["patch13"], s["patch14"], s["patch15"]]
            order = [(("conv", g), "vs"[g]) for g in range(2)] + [(("turn", g), "v") for g in range(2)]
            jobs = Jobs(c, s, order)

            @block.sync
            def _(sp):
                sp.dma_start(convw[:, :, :], w["conv_w"]).then_inc(s["convw_in"], 16)
                for k in range(0, STEPS, 2):
                    sp.dma_start(patches[:, k, :], w["patches"][:, k, :]).then_inc(arrived[k], 16)
                c.load_weights(sp, TOK + EARLY)

            @block.scalar
            def _(act):
                for k in range(1, STEPS, 2):
                    act.dma_start(patches[:, k, :], w["patches"][:, k, :]).then_inc(arrived[k], 16)
                act.wait_ge(*jobs.ready(("conv", 1)))
                nc.scalar.copy(xT[:, BANK:], jobs.bank(("conv", 1))).then_inc(s["scalar_took"], 1)

            @block.tensor
            def _(pe):
                pe.wait_ge(s["convw_in"], 16)
                for k in range(STEPS):
                    pe.wait_ge(arrived[k], 16)
                    for g in range(2):
                        last = pe.matmul(jobs.bank(("conv", g)), convw[:, k, :],
                                         patches[:, k, g * BANK:(g + 1) * BANK],
                                         start=(k == 0), stop=(k == STEPS - 1))
                        if k == STEPS - 1:
                            last.then_inc(s["product_ready"], 1)
                for g in range(2):
                    pe.wait_ge(*jobs.taken(("conv", g)))
                    for i in range(4):
                        last = pe.transpose(jobs.bank(("turn", g))[:, i * P:(i + 1) * P],
                                            xT[:, g * BANK + i * P:g * BANK + (i + 1) * P], c.ident[:, :])
                    last.then_inc(s["product_ready"], 1)

            @block.vector
            def _(dve):
                dve.wait_ge(*jobs.ready(("conv", 0)))
                nc.vector.tensor_copy(xT[:, 0:BANK], jobs.bank(("conv", 0))).then_inc(s["vector_took"], 1)
                dve.wait_ge(c.rows_in, 16)
                for g in range(2):
                    dve.wait_ge(*jobs.ready(("turn", g)))
                    nc.vector.tensor_tensor(
                        c.X[:, 4 * g:4 * g + 4, 0:DT], jobs.bank(("turn", g)).rearrange("p (t d) -> p t d", d=DT),
                        c.row("conv_b").unsqueeze(1).to_broadcast([P, 4, DT]), ALU.add).then_inc(s["vector_took"], 1)


def tokenizer_attention(c, layer):
    nc = c.nc
    DH, M4 = 64, 4
    INNER = 512
    qkv, out_w = c.tile["tok_qkv"][:, layer, :], c.tile["tok_out"][:, layer]
    with ExitStack() as mem:
        def sb(name, shape):
            return mem.enter_context(nc.sbuf_tensor(name + str(layer), shape, F32))
        qshift, qexp = sb("qshift", [P, 2, INNER]), sb("qexp", [P, 2, INNER])
        qmax, qsum, qinv = sb("qmax", [P, NT, 8]), sb("qsum", [P, NT, 8]), sb("qinv", [P, NT, 8])
        kmax, ksum, kinv = sb("kmax", [P, M4, B]), sb("ksum", [P, M4, B]), sb("kinv", [P, M4, B])
        kexp = sb("kexp", [P, M4, T])
        ktok = sb("ktok", [P, NT, INNER])
        vtok = sb("vtok", [P, NT, INNER])
        qT = sb("qT", [P, M4, T])
        ctx = sb("ctxbd", [P, B, M4, P])
        qprob = sb("qprob", [P, NT, INNER])
        attT = kexp
        ks = [("k", m, g) for m in range(M4) for g in range(2)]
        order = [(k, "s") for k in ks]
        for t in range(NT):
            order += [(("q", t), "v"), (("v", t), "s")]
        order += [(("kt", t), "s") for t in range(NT)]
        order += [(("qt", t), "v") for t in range(NT)]
        order += [(("ctx", b), "v") for b in range(B)]
        order += [(("att", b, h), "sv"[h]) for b in range(B) for h in range(2)]
        order += [(("out", g), "v") for g in range(2)]
        if layer == 1:
            c.choice = sb("choice", [P, 9])
            c.coef_in, c.coef_hid = sb("coef_in", [HF, 2, FF]), sb("coef_hid", [P, FT, D])
        with stage(nc, JOB_SEMS + "kmax_ready ctx_zero q_exped q_normed pool_step") as (block, s):
            jobs = Jobs(c, s, order)

            @block.gpsimd
            def _(pool):
                nc.gpsimd.memset(ctx[:, :, :, :], 0.0).then_inc(s["ctx_zero"], 1)
                if layer == 1:
                    mask_entangled_ffn(c, pool, Steps(pool, s["pool_step"]))

            @block.tensor
            def _(pe):
                if layer == 0:
                    for name in TOK:
                        pe.wait_ge(c.weights_in[name], 16)
                for key, _ in order:
                    kind, bank = key[0], jobs.bank(key)
                    jobs.bank_free(pe, key)
                    if kind == "k":
                        _, m, g = key
                        last = pe.matmul(bank, qkv[:, INNER + m * P:INNER + (m + 1) * P],
                                         c.YT[:, 0, g * BANK:(g + 1) * BANK], start=True, stop=True)
                    elif kind in "qv":
                        t = key[1]
                        lo = 0 if kind == "q" else 2 * INNER
                        last = pe.matmul(bank, c.YT[:, 0, t * P:(t + 1) * P], qkv[:, lo:lo + INNER],
                                         start=True, stop=True)
                    elif kind == "kt":
                        t = key[1]
                        pe.wait_ge(s["scalar_took"], 8)
                        for m in range(M4):
                            last = pe.transpose(bank[:, m * P:(m + 1) * P], kexp[:, m, t * P:(t + 1) * P],
                                                c.ident[:, :])
                    elif kind == "qt":
                        t = key[1]
                        pe.wait_ge(s["q_normed"], t + 1)
                        for m in range(M4):
                            last = pe.transpose(bank[:, m * P:(m + 1) * P], qprob[:, t, m * P:(m + 1) * P],
                                                c.ident[:, :])
                    elif kind == "ctx":
                        b = key[1]
                        pe.wait_ge(*jobs.taken(("kt", TPB * b + 1)))
                        for m in range(M4):
                            for i in range(TPB):
                                t = TPB * b + i
                                last = pe.matmul(bank[:, m * P:(m + 1) * P], ktok[:, t, m * P:(m + 1) * P],
                                                 vtok[:, t, m * P:(m + 1) * P], start=(i == 0), stop=(i == TPB - 1))
                    elif kind == "att":
                        _, b, h = key
                        pe.wait_ge(*jobs.taken(("ctx", b)))
                        for i in range(2):
                            m = 2 * h + i
                            last = pe.matmul(bank[:, i * N:(i + 1) * N], ctx[:, b, m, :],
                                             qT[:, m, b * N:(b + 1) * N], start=True, stop=True)
                    else:
                        g = key[1]
                        pe.wait_ge(*jobs.taken(("att", 2 * g + 1, 0)))
                        pe.wait_ge(*jobs.taken(("att", 2 * g + 1, 1)))
                        for i in range(4):
                            t = 4 * g + i
                            for m in range(M4):
                                last = pe.matmul(bank[:, i * P:(i + 1) * P], attT[:, m, t * P:(t + 1) * P],
                                                 out_w[:, m, :], start=(m == 0), stop=(m == M4 - 1))
                    last.then_inc(s["product_ready"], 1)

            @block.scalar
            def _(act):
                for n, key in enumerate(ks):
                    _, m, g = key
                    act.wait_ge(s["kmax_ready"], n + 1)
                    for i in range(2):
                        b = 2 * g + i
                        last = nc.scalar.activation(kexp[:, m, b * N:(b + 1) * N], jobs.bank(key)[:, i * N:(i + 1) * N],
                                                    ACT.Exp, bias=kmax[:, m, b:b + 1], accum_out=ksum[:, m, b:b + 1])
                    last.then_inc(s["scalar_took"], 1)
                for t in range(NT):
                    act.wait_ge(*jobs.taken(("q", t)))
                    if t >= 2:
                        act.wait_ge(s["q_normed"], t - 1)
                    nc.scalar.activation(qexp[:, t % 2, :], qshift[:, t % 2, :], ACT.Exp).then_inc(s["q_exped"], 1)
                    act.wait_ge(*jobs.ready(("v", t)))
                    nc.scalar.copy(vtok[:, t, :], jobs.bank(("v", t))).then_inc(s["scalar_took"], 1)
                for t in range(NT):
                    act.wait_ge(*jobs.ready(("kt", t)))
                    nc.scalar.copy(ktok[:, t, :], jobs.bank(("kt", t))).then_inc(s["scalar_took"], 1)
                for b in range(B):
                    act.wait_ge(*jobs.ready(("att", b, 0)))
                    nc.scalar.copy(attT[:, 0:2, b * N:(b + 1) * N],
                                   jobs.bank(("att", b, 0)).rearrange("p (m n) -> p m n", m=2)).then_inc(s["scalar_took"], 1)

            @block.vector
            def _(dve):
                step = Steps(dve, s["vector_step"])
                for key in ks:
                    _, m, g = key
                    dve.wait_ge(*jobs.ready(key))
                    nc.vector.tensor_reduce(kmax[:, m, 2 * g:2 * g + 2],
                                            jobs.bank(key).rearrange("p (b n) -> p b n", b=2), AX.X, ALU.max,
                                            negate=True).then_inc(s["kmax_ready"], 1)

                def normalise_q(t):
                    dve.wait_ge(s["q_exped"], t + 1)
                    e = qexp[:, t % 2, :].rearrange("p (h d) -> p h d", d=DH)
                    step.then(nc.vector.tensor_reduce(qsum[:, t, :], e, AX.X, ALU.add))
                    step.then(nc.vector.reciprocal(qinv[:, t, :], qsum[:, t, :]))
                    nc.vector.scalar_tensor_tensor(
                        qprob[:, t, :].rearrange("p (h d) -> p h d", d=DH), e, DH ** -0.5,
                        qinv[:, t, :].unsqueeze(2).to_broadcast([P, 8, DH]), ALU.mult, ALU.mult).then_inc(s["q_normed"], 1)

                for t in range(NT):
                    dve.wait_ge(*jobs.ready(("q", t)))
                    q = jobs.bank(("q", t)).rearrange("p (h d) -> p h d", d=DH)
                    step.then(nc.vector.tensor_reduce(qmax[:, t, :], q, AX.X, ALU.max))
                    if t >= 2:
                        dve.wait_ge(s["q_exped"], t - 1)
                    nc.vector.tensor_tensor(qshift[:, t % 2, :].rearrange("p (h d) -> p h d", d=DH), q,
                                            qmax[:, t, :].unsqueeze(2).to_broadcast([P, 8, DH]),
                                            ALU.subtract).then_inc(s["vector_took"], 1)
                    if t >= 1:
                        normalise_q(t - 1)
                normalise_q(NT - 1)
                for t in range(NT):
                    dve.wait_ge(*jobs.ready(("qt", t)))
                    nc.vector.tensor_copy(qT[:, :, t * P:(t + 1) * P],
                                          jobs.bank(("qt", t)).rearrange("p (m n) -> p m n", m=M4)).then_inc(s["vector_took"], 1)
                dve.wait_ge(s["scalar_took"], 8)
                dve.wait_ge(s["ctx_zero"], 1)
                step.then(nc.vector.reciprocal(kinv[:, :, :], ksum[:, :, :]))
                for b in range(B):
                    dve.wait_ge(*jobs.ready(("ctx", b)))
                    for h in range(2):
                        r = slice(h * DH, (h + 1) * DH)
                        last = nc.vector.tensor_tensor(
                            ctx[r, b, :, r], jobs.bank(("ctx", b)).rearrange("p (m d) -> p m d", m=M4)[r, :, r],
                            kinv[r, :, b:b + 1].to_broadcast([DH, M4, DH]), ALU.mult)
                        if h == 1:
                            last.then_inc(s["vector_took"], 1)
                for b in range(B):
                    dve.wait_ge(*jobs.ready(("att", b, 1)))
                    nc.vector.tensor_copy(attT[:, 2:4, b * N:(b + 1) * N],
                                          jobs.bank(("att", b, 1)).rearrange("p (m n) -> p m n", m=2)).then_inc(s["vector_took"], 1)
                add_product_and_bias(c, dve, step, jobs, s, c.row(f"tok_out_b{layer}"))


def add_product_and_bias(c, dve, step, jobs, s, bias):
    nc = c.nc
    for g in range(2):
        dve.wait_ge(*jobs.ready(("out", g)))
        xs = c.X[:, 4 * g:4 * g + 4, 0:DT]
        step.then(nc.vector.tensor_tensor(xs, xs, jobs.bank(("out", g)).rearrange("p (t d) -> p t d", d=DT), ALU.add))
        nc.vector.tensor_tensor(xs, xs, bias.unsqueeze(1).to_broadcast([P, 4, DT]), ALU.add).then_inc(s["vector_took"], 1)


def tokenizer_ffn(c, layer):
    nc = c.nc
    M4 = 4
    ff1, ff2 = c.tile["tok_ff1"][:, layer, :], c.tile["tok_ff2"][:, layer]
    with ExitStack() as mem:
        hid = mem.enter_context(nc.sbuf_tensor(f"tokhid{layer}", [P, M4, T], F32))
        order = [(("h", m, g), "s") for g in range(2) for m in range(M4)] + [(("out", g), "v") for g in range(2)]
        with stage(nc, JOB_SEMS) as (block, s):
            jobs = Jobs(c, s, order)

            @block.tensor
            def _(pe):
                for key, _ in order:
                    bank = jobs.bank(key)
                    jobs.bank_free(pe, key)
                    if key[0] == "h":
                        _, m, g = key
                        last = pe.matmul(bank, ff1[:, m * P:(m + 1) * P], c.YT[:, 0, g * BANK:(g + 1) * BANK],
                                         start=True, stop=True)
                    else:
                        g = key[1]
                        pe.wait_ge(*jobs.taken(("h", M4 - 1, g)))
                        for i in range(4):
                            t = 4 * g + i
                            for m in range(M4):
                                last = pe.matmul(bank[:, i * P:(i + 1) * P], hid[:, m, t * P:(t + 1) * P], ff2[:, m, :],
                                                 start=(m == 0), stop=(m == M4 - 1))
                    last.then_inc(s["product_ready"], 1)

            @block.scalar
            def _(act):
                for key in jobs.by("s"):
                    _, m, g = key
                    act.wait_ge(*jobs.ready(key))
                    b = c.col(f"tok_ff1_b{layer}")[:, m:m + 1]
                    nc.scalar.activation(hid[:, m, g * BANK:(g + 1) * BANK], jobs.bank(key), ACT.Gelu,
                                         bias=b).then_inc(s["scalar_took"], 1)

            @block.vector
            def _(dve):
                step = Steps(dve, s["vector_step"])
                add_product_and_bias(c, dve, step, jobs, s, c.row(f"tok_ff2_b{layer}"))


def tokenizer_head(c):
    nc = c.nc
    order = [(("head", t), "v") for t in range(0, NT, 2)]
    with stage(nc, JOB_SEMS) as (block, s):
        jobs = Jobs(c, s, order)

        @block.tensor
        def _(pe):
            for key, _ in order:
                for i in range(2):
                    t = key[1] + i
                    last = pe.matmul(jobs.bank(key)[:, i * D:(i + 1) * D], c.YT[:, 0, t * P:(t + 1) * P], c.tile["head_w"][:, :],
                                     start=True, stop=True)
                last.then_inc(s["product_ready"], 1)

        @block.vector
        def _(dve):
            for key in jobs.by("v"):
                t = key[1]
                dve.wait_ge(*jobs.ready(key))
                nc.vector.tensor_tensor(c.H[:, t:t + 2, :], jobs.bank(key)[:, 0:2 * D].rearrange("p (t d) -> p t d", t=2),
                                        c.row("head_b").unsqueeze(1).to_broadcast([P, 2, D]),
                                        ALU.add).then_inc(s["vector_took"], 1)


def prepare(c):
    nc = c.nc
    with stage(nc, "ident_zero ident_ready tri_full before_full") as (block, s):
        @block.sync
        def _(sp):
            sp.dma_start(c.cols[:, :], c.w["cols"]).then_inc(c.cols_in, 16)
            sp.dma_start(c.rows[:, :], c.w["rows"].broadcast_to([P, ROW_LEN])).then_inc(c.rows_in, 16)
            sp.wait_ge(c.cols_in, 16)
            sp.wait_ge(c.rows_in, 16)

        @block.vector
        def _(dve):
            nc.vector.memset(c.eps5, 1e-5)
            nc.vector.memset(c.eps6, 1e-6)

        @block.gpsimd
        def _(pool):
            nc.gpsimd.memset(c.zero_row[:, :], 0.0)
            nc.gpsimd.memset(c.full[:, :], 1.0)
            nc.gpsimd.memset(c.tri[:, :], 1.0).then_inc(s["tri_full"], 1)
            nc.gpsimd.memset(c.before[:, :, :], float(P)).then_inc(s["before_full"], 1)
            nc.gpsimd.iota(c.multiples[:, :], pattern=[[P, BLOCKS]], base=0, channel_multiplier=0,
                           allow_small_or_imprecise_dtypes=True)
            nc.gpsimd.iota(c.rank[:, :], pattern=[[-1, 16]], base=16, channel_multiplier=0,
                           allow_small_or_imprecise_dtypes=True)
            nc.gpsimd.memset(c.ident[:, :], 0.0).then_inc(s["ident_zero"], 1)
            pool.wait_ge(s["tri_full"], 1)
            nc.gpsimd.affine_select(out=c.tri[:, :], in_=c.tri[:, :], compare_op=ALU.is_ge, fill=0.0, base=0,
                                    pattern=[[1, P]], channel_multiplier=-1)
            pool.wait_ge(s["before_full"], 1)
            nc.gpsimd.affine_select(out=c.before[:, :, :], in_=c.before[:, :, :], compare_op=ALU.is_gt, fill=0.0, base=0,
                                    pattern=[[1, 16], [-1, 16]], channel_multiplier=0)
            pool.wait_ge(s["ident_zero"], 1)
            nc.gpsimd.affine_select(out=c.ident[:, :], in_=c.ident[:, :], compare_op=ALU.not_equal, fill=1.0, base=0,
                                    pattern=[[-1, P]], channel_multiplier=1).then_inc(s["ident_ready"], 1)


DILATIONS = [(1, 2, 4), (1, 1, 1), (4, 8, 16), (8, 16, 32), (32, 64, 128), (64, 128, 64), (64, 128, 256), (1, 100, 200),
             (1, 125, 250), (1, 256, 512), (3, 9, 27), (5, 25, 125)]
TAPS = 4
PAIRS = NH // 2
MD = 64
CHUNK = 64


def add_rows(c, dve, step, jobs, s, name, bias=None):
    nc = c.nc
    for t in range(0, NT, 2):
        dve.wait_ge(*jobs.ready((name, t)))
        h, p = c.H[:, t:t + 2, :], jobs.bank((name, t))[:, 0:2 * D].rearrange("p (t d) -> p t d", t=2)
        if bias is None:
            nc.vector.tensor_tensor(h, h, p, ALU.add).then_inc(s["vector_took"], 1)
        else:
            step.then(nc.vector.tensor_tensor(h, h, p, ALU.add))
            nc.vector.tensor_tensor(h, h, bias.unsqueeze(1).to_broadcast([P, 2, D]), ALU.add).then_inc(s["vector_took"], 1)


def gated_convolutions(c):
    nc = c.nc
    with ExitStack() as mem:
        def sb(name, shape):
            return mem.enter_context(nc.sbuf_tensor(name, shape, F32))
        gateT, valueT, headT = sb("gateT", [HF, 2, T]), sb("valueT", [HF, 2, T]), sb("headT", [HF, 2, T])
        memT = sb("memT", [MD, T])
        channels_out = nc.dram_tensor("gated_channels", (D, T), F32, kind="Internal").ap()
        channels_back = nc.dram_tensor("convolved_channels", (D, T), F32, kind="Internal").ap()
        convolve_and_remember(c, gateT, valueT, headT, memT, channels_out, channels_back)
        mix_channels(c, headT, memT, channels_back)


def convolve_and_remember(c, gateT, valueT, headT, memT, channels_out, channels_back):
    nc = c.nc
    KG = MD + 4
    MV = KG + MD
    with ExitStack() as mem:
        def sb(name, shape):
            return mem.enter_context(nc.sbuf_tensor(name, shape, F32))
        conv = [sb("conv_a", [P, PAIRS, N]), sb("conv_b_", [P, PAIRS, N])]
        tap_one = sb("tap_one", [P, PAIRS * 3])
        mem_v, mem_out = sb("mem_v", [P, MD]), sb("mem_out", [P, MD])
        mask = sb("head_mask", [MD, 4, HD])
        uv = sb("mem_uv", [MD, MD])
        qT = sb("mem_qT", [MD, T])
        kv = sb("mem_kv", [P, NT, MV])
        gate = sb("mem_gate", [P, NT, 4])
        gate16 = sb("mem_gate16", [P, NT, 4, HD])
        kg = sb("mem_kg", [P, NT, 4, HD])
        ones = sb("ones_col", [P, 1])
        writes = sb("mem_writes", [MD, B, 3, MD])
        gsum = sb("mem_gsum", [MD, B, 3])
        decay = sb("mem_decay", [MD, B, 3])
        state = sb("mem_state", [MD, 3, B, MD])
        order = []
        for m, g in ((1, 0), (1, 1), (0, 0), (0, 1)):
            order += [(("gate", m, g), "s"), (("value", m, g), "v")]
        order += [(("uv",), "v")]
        order += [(("mq", g), "s") for g in range(2)]
        order += [(("kv", t), "s") for t in range(NT)]
        order += [(("head", m, g), "s") for m in range(2) for g in range(2)]
        order += [((kind, odd), "s") for odd in range(2) for kind in ("write", "gsum")]
        order += [(("read", b2), "s") for b2 in range(2)]
        names = JOB_SEMS + ("mem_w_in mask_step gates_in pool_step gate_ready kg_ready states_ready stored loaded "
                            "convolved returned ones_ready logits_ready zeroed")
        with stage(nc, names) as (block, s):
            jobs = Jobs(c, s, order)

            @block.sync
            def _(sp):
                sp.dma_start(mem_v[:, :], c.w["mem_v"]).then_inc(s["mem_w_in"], 16)
                sp.dma_start(mem_out[:, :], c.w["mem_out"]).then_inc(s["mem_w_in"], 16)
                for m in (1, 0):
                    for g in range(2):
                        sp.wait_ge(*jobs.taken(("value", m, g)))
                    sp.dma_start(channels_out[m * HF:(m + 1) * HF, :], valueT[:, m, :]).then_inc(s["stored"], 16)
                sp.wait_ge(s["stored"], 32)
                for hh in range(2):
                    for b in range(B):
                        lo = hh * 64 + b * HD
                        src = channels_out.rearrange("(q h d) n -> h d q n", q=PAIRS, h=2)[hh][:, :, b * N:(b + 1) * N]
                        sp.dma_start(conv[0][lo:lo + HD, :, :], src).then_inc(s["loaded"], 16)
                sp.wait_ge(s["convolved"], 1)
                for hh in range(2):
                    for b in range(B):
                        lo = hh * 64 + b * HD
                        dst = channels_back.rearrange("(q h d) n -> h d q n", q=PAIRS, h=2)[hh][:, :, b * N:(b + 1) * N]
                        sp.dma_start(dst, conv[1][lo:lo + HD, :, :]).then_inc(s["returned"], 16)
                sp.wait_ge(s["returned"], 16 * 8)

            @block.tensor
            def _(pe):
                for name in EARLY:
                    pe.wait_ge(c.weights_in[name], 16)
                for key, _ in order:
                    kind, bank = key[0], jobs.bank(key)
                    jobs.bank_free(pe, key)
                    if kind in ("gate", "value", "head"):
                        _, m, g = key
                        w = c.tile["router_wT"] if kind == "head" else c.tile["gate_wT"]
                        lo = m * HF + (D if kind == "gate" else 0)
                        for k in range(2):
                            last = pe.matmul(bank[0:HF, :], w[:, k, lo:lo + HF], c.XT[:, k, g * BANK:(g + 1) * BANK],
                                             start=(k == 0), stop=(k == 1))
                    elif kind == "uv":
                        pe.wait_ge(s["mem_w_in"], 32)
                        last = pe.matmul(bank[0:MD, 0:MD], mem_v[:, :], mem_out[:, :], start=True, stop=True)
                    elif kind == "mq":
                        g = key[1]
                        pe.wait_ge(*jobs.taken(("value", 1, g)))
                        last = pe.matmul(bank[0:MD, :], c.tile["mem_qk"][:, 0:MD], valueT[0:MD, 1, g * BANK:(g + 1) * BANK],
                                         start=True, stop=True)
                    elif kind == "kv":
                        t = key[1]
                        pe.wait_ge(*jobs.taken(("uv",)))
                        x = valueT[0:MD, 1, t * P:(t + 1) * P]
                        pe.matmul(bank[:, 0:KG], x, c.tile["mem_qk"][:, MD:MD + KG], start=True, stop=True)
                        last = pe.matmul(bank[:, KG:MV], x, uv[:, :], start=True, stop=True)
                    elif kind in ("write", "gsum"):
                        pe.wait_ge(s["kg_ready"], 1)
                        pe.wait_ge(s["ones_ready"], 1)
                        odd = key[1]
                        chunks = [(b, i) for b in range(B) for i in ((1,) if odd else (0, 2))]
                        r = slice(64 * odd, 64 * odd + 64)
                        for n, (b, i) in enumerate(chunks):
                            t = TPB * b + i // 2
                            if kind == "write":
                                last = pe.matmul(bank[0:MD, n * MD:(n + 1) * MD], kg[r, t].rearrange("p m d -> p (m d)"),
                                                 kv[r, t, KG:MV], start=True, stop=True)
                            else:
                                last = pe.matmul(bank[0:MD, n:n + 1], gate16[r, t].rearrange("p m d -> p (m d)"),
                                                 ones[r, :], start=True, stop=True)
                    else:
                        pe.wait_ge(s["states_ready"], 1)
                        for n in range(6):
                            b, i = 2 * key[1] + n // 3, n % 3
                            at = b * N + (i + 1) * CHUNK
                            last = pe.matmul(bank[0:MD, n * CHUNK:(n + 1) * CHUNK], state[:, i, b, :],
                                             qT[:, at:at + CHUNK], start=True, stop=True)
                    last.then_inc(s["product_ready"], 1)

            @block.scalar
            def _(act):
                def sigmoid_gate(m, g):
                    act.wait_ge(*jobs.ready(("gate", m, g)))
                    nc.scalar.activation(gateT[:, m, g * BANK:(g + 1) * BANK], jobs.bank(("gate", m, g))[0:HF, :],
                                         ACT.Sigmoid).then_inc(s["scalar_took"], 1)
                for m, g in ((1, 0), (1, 1), (0, 0), (0, 1)):
                    sigmoid_gate(m, g)
                for g in range(2):
                    act.wait_ge(*jobs.ready(("mq", g)))
                    nc.scalar.copy(qT[:, g * BANK:(g + 1) * BANK], jobs.bank(("mq", g))[0:MD, :]).then_inc(s["scalar_took"], 1)
                for t in range(NT):
                    act.wait_ge(*jobs.ready(("kv", t)))
                    nc.scalar.copy(kv[:, t, :], jobs.bank(("kv", t))[:, 0:MV]).then_inc(s["scalar_took"], 1)
                for m in range(2):
                    for g in range(2):
                        act.wait_ge(*jobs.ready(("head", m, g)))
                        nc.scalar.activation(headT[:, m, g * BANK:(g + 1) * BANK], jobs.bank(("head", m, g))[0:HF, :],
                                             ACT.Sigmoid, bias=c.col("router_b")[0:HF, m:m + 1]).then_inc(s["scalar_took"], 1)
                act.wait_ge(s["logits_ready"], 1)
                nc.scalar.activation(gate[:, :, :], gate[:, :, :], ACT.Sigmoid).then_inc(s["gate_ready"], 1)
                for odd in range(2):
                    z = slice(1, 2) if odd else slice(0, 3, 2)
                    n = B * (1 if odd else 2)
                    act.wait_ge(*jobs.ready(("write", odd)))
                    nc.scalar.copy(writes[:, :, z, :], jobs.bank(("write", odd))[0:MD, 0:n * MD].rearrange(
                        "p (b i d) -> p b i d", b=B, d=MD)).then_inc(s["scalar_took"], 1)
                    act.wait_ge(*jobs.ready(("gsum", odd)))
                    nc.scalar.copy(gsum[:, :, z], jobs.bank(("gsum", odd))[0:MD, 0:n].rearrange(
                        "p (b i) -> p b i", b=B)).then_inc(s["scalar_took"], 1)
                for b2 in range(2):
                    act.wait_ge(*jobs.ready(("read", b2)))
                    nc.scalar.copy(memT.rearrange("p (b n) -> p b n", b=B)[:, 2 * b2:2 * b2 + 2, CHUNK:N],
                                   jobs.bank(("read", b2))[0:MD, 0:6 * CHUNK].rearrange("p (b n) -> p b n", b=2)
                                   ).then_inc(s["scalar_took"], 1)

            @block.gpsimd
            def _(pool):
                step = Steps(pool, s["pool_step"])
                nc.gpsimd.memset(memT.rearrange("p (b n) -> p b n", b=B)[:, :, 0:CHUNK], 0.0).then_inc(s["zeroed"], 1)
                nc.gpsimd.memset(ones[:, :], 1.0).then_inc(s["ones_ready"], 1)
                step.then(nc.gpsimd.memset(mask[:, :, :], 1.0))
                step.then(nc.gpsimd.affine_select(out=mask[:, :, :], in_=mask[:, :, :], compare_op=ALU.is_ge, fill=0.0,
                                                  base=0, pattern=[[-HD, 4], [0, HD]], channel_multiplier=1))
                nc.gpsimd.affine_select(out=mask[:, :, :], in_=mask[:, :, :], compare_op=ALU.is_ge, fill=0.0,
                                        base=HD - 1, pattern=[[HD, 4], [0, HD]],
                                        channel_multiplier=-1).then_inc(s["mask_step"], 1)
                pool.wait_ge(*jobs.taken(("kv", NT - 1)))
                nc.gpsimd.tensor_tensor(gate[:, :, :], kv[:, :, MD:KG],
                                        c.row("mem_Wg_b").unsqueeze(1).to_broadcast([P, NT, 4]),
                                        ALU.add).then_inc(s["logits_ready"], 1)
                pool.wait_ge(s["gate_ready"], 1)
                g16 = gate[:, :, :].unsqueeze(3).to_broadcast([P, NT, 4, HD])
                step.then(nc.gpsimd.tensor_copy(gate16[:, :, :, :], g16))
                for t in range(NT):
                    last = nc.gpsimd.tensor_tensor(kg[:, t, :, :], kv[:, t, 0:MD].rearrange("p (m d) -> p m d", d=HD),
                                                   gate16[:, t, :, :], ALU.mult)
                last.then_inc(s["kg_ready"], 1)
                pool.wait_ge(*jobs.taken(("gsum", 1)))
                pool.wait_ge(s["mask_step"], 1)
                step.then(nc.gpsimd.tensor_scalar(decay[:, :, :], gsum[:, :, :], -1.0 / CHUNK, 1.0, ALU.mult, ALU.add))
                m3 = mask.rearrange("p m d -> p (m d)").unsqueeze(1).to_broadcast([MD, B, MD])
                for i in range(3):
                    step.then(nc.gpsimd.tensor_tensor(writes[:, :, i, :], writes[:, :, i, :], m3, ALU.mult))
                step.then(nc.gpsimd.tensor_copy(state[:, 0, :, :], writes[:, :, 0, :]))
                for i in (1, 2):
                    d = decay[:, :, i:i + 1].to_broadcast([MD, B, MD])
                    step.then(nc.gpsimd.tensor_tensor(state[:, i, :, :], state[:, i - 1, :, :], d, ALU.mult))
                    ins = nc.gpsimd.tensor_tensor(state[:, i, :, :], state[:, i, :, :], writes[:, :, i, :], ALU.add)
                    if i == 1:
                        step.then(ins)
                    else:
                        ins.then_inc(s["states_ready"], 1)

            @block.vector
            def _(dve):
                step = Steps(dve, s["vector_step"])
                dve.wait_ge(c.cols_in, 16)
                taps = c.col("conv_taps").rearrange("p (q j k) -> p q j k", q=PAIRS, j=3)
                bias = c.col("conv_bias").rearrange("p (q j) -> p q j", q=PAIRS)
                step.then(nc.vector.tensor_scalar(tap_one.rearrange("p (q j) -> p q j", q=PAIRS), taps[:, :, :, TAPS - 1],
                                                  1.0, None, ALU.add))
                for m, g in ((1, 0), (1, 1), (0, 0), (0, 1)):
                    dve.wait_ge(*jobs.ready(("value", m, g)))
                    dve.wait_ge(*jobs.taken(("gate", m, g)))
                    nc.vector.tensor_tensor(valueT[:, m, g * BANK:(g + 1) * BANK], jobs.bank(("value", m, g))[0:HF, :],
                                            gateT[:, m, g * BANK:(g + 1) * BANK], ALU.mult).then_inc(s["vector_took"], 1)
                dve.wait_ge(*jobs.ready(("uv",)))
                dve.wait_ge(s["mask_step"], 1)
                nc.vector.tensor_tensor(uv[:, :], jobs.bank(("uv",))[0:MD, 0:MD], mask.rearrange("p m d -> p (m d)"),
                                        ALU.mult).then_inc(s["vector_took"], 1)
                dve.wait_ge(s["loaded"], 16 * 8)
                done = {}
                src, dst = conv
                for j in range(3):
                    chains = []
                    for q in range(PAIRS):
                        ops = [(slice(0, P), 0, None)]
                        for k in range(TAPS - 1):
                            for hh in range(2):
                                shift = (TAPS - 1 - k) * DILATIONS[2 * q + hh][j]
                                if shift < N:
                                    ops.append((slice(64 * hh, 64 * hh + 64), shift, k))
                        chains.append(ops)
                    for n in range(max(map(len, chains))):
                        for q in range(PAIRS):
                            if n >= len(chains[q]):
                                continue
                            r, shift, k = chains[q][n]
                            if q in done:
                                dve.wait_ge(s["vector_step"], done[q])
                            if k is None:
                                ins = nc.vector.tensor_scalar(dst[:, q, :], src[:, q, :], tap_one[:, 3 * q + j:3 * q + j + 1],
                                                              bias[:, q, j:j + 1], ALU.mult, ALU.add)
                            else:
                                ins = nc.vector.scalar_tensor_tensor(dst[r, q, shift:N], src[r, q, 0:N - shift],
                                                                     taps[r, q, j, k:k + 1], dst[r, q, shift:N],
                                                                     ALU.mult, ALU.add)
                            done[q] = step.mark(ins)
                    src, dst = dst, src
                dve.wait_ge(s["vector_step"], step.n)
                nc.vector.engine_nop().then_inc(s["convolved"], 1)


def mix_channels(c, headT, memT, channels_back):
    nc = c.nc
    with ExitStack() as mem:
        convT = mem.enter_context(nc.sbuf_tensor("convT", [HF, 2, T], F32))
        gateT = mem.enter_context(nc.sbuf_tensor("mixgT", [HF, 2, T], F32))
        order = [(("mg", m, g), "s") for g in range(2) for m in range(2)] + [(("mix", t), "v") for t in range(0, NT, 2)]
        with stage(nc, JOB_SEMS + "channels_in weighted gated") as (block, s):
            jobs = Jobs(c, s, order)

            @block.sync
            def _(sp):
                sp.dma_start(convT[:, :, :], channels_back.rearrange("(m p) n -> p m n", m=2)).then_inc(s["channels_in"], 16)

            @block.tensor
            def _(pe):
                for key, _ in order:
                    bank = jobs.bank(key)
                    jobs.bank_free(pe, key)
                    if key[0] == "mg":
                        _, m, g = key
                        pe.wait_ge(s["weighted"], g + 1)
                        for k in range(2):
                            last = pe.matmul(bank[0:HF, :], c.tile["mixg_wT"][:, k, m * HF:(m + 1) * HF],
                                             convT[:, k, g * BANK:(g + 1) * BANK], start=(k == 0), stop=(k == 1))
                    else:
                        pe.wait_ge(s["gated"], key[1] // 4 + 1)
                        for i in range(2):
                            t = key[1] + i
                            for k in range(2):
                                last = pe.matmul(bank[:, i * D:(i + 1) * D], gateT[:, k, t * P:(t + 1) * P],
                                                 c.tile["mix_wT"][:, k, :], start=(k == 0), stop=(k == 1))
                    last.then_inc(s["product_ready"], 1)

            @block.scalar
            def _(act):
                for key in jobs.by("s"):
                    _, m, g = key
                    act.wait_ge(*jobs.ready(key))
                    nc.scalar.activation(gateT[:, m, g * BANK:(g + 1) * BANK], jobs.bank(key)[0:HF, :], ACT.Sigmoid,
                                         bias=c.col("mixg_b")[0:HF, m:m + 1]).then_inc(s["scalar_took"], 1)

            @block.vector
            def _(dve):
                step = Steps(dve, s["vector_step"])
                dve.wait_ge(s["channels_in"], 16)
                step.then(nc.vector.tensor_tensor(convT[0:MD, 1, :], convT[0:MD, 1, :], memT[:, :], ALU.add))
                for g in range(2):
                    z = slice(g * BANK, (g + 1) * BANK)
                    nc.vector.tensor_tensor(convT[:, :, z], convT[:, :, z], headT[:, :, z], ALU.mult).then_inc(s["weighted"], 1)
                for g in range(2):
                    z = slice(g * BANK, (g + 1) * BANK)
                    dve.wait_ge(*jobs.taken(("mg", 1, g)))
                    dve.wait_ge(s["weighted"], g + 1)
                    nc.vector.tensor_tensor(gateT[:, :, z], gateT[:, :, z], convT[:, :, z], ALU.mult).then_inc(s["gated"], 1)
                add_rows(c, dve, step, jobs, s, "mix", c.row("mix_b"))


EMBEDS, RATIOS = (96, 144, 192), (2, 3, 4)


def mask_entangled_ffn(c, pool, step):
    nc = c.nc
    for name in ("ffn_fcT", "ffn_proj"):
        pool.wait_ge(c.weights_in[name], 16)
    alpha = c.row("alpha")
    for i in range(3):
        step.then(nc.gpsimd.tensor_scalar(c.choice[:, 3 * i:3 * i + 3], alpha[:, 3:6], alpha[:, i:i + 1], None, ALU.mult))
    step.mark(nc.gpsimd.memset(c.coef_in[:, :, :], 0.0))
    step.then(nc.gpsimd.memset(c.coef_hid[:, :, :], 0.0))

    def add_choice(region, a):
        step.then(nc.gpsimd.tensor_scalar(region, region, a, None, ALU.add))

    for i, e in enumerate(EMBEDS):
        for j, r in enumerate(RATIOS):
            a, wide = c.choice[:, 3 * i + j:3 * i + j + 1], r * e
            add_choice(c.coef_in[:, 0, 0:wide], a[0:HF])
            if e > HF:
                add_choice(c.coef_in[0:e - HF, 1, 0:wide], a[0:e - HF])
            add_choice(c.coef_hid[:, 0:wide // P, 0:e], a)
            if wide % P:
                add_choice(c.coef_hid[0:wide % P, wide // P, 0:e], a[0:wide % P])
    step.mark(nc.gpsimd.tensor_tensor(c.ffn_b0[:, :], c.col("ffn_b_fc"), c.coef_hid[:, :, 0], ALU.mult))
    step.mark(nc.gpsimd.tensor_tensor(c.ffn_b1[:, :], c.row("ffn_b_proj"), c.coef_hid[:, 0, :], ALU.mult))
    step.mark(nc.gpsimd.tensor_tensor(c.tile["ffn_fcT"][:, :, :], c.tile["ffn_fcT"][:, :, :], c.coef_in[:, :, :], ALU.mult))
    step.then(nc.gpsimd.tensor_tensor(c.tile["ffn_proj"][:, :, :], c.tile["ffn_proj"][:, :, :], c.coef_hid[:, :, :], ALU.mult))


def entangled_ffn(c):
    nc = c.nc
    with ExitStack() as mem:
        hid = mem.enter_context(nc.sbuf_tensor("ffn_hidden", [P, FT, T], F32))
        order = [(("h", m, g), "s") for g in range(2) for m in range(FT)] + [(("out", t), "v") for t in range(0, NT, 2)]
        with stage(nc, JOB_SEMS) as (block, s):
            jobs = Jobs(c, s, order)

            @block.tensor
            def _(pe):
                for key, _ in order:
                    bank = jobs.bank(key)
                    jobs.bank_free(pe, key)
                    if key[0] == "h":
                        _, m, g = key
                        for k in range(2):
                            last = pe.matmul(bank, c.tile["ffn_fcT"][:, k, m * P:(m + 1) * P], c.XT[:, k, g * BANK:(g + 1) * BANK],
                                             start=(k == 0), stop=(k == 1))
                    else:
                        pe.wait_ge(*jobs.taken(("h", FT - 1, key[1] // 4)))
                        for i in range(2):
                            t = key[1] + i
                            for m in range(FT):
                                last = pe.matmul(bank[:, i * D:(i + 1) * D], hid[:, m, t * P:(t + 1) * P],
                                                 c.tile["ffn_proj"][:, m, :], start=(m == 0), stop=(m == FT - 1))
                    last.then_inc(s["product_ready"], 1)

            @block.scalar
            def _(act):
                for key in jobs.by("s"):
                    _, m, g = key
                    act.wait_ge(*jobs.ready(key))
                    nc.scalar.activation(hid[:, m, g * BANK:(g + 1) * BANK], jobs.bank(key), ACT.Gelu_apprx_tanh,
                                         bias=c.ffn_b0[:, m:m + 1]).then_inc(s["scalar_took"], 1)

            @block.vector
            def _(dve):
                add_rows(c, dve, Steps(dve, s["vector_step"]), jobs, s, "out", c.ffn_b1[:, :])


COMBOS = B * PAIRS
ORDER_RP = [(b, hg) for b in range(B) for hg in range(HG)]


def combo(b, p):
    return b * PAIRS + p


def nystrom_attention(c):
    nc = c.nc
    with ExitStack() as mem:
        def sb(name, shape):
            return mem.enter_context(nc.sbuf_tensor(name, shape, F32))
        c.Vtok = sb("nys_Vtok", [P, NT, D])
        c.k1T = sb("nys_k1T", [P, PAIRS, T])
        c.W = sb("nys_W", [P, COMBOS, HD])
        c.QL, c.KL = sb("nys_QL", [P, HG, B * LM]), sb("nys_KL", [P, HG, B * LM])
        with ExitStack() as early:
            c.QT, c.KTok = c.sb("nys_QT", [P, HG, T], early), c.sb("nys_KT_feat", [P, HG, T], early)
            nystrom_project(c)
            nystrom_token_kernels(c)
        c.KT, c.V, c.VT = (sb(n, [P, COMBOS, P]) for n in ("nys_KT", "nys_inv", "nys_invT"))
        nystrom_landmark_kernel(c)
        nystrom_invert(c)
        nystrom_apply(c)


def nystrom_project(c):
    nc = c.nc
    order = [(("qk", m, g), "s") for m in range(2 * HG) for g in range(2)] + [(("v", t), "v") for t in range(0, NT, 2)]
    with stage(nc, JOB_SEMS) as (block, s):
        jobs = Jobs(c, s, order)

        @block.tensor
        def _(pe):
            for key, _ in order:
                bank = jobs.bank(key)
                jobs.bank_free(pe, key)
                if key[0] == "qk":
                    _, m, g = key
                    for k in range(2):
                        last = pe.matmul(bank, c.tile["nys_qk"][:, k, m * P:(m + 1) * P], c.XT[:, k, g * BANK:(g + 1) * BANK],
                                         start=(k == 0), stop=(k == 1))
                else:
                    for i in range(2):
                        t = key[1] + i
                        for k in range(2):
                            last = pe.matmul(bank[:, i * D:(i + 1) * D], c.XT[:, k, t * P:(t + 1) * P], c.tile["nys_v"][:, k, :],
                                             start=(k == 0), stop=(k == 1))
                last.then_inc(s["product_ready"], 1)

        @block.scalar
        def _(act):
            for key in jobs.by("s"):
                _, m, g = key
                act.wait_ge(*jobs.ready(key))
                dst, scale = (c.QT, 1.0 / HD ** 0.5) if m < HG else (c.KTok, 1.0)
                nc.scalar.mul(dst[:, m % HG, g * BANK:(g + 1) * BANK], jobs.bank(key), scale).then_inc(s["scalar_took"], 1)

        @block.vector
        def _(dve):
            step = Steps(dve, s["vector_step"])
            for key in jobs.by("v"):
                t = key[1]
                dve.wait_ge(*jobs.ready(key))
                nc.vector.tensor_copy(c.Vtok[:, t:t + 2, :], jobs.bank(key)[:, 0:2 * D].rearrange(
                    "p (t d) -> p t d", t=2)).then_inc(s["vector_took"], 1)
            for m in range(2 * HG):
                src, dst = (c.QT, c.QL) if m < HG else (c.KTok, c.KL)
                dve.wait_ge(*jobs.taken(("qk", m, 1)))
                step.then(nc.vector.tensor_reduce(dst[:, m % HG, :], src[:, m % HG, :].rearrange(
                    "p (l s) -> p l s", s=N // LM), AX.X, ALU.add))
                step.mark(nc.vector.tensor_scalar(dst[:, m % HG, :], dst[:, m % HG, :], 1.0 / (N // LM), None, ALU.mult))


def head_rows(h):
    return slice(SLOT * (h % 4), SLOT * (h % 4) + SLOT)


def nystrom_landmark_kernel(c):
    nc = c.nc
    with ExitStack() as mem:
        def sb(name, shape):
            return mem.enter_context(nc.sbuf_tensor(name, shape, F32))
        shifted = sb("k2_shifted", [P, COMBOS, LM])
        kexp = sb("k2_exp", [P, COMBOS, LM])
        K = sb("k2", [P, COMBOS, LM])
        Kdiag = sb("k2_diag", [P, COMBOS, P])
        kmax, ksum, kinv = sb("k2_max", [P, COMBOS]), sb("k2_sum", [P, COMBOS]), sb("k2_inv", [P, COMBOS])
        colsum, dinv = sb("k2_colsum", [P, COMBOS]), sb("k2_dinv", [P, COMBOS])
        best = sb("k2_best", [COMBOS, 2])
        spread = sb("k2_spread", [COMBOS, P])
        order = [(("k2", rp, n), "v") for rp in range(2) for n in range(2)]
        order += [(("turn", n), "v") for n in range(6)] + [(("sums",), "v"), (("inv",), "v")]
        with stage(nc, JOB_SEMS + "exped diag_zero diag_ready colsum_ready spread_ready") as (block, s):
            jobs = Jobs(c, s, order)

            def members(rp, n):
                return [(b, 2 * hg + rp) for b, hg in ORDER_RP[6 * n:6 * n + 6]]

            @block.gpsimd
            def _(pool):
                nc.gpsimd.memset(Kdiag[:, :, :], 0.0).then_inc(s["diag_zero"], 1)

            @block.tensor
            def _(pe):
                for key, _ in order:
                    kind, bank = key[0], jobs.bank(key)
                    jobs.bank_free(pe, key)
                    if kind == "k2":
                        for i, (b, p) in enumerate(members(key[1], key[2])):
                            for half in range(2):
                                h = 2 * p + half
                                r, z = head_rows(h), slice(b * LM, (b + 1) * LM)
                                last = pe.matmul(bank[64 * half:64 * half + 64, i * LM:(i + 1) * LM],
                                                 c.QL[r, h // 4, z], c.KL[r, h // 4, z], start=True, stop=True,
                                                 tile_position=(SLOT * (h % 4), 64 * half))
                    elif kind == "turn":
                        pe.wait_ge(s["diag_ready"], 1)
                        for i in range(4):
                            last = pe.transpose(bank[:, i * P:(i + 1) * P], Kdiag[:, 4 * key[1] + i, :], c.ident[:, :])
                    elif kind == "sums":
                        pe.wait_ge(s["colsum_ready"], 1)
                        last = pe.transpose(bank[0:COMBOS, 0:P], colsum[:, :], c.ident[:, :])
                    else:
                        pe.wait_ge(s["spread_ready"], 1)
                        last = pe.transpose(bank[:, 0:COMBOS], spread[:, :], c.ident[0:COMBOS, 0:COMBOS])
                    last.then_inc(s["product_ready"], 1)

            @block.scalar
            def _(act):
                act.wait_ge(*jobs.taken(("k2", 1, 1)))
                nc.scalar.activation(kexp[:, :, :], shifted[:, :, :], ACT.Exp).then_inc(s["exped"], 1)

            @block.vector
            def _(dve):
                step = Steps(dve, s["vector_step"])
                for key in [k for k in jobs.by("v") if k[0] == "k2"]:
                    _, rp, n = key
                    dve.wait_ge(*jobs.ready(key))
                    src = jobs.bank(key)[:, 0:6 * LM].rearrange("p (b g l) -> p b g l", b=2, g=HG)
                    view = lambda m: m.rearrange("p (b g r) -> p b g r", b=B, g=HG)[:, 2 * n:2 * n + 2, :, rp]
                    step.then(nc.vector.tensor_reduce(view(kmax), src, AX.X, ALU.max))
                    dst = shifted.rearrange("p (b g r) l -> p b g r l", b=B, g=HG)
                    for b in range(2):
                        last = nc.vector.tensor_tensor(dst[:, 2 * n + b, :, rp, :], src[:, b], view(kmax)[:, b].unsqueeze(
                            2).to_broadcast([P, HG, LM]), ALU.subtract)
                    last.then_inc(s["vector_took"], 1)
                dve.wait_ge(s["exped"], 1)
                step.then(nc.vector.tensor_reduce(ksum[:, :], kexp[:, :, :], AX.X, ALU.add))
                step.then(nc.vector.reciprocal(kinv[:, :], ksum[:, :]))
                step.then(nc.vector.tensor_tensor(K[:, :, :], kexp[:, :, :], kinv[:, :].unsqueeze(2).to_broadcast(
                    [P, COMBOS, LM]), ALU.mult))
                dve.wait_ge(s["diag_zero"], 1)
                nc.vector.tensor_copy(Kdiag[0:64, :, 0:LM], K[0:64, :, :])
                nc.vector.tensor_copy(Kdiag[64:P, :, LM:P], K[64:P, :, :]).then_inc(s["diag_ready"], 1)
                for n in range(6):
                    dve.wait_ge(*jobs.ready(("turn", n)))
                    nc.vector.tensor_copy(c.KT[:, 4 * n:4 * n + 4, :].rearrange("p c l -> p (c l)"), jobs.bank(("turn", n))
                                          ).then_inc(s["vector_took"], 1)
                dve.wait_ge(*jobs.taken(("turn", 5)))
                nc.vector.tensor_reduce(colsum[:, :], c.KT[:, :, :], AX.X, ALU.add).then_inc(s["colsum_ready"], 1)
                dve.wait_ge(*jobs.ready(("sums",)))
                nc.vector.tensor_reduce(best[:, :], jobs.bank(("sums",))[0:COMBOS, 0:P].rearrange("p (h l) -> p h l", h=2),
                                        AX.X, ALU.max).then_inc(s["vector_took"], 1)
                dve.wait_ge(*jobs.taken(("sums",)))
                step.then(nc.vector.reciprocal(best[:, :], best[:, :]))
                nc.vector.tensor_copy(spread.rearrange("p (h l) -> p h l", h=2), best[:, :].unsqueeze(2).to_broadcast(
                    [COMBOS, 2, LM])).then_inc(s["spread_ready"], 1)
                dve.wait_ge(*jobs.ready(("inv",)))
                nc.vector.tensor_copy(dinv[:, :], jobs.bank(("inv",))[:, 0:COMBOS]).then_inc(s["vector_took"], 1)
                dve.wait_ge(*jobs.taken(("inv",)))
                d = dinv[:, :].unsqueeze(2).to_broadcast([P, COMBOS, P])
                nc.vector.tensor_tensor(c.V[:, :, :], c.KT[:, :, :], d, ALU.mult)
                step.then(nc.vector.tensor_tensor(c.VT[:, :, :], Kdiag[:, :, :], d, ALU.mult))


def nystrom_token_kernels(c):
    nc = c.nc
    with ExitStack() as mem:
        def sb(name, shape):
            return mem.enter_context(nc.sbuf_tensor(name, shape, F32))
        k1 = sb("k1", [P, NT, NH, LM])
        shifted, exped = sb("k1_shifted", [P, 2, 8, LM]), sb("k1_exped", [P, 2, 8, LM])
        kmax, ksum, kinv = (sb("k1_" + n, [P, NT * NH // 8, 8]) for n in ("max", "sum", "inv"))
        KLdiag = sb("k1_landmarks", [P, HG, B, 4, LM])
        k3 = sb("k3", [P, COMBOS, N])
        k3T = c.k1T.rearrange("p q t -> p (q t)").rearrange("p (c j l) -> p c j l", c=COMBOS, j=TPB)
        k3max, k3sum, k3inv = sb("k3_max", [P, COMBOS]), sb("k3_sum", [P, COMBOS]), sb("k3_inv", [P, COMBOS])
        k3jobs = [("k3", rp, n) for rp in range(2) for n in range(6)]
        k1jobs = [("k1", n) for n in range(NT * NH // 8)]
        order = [(k, "s") for k in k3jobs] + [(k, "v") for k in k1jobs]
        order += [(("k3T", n), "s") for n in range(12)]
        order += [(("W", n), "v") for n in range(2 * B)]
        order += [(("k1T", p, g), "vs"[g]) for p in range(PAIRS) for g in range(2)]
        with stage(nc, JOB_SEMS + "k3max_ready k1_exped k1_normed diag_zero diag_ready") as (block, s):
            jobs = Jobs(c, s, order)

            def members(rp, n):
                return [(b, 2 * hg + rp) for b, hg in ORDER_RP[2 * n:2 * n + 2]]

            @block.gpsimd
            def _(pool):
                nc.gpsimd.memset(KLdiag[:, :, :, :, :], 0.0).then_inc(s["diag_zero"], 1)

            @block.tensor
            def _(pe):
                for key, _ in order:
                    kind, bank = key[0], jobs.bank(key)
                    jobs.bank_free(pe, key)
                    if kind == "k3":
                        for i, (b, p) in enumerate(members(key[1], key[2])):
                            for half in range(2):
                                h = 2 * p + half
                                r = head_rows(h)
                                last = pe.matmul(bank[64 * half:64 * half + 64, i * N:(i + 1) * N],
                                                 c.QL[r, h // 4, b * LM:(b + 1) * LM], c.KTok[r, h // 4, b * N:(b + 1) * N],
                                                 start=True, stop=True, tile_position=(SLOT * (h % 4), 64 * half))
                    elif kind == "k1":
                        pe.wait_ge(s["diag_ready"], 4)
                        for i in range(2):
                            t, hg = divmod(2 * key[1] + i, HG)
                            last = pe.matmul(bank[:, i * N:(i + 1) * N], c.QT[:, hg, t * P:(t + 1) * P],
                                             KLdiag[:, hg, t // TPB].rearrange("p r l -> p (r l)"), start=True, stop=True)
                    elif kind == "k3T":
                        n = key[1]
                        pe.wait_ge(*jobs.taken(k3jobs[-1]))
                        for i in range(4):
                            last = pe.transpose(bank[:, i * P:(i + 1) * P], k3[:, 2 * n + i // 2, (i % 2) * P:(i % 2 + 1) * P],
                                                c.ident[:, :])
                    elif kind == "W":
                        for i in range(3):
                            co = 3 * key[1] + i
                            b, w0 = co // PAIRS, 32 * i
                            pe.wait_ge(*jobs.taken(("k3T", co // 2)))
                            for j in range(TPB):
                                last = pe.matmul(bank[:, i * P:(i + 1) * P], k3T[:, co, j, :],
                                                 c.Vtok[:, TPB * b + j, w0:w0 + P], start=(j == 0), stop=(j == 1))
                    else:
                        _, p, g = key
                        pe.wait_ge(s["k1_normed"], len(k1jobs) // 2 * (g + 1))
                        for i in range(4):
                            last = pe.transpose(bank[:, i * P:(i + 1) * P],
                                                k1[:, 4 * g + i, 2 * p:2 * p + 2, :].rearrange("p h l -> p (h l)"),
                                                c.ident[:, :])
                    last.then_inc(s["product_ready"], 1)

            @block.scalar
            def _(act):
                for n, key in enumerate(k3jobs):
                    act.wait_ge(s["k3max_ready"], n + 1)
                    for i, (b, p) in enumerate(members(key[1], key[2])):
                        co = combo(b, p)
                        last = nc.scalar.activation(k3[:, co, :], jobs.bank(key)[:, i * N:(i + 1) * N], ACT.Exp,
                                                    bias=k3max[:, co:co + 1], accum_out=k3sum[:, co:co + 1])
                    last.then_inc(s["scalar_took"], 1)
                for n, key in enumerate(k1jobs):
                    act.wait_ge(*jobs.taken(key))
                    if n >= 2:
                        act.wait_ge(s["k1_normed"], n - 1)
                    nc.scalar.activation(exped[:, n % 2], shifted[:, n % 2], ACT.Exp).then_inc(s["k1_exped"], 1)
                for n in range(12):
                    act.wait_ge(*jobs.ready(("k3T", n)))
                    nc.scalar.copy(k3T[:, 2 * n:2 * n + 2, :, :].rearrange("p c j l -> p (c j l)"),
                                   jobs.bank(("k3T", n))).then_inc(s["scalar_took"], 1)
                for p in range(PAIRS):
                    act.wait_ge(*jobs.ready(("k1T", p, 1)))
                    nc.scalar.copy(c.k1T[:, p, BANK:T], jobs.bank(("k1T", p, 1))).then_inc(s["scalar_took"], 1)

            @block.vector
            def _(dve):
                step = Steps(dve, s["vector_step"])
                for key in k3jobs:
                    _, rp, n = key
                    dve.wait_ge(*jobs.ready(key))
                    for i, (b, p) in enumerate(members(rp, n)):
                        co = combo(b, p)
                        last = nc.vector.tensor_reduce(k3max[:, co:co + 1], jobs.bank(key)[:, i * N:(i + 1) * N], AX.X,
                                                       ALU.max, negate=True)
                    last.then_inc(s["k3max_ready"], 1)

                dve.wait_ge(s["diag_zero"], 1)
                for r in range(4):
                    rows = head_rows(r)
                    nc.vector.tensor_copy(KLdiag[rows, :, :, r, :], c.KL[rows].rearrange("p g (b l) -> p g b l", b=B)
                                          ).then_inc(s["diag_ready"], 1)

                def normalise(n):
                    dve.wait_ge(s["k1_exped"], n + 1)
                    step.then(nc.vector.tensor_reduce(ksum[:, n], exped[:, n % 2], AX.X, ALU.add))
                    step.then(nc.vector.reciprocal(kinv[:, n], ksum[:, n]))
                    dst = k1.rearrange("p t h l -> p (t h) l")[:, 8 * n:8 * n + 8, :]
                    nc.vector.tensor_tensor(dst, exped[:, n % 2], kinv[:, n].unsqueeze(2).to_broadcast([P, 8, LM]),
                                            ALU.mult).then_inc(s["k1_normed"], 1)

                for n, key in enumerate(k1jobs):
                    dve.wait_ge(*jobs.ready(key))
                    src = jobs.bank(key).rearrange("p (a l) -> p a l", l=LM)
                    step.then(nc.vector.tensor_reduce(kmax[:, n], src, AX.X, ALU.max))
                    if n >= 2:
                        dve.wait_ge(s["k1_exped"], n - 1)
                    nc.vector.tensor_tensor(shifted[:, n % 2], src, kmax[:, n].unsqueeze(2).to_broadcast([P, 8, LM]),
                                            ALU.subtract).then_inc(s["vector_took"], 1)
                    if n:
                        normalise(n - 1)
                normalise(len(k1jobs) - 1)
                dve.wait_ge(*jobs.taken(k3jobs[-1]))
                step.then(nc.vector.reciprocal(k3inv[:, :], k3sum[:, :]))
                for n in range(2 * B):
                    dve.wait_ge(*jobs.ready(("W", n)))
                    z = slice(3 * n, 3 * n + 3)
                    at = 96 * (n % 2)
                    src = jobs.bank(("W", n))[:, 0:3 * P].rearrange("p (c x) -> p c x", x=P)
                    for half in range(2):
                        r = slice(64 * half, 64 * half + 64)
                        last = nc.vector.tensor_tensor(c.W[r, z, :], src[r, :, at + HD * half:at + HD * half + HD],
                                                       k3inv[r, z].unsqueeze(2).to_broadcast([64, 3, HD]), ALU.mult)
                    last.then_inc(s["vector_took"], 1)
                for p in range(PAIRS):
                    dve.wait_ge(*jobs.ready(("k1T", p, 0)))
                    nc.vector.tensor_copy(c.k1T[:, p, 0:BANK], jobs.bank(("k1T", p, 0))).then_inc(s["vector_took"], 1)


def nystrom_invert(c):
    nc = c.nc
    G, ITERS, BANKS = 6, 6, 6
    PER = COMBOS // G
    with ExitStack() as mem:
        def sb(name, shape):
            return mem.enter_context(nc.sbuf_tensor(name, shape, F32))
        AT = sb("inv_AT", [P, COMBOS, P])
        R = sb("inv_rest", [P, COMBOS, P])
        eyes = sb("inv_eyes", [P, 3, P])
        products = {"A": (c.KT, c.V, "v"), "AT": (c.V, c.KT, "s"), "C": (AT, R, "v"), "E": (AT, R, "v"),
                    "V": (c.VT, R, "s"), "VT": (R, c.VT, "s")}
        keys = [(name, g) for names in (("A", "AT"), ("C",), ("E",), ("V", "VT")) for g in range(G) for name in names]
        by = {who: [key for key in keys if products[key[0]][2] == who] for who in "vs"}
        NJ = len(keys)
        assert NJ % BANKS == 0
        with stage(nc, JOB_SEMS) as (block, s):

            def group(m, g):
                return m[:, PER * g:PER * g + PER, :].rearrange("p c l -> p (c l)")

            def bank(key):
                return c.bank[keys.index(key) % BANKS]

            def taken(key, it):
                who = products[key[0]][2]
                return s["vector_took" if who == "v" else "scalar_took"], it * len(by[who]) + by[who].index(key) + 1

            @block.tensor
            def _(pe):
                pe.wait_ge(s["vector_step"], 3)

                def iterate(it, first=False):
                    for k, key in enumerate(keys):
                        name, g = key
                        if k >= BANKS:
                            pe.wait_ge(*taken(keys[k - BANKS], it))
                        elif not first:
                            pe.wait_ge(*taken(keys[k + NJ - BANKS], it - 1))
                        if name == "A" and not first:
                            pe.wait_ge(*taken(("VT", g), it - 1))
                        if name == "C":
                            pe.wait_ge(*taken(("A", g), it))
                            pe.wait_ge(*taken(("AT", g), it))
                        if name == "E":
                            pe.wait_ge(*taken(("C", g), it))
                        if name == "V":
                            pe.wait_ge(*taken(("E", g), it))
                        lhsT, rhs, _ = products[name]
                        for i in range(PER):
                            last = pe.matmul(bank(key)[:, i * P:(i + 1) * P], lhsT[:, PER * g + i, :], rhs[:, PER * g + i, :],
                                             start=True, stop=True)
                        last.then_inc(s["product_ready"], 1)

                iterate(0, first=True)
                with pe.Fori(1, ITERS, 1) as it:
                    iterate(it)

            @block.scalar
            def _(act):
                with act.Fori(0, ITERS, 1) as it:
                    for key in by["s"]:
                        name, g = key
                        k = keys.index(("VT", g) if name == "V" else key)
                        act.wait_ge(s["product_ready"], it * NJ + k + 1)
                        dst, scale = {"AT": (AT, 1.0), "V": (c.V, 0.25), "VT": (c.VT, 0.25)}[name]
                        nc.scalar.mul(group(dst, g), bank(key), scale).then_inc(s["scalar_took"], 1)

            @block.vector
            def _(dve):
                step = Steps(dve, s["vector_step"])
                for i, a in enumerate((7.0, 15.0, 13.0)):
                    step.mark(nc.vector.tensor_scalar(eyes[:, i, :], c.ident[:, :], a, None, ALU.mult))
                dve.wait_ge(s["vector_step"], step.n)
                with dve.Fori(0, ITERS, 1) as it:
                    for key in by["v"]:
                        name, g = key
                        dve.wait_ge(s["product_ready"], it * NJ + keys.index(key) + 1)
                        eye = eyes[:, {"A": 0, "C": 1, "E": 2}[name], :].unsqueeze(1).to_broadcast([P, PER, P])
                        nc.vector.scalar_tensor_tensor(
                            R[:, PER * g:PER * g + PER, :], bank(key).rearrange("p (c l) -> p c l", c=PER), -1.0, eye,
                            ALU.mult, ALU.add).then_inc(s["vector_took"], 1)


def nystrom_apply(c):
    nc = c.nc
    with ExitStack() as mem:
        Zdiag = mem.enter_context(nc.sbuf_tensor("nys_Z", [P, COMBOS, 32], F32))
        SVT = mem.enter_context(nc.sbuf_tensor("nys_SVT", [HF, 2, T], F32))
        order = [(("Z",), "v")] + [(("sv", hh, g), "sv"[hh]) for g in range(2) for hh in range(2)]
        order += [(("out", t), "v") for t in range(0, NT, 2)]
        with stage(nc, JOB_SEMS + "z_zero") as (block, s):
            jobs = Jobs(c, s, order)

            @block.gpsimd
            def _(pool):
                nc.gpsimd.memset(Zdiag[:, :, :], 0.0).then_inc(s["z_zero"], 1)

            @block.tensor
            def _(pe):
                for key, _ in order:
                    kind, bank = key[0], jobs.bank(key)
                    jobs.bank_free(pe, key)
                    if kind == "Z":
                        for co in range(COMBOS):
                            for half in range(2):
                                r = slice(64 * half, 64 * half + 64)
                                last = pe.matmul(bank[r, co * HD:(co + 1) * HD], c.VT[r, co, r], c.W[r, co, :], start=True,
                                                 stop=True, tile_position=(64 * half, 64 * half))
                    elif kind == "sv":
                        _, hh, g = key
                        pe.wait_ge(*jobs.taken(("Z",)))
                        for j in range(3):
                            p = 3 * hh + j
                            for b2 in range(2):
                                b = 2 * g + b2
                                last = pe.matmul(bank[32 * j:32 * j + 32, b2 * N:(b2 + 1) * N], Zdiag[:, combo(b, p), :],
                                                 c.k1T[:, p, b * N:(b + 1) * N], start=True, stop=True,
                                                 tile_position=(0, 32 * j))
                    else:
                        t0 = key[1]
                        for hh in range(2):
                            pe.wait_ge(*jobs.taken(("sv", hh, t0 // 4)))
                        for i in range(2):
                            t = t0 + i
                            for k in range(2):
                                last = pe.matmul(bank[:, i * D:(i + 1) * D], SVT[:, k, t * P:(t + 1) * P], c.tile["nys_proj"][:, k, :],
                                                 start=(k == 0), stop=(k == 1))
                    last.then_inc(s["product_ready"], 1)

            @block.scalar
            def _(act):
                for key in jobs.by("s"):
                    g = key[2]
                    act.wait_ge(*jobs.ready(key))
                    nc.scalar.copy(SVT[:, 0, g * BANK:(g + 1) * BANK], jobs.bank(key)[0:HF, :]).then_inc(s["scalar_took"], 1)

            @block.vector
            def _(dve):
                step = Steps(dve, s["vector_step"])
                step.then(nc.vector.tensor_tensor(c.H[:, :, :], c.H[:, :, :], c.Vtok[:, :, :], ALU.add))
                dve.wait_ge(*jobs.ready(("Z",)))
                dve.wait_ge(s["z_zero"], 1)
                src = jobs.bank(("Z",))[:, 0:COMBOS * HD].rearrange("p (c d) -> p c d", c=COMBOS)
                nc.vector.tensor_copy(Zdiag[0:64, :, 0:HD], src[0:64])
                nc.vector.tensor_copy(Zdiag[64:P, :, HD:32], src[64:P]).then_inc(s["vector_took"], 1)
                for g in range(2):
                    dve.wait_ge(*jobs.ready(("sv", 1, g)))
                    nc.vector.tensor_copy(SVT[:, 1, g * BANK:(g + 1) * BANK], jobs.bank(("sv", 1, g))[0:HF, :]
                                          ).then_inc(s["vector_took"], 1)
                add_rows(c, dve, step, jobs, s, "out", c.row("nys_b_proj"))



def softmax_rows(c, dve, step, s, logits, work, shape):
    nc = c.nc
    mx, sm = work
    step.then(nc.vector.tensor_reduce(mx, logits, AX.X, ALU.max))
    nc.vector.tensor_tensor(logits, logits, mx.unsqueeze(2).to_broadcast(shape), ALU.subtract).then_inc(s["shifted"], 1)
    dve.wait_ge(s["exped"], 1)
    step.then(nc.vector.tensor_reduce(sm, logits, AX.X, ALU.add))
    step.then(nc.vector.reciprocal(sm, sm))
    step.then(nc.vector.tensor_tensor(logits, logits, sm.unsqueeze(2).to_broadcast(shape), ALU.mult))


def pick_first_best(c, step, probs, best, eq, onehot, rank, shape):
    nc = c.nc
    bc = lambda m: m.unsqueeze(2).to_broadcast(shape)
    step.then(nc.vector.tensor_reduce(best, probs, AX.X, ALU.max))
    step.then(nc.vector.tensor_tensor(eq, probs, bc(best), ALU.is_equal))
    step.then(nc.vector.tensor_tensor(eq, eq, rank.unsqueeze(1).to_broadcast(shape), ALU.mult))
    step.then(nc.vector.tensor_reduce(c.pick_top[:, :], eq, AX.X, ALU.max))
    step.then(nc.vector.tensor_tensor(onehot, eq, bc(c.pick_top[:, :]), ALU.is_equal))


def route_top2(c, router, gate, slots, block_expert, eps, b2=None):
    nc = c.nc
    E = 8
    shape = [P, NT, E]
    with ExitStack() as mem:
        def sb(name, shape_):
            return mem.enter_context(nc.sbuf_tensor(name + str(c.uid()), shape_, F32))
        probs, eq, one1, one2 = sb("probs", shape), sb("eq", shape), sb("first", shape), sb("second", shape)
        mx, sm, tot = (sb(n, [P, NT]) for n in ("mx", "sm", "tot"))
        m1, m2 = gate
        chosen, gates = sb("chosen", shape), sb("gates", shape)
        places = Places(c, mem, E)
        gatesT = sb("gatesT", [E, T])
        order = [(("logits",), "v"), (("count",), "v")]
        if b2 is not None:
            order += [(("turn", g), "v") for g in range(2)] + [(("out", t), "v") for t in range(0, NT, 2)]
        with stage(nc, JOB_SEMS + "shifted exped picked gates_ready") as (block, s):
            jobs = Jobs(c, s, order)

            @block.tensor
            def _(pe):
                for name in ("moe1_gate", "moe1_b2"):
                    pe.wait_ge(c.weights_in[name], 16)
                for key, _ in order:
                    bank = jobs.bank(key)
                    if key[0] == "logits":
                        for t in range(NT):
                            for k in range(2):
                                last = pe.matmul(bank[:, t * E:(t + 1) * E], c.XT[:, k, t * P:(t + 1) * P], router[:, k, :],
                                                 start=(k == 0), stop=(k == 1))
                    elif key[0] == "count":
                        pe.wait_ge(s["picked"], 1)
                        last = places.count(pe, bank, chosen)
                    elif key[0] == "turn":
                        pe.wait_ge(s["gates_ready"], 1)
                        for i in range(4):
                            last = pe.transpose(bank[0:E, i * P:(i + 1) * P], gates[:, 4 * key[1] + i, :], c.ident[:, :])
                    else:
                        pe.wait_ge(*jobs.taken(("turn", 1)))
                        for i in range(2):
                            t = key[1] + i
                            last = pe.matmul(bank[:, i * D:(i + 1) * D], gatesT[:, t * P:(t + 1) * P], b2[:, :],
                                             start=True, stop=True)
                    last.then_inc(s["product_ready"], 1)

            @block.scalar
            def _(act):
                act.wait_ge(s["shifted"], 1)
                nc.scalar.activation(probs[:, :, :], probs[:, :, :], ACT.Exp).then_inc(s["exped"], 1)

            @block.vector
            def _(dve):
                step = Steps(dve, s["vector_step"])
                dve.wait_ge(*jobs.ready(("logits",)))
                nc.vector.tensor_copy(probs[:, :, :], jobs.bank(("logits",))[:, 0:NT * E].rearrange(
                    "p (t e) -> p t e", e=E)).then_inc(s["vector_took"], 1)
                dve.wait_ge(*jobs.taken(("logits",)))
                softmax_rows(c, dve, step, s, probs[:, :, :], (mx[:, :], sm[:, :]), shape)
                rank = c.rank[:, 0:E]
                pick_first_best(c, step, probs[:, :, :], m1[:, :], eq[:, :, :], one1[:, :, :], rank, shape)
                step.then(nc.vector.scalar_tensor_tensor(probs[:, :, :], one1[:, :, :], -2.0, probs[:, :, :], ALU.mult,
                                                         ALU.add))
                pick_first_best(c, step, probs[:, :, :], m2[:, :], eq[:, :, :], one2[:, :, :], rank, shape)
                nc.vector.tensor_tensor(chosen[:, :, :], one1[:, :, :], one2[:, :, :], ALU.add).then_inc(s["picked"], 1)
                dve.wait_ge(*jobs.ready(("count",)))
                places.find(dve, step, jobs, (one1, one2), slots, block_expert)
                step.then(nc.vector.tensor_tensor(tot[:, :], m1[:, :], m2[:, :], ALU.add))
                if eps:
                    step.then(nc.vector.tensor_scalar(tot[:, :], tot[:, :], eps, None, ALU.add))
                step.then(nc.vector.reciprocal(tot[:, :], tot[:, :]))
                for m in (m1, m2):
                    step.then(nc.vector.tensor_tensor(m[:, :], m[:, :], tot[:, :], ALU.mult))
                if b2 is not None:
                    for one, m in ((one1, m1), (one2, m2)):
                        step.then(nc.vector.tensor_tensor(one[:, :, :], one[:, :, :], m[:, :].unsqueeze(2).to_broadcast(
                            shape), ALU.mult))
                    nc.vector.tensor_tensor(gates[:, :, :], one1[:, :, :], one2[:, :, :], ALU.add).then_inc(
                        s["gates_ready"], 1)
                    for g in range(2):
                        dve.wait_ge(*jobs.ready(("turn", g)))
                        nc.vector.tensor_copy(gatesT[:, g * BANK:(g + 1) * BANK], jobs.bank(("turn", g))[0:E, :]
                                              ).then_inc(s["vector_took"], 1)
                    add_rows(c, dve, step, jobs, s, "out")


class Places:

    def __init__(self, c, mem, experts):
        self.c, self.E = c, experts

        def sb(name, shape):
            return mem.enter_context(c.nc.sbuf_tensor(name + str(c.uid()), shape, F32))
        self.counts = sb("counts", [P, NT + 1, experts])
        self.over, self.blocks = sb("over", [P, experts, T // P]), sb("blocks", [P, experts])
        self.ahead, self.start = sb("ahead", [P, experts, experts]), sb("start", [P, experts])
        self.end = sb("end", [P, experts])
        self.past, self.number = sb("past", [P, BLOCKS, experts]), sb("number", [P, BLOCKS])
        self.where, self.slot = sb("where", [P, NT, experts]), sb("slot", [P, NT])

    def count(self, pe, bank, chosen):
        flat, n = chosen.rearrange("p t e -> p (t e)"), NT * self.E
        pe.matmul(bank[:, 0:n], self.c.tri[:, :], flat, start=True, stop=True)
        return pe.matmul(bank[:, n:2 * n], self.c.full[:, :], flat, start=True, stop=True)

    def find(self, dve, step, jobs, picks, slots, block_expert):
        c, nc, E = self.c, self.c.nc, self.E
        counts, start = self.counts, self.start
        both = jobs.bank(("count",))[:, 0:2 * NT * E].rearrange("p (w t e) -> p w t e", w=2, t=NT)
        step.then(nc.vector.memset(counts[:, 0, :], 0.0))
        for t in range(NT):
            step.then(nc.vector.tensor_tensor(counts[:, t + 1, :], counts[:, t, :], both[:, 1, t, :], ALU.add))
        nc.vector.tensor_tensor(counts[:, 0:NT, :], counts[:, 0:NT, :], both[:, 0], ALU.add
                                ).then_inc(jobs.sems["vector_took"], 1)
        dve.wait_ge(*jobs.taken(("count",)))
        shape = [P, E, T // P]
        step.then(nc.vector.tensor_tensor(self.over[:, :, :], counts[:, NT, :].unsqueeze(2).to_broadcast(shape),
                                          c.multiples[:, 0:T // P].unsqueeze(1).to_broadcast(shape), ALU.is_gt))
        step.then(nc.vector.tensor_reduce(self.blocks[:, :], self.over[:, :, :], AX.X, ALU.add))
        step.then(nc.vector.tensor_tensor(self.ahead[:, :, :], c.before[:, 0:E, 0:E],
                                          self.blocks[:, :].unsqueeze(1).to_broadcast([P, E, E]), ALU.mult))
        step.then(nc.vector.tensor_reduce(start[:, :], self.ahead[:, :, :], AX.X, ALU.add))
        step.then(nc.vector.scalar_tensor_tensor(self.end[:, :], self.blocks[:, :], float(P), start[:, :], ALU.mult, ALU.add))
        shape = [P, BLOCKS, E]
        step.then(nc.vector.tensor_tensor(self.past[:, :, :], c.multiples[:, :].unsqueeze(2).to_broadcast(shape),
                                          self.end[:, :].unsqueeze(1).to_broadcast(shape), ALU.is_ge))
        step.then(nc.vector.tensor_reduce(self.number[:, :], self.past[:, :, :], AX.X, ALU.add))
        step.then(nc.vector.tensor_scalar(block_expert[:, :], self.number[:, :], float(E - 1), None, ALU.min))
        step.then(nc.vector.tensor_scalar(start[:, :], start[:, :], -1.0, None, ALU.add))
        shape = [P, NT, E]
        step.then(nc.vector.tensor_tensor(counts[:, 0:NT, :], counts[:, 0:NT, :], start[:, :].unsqueeze(1).to_broadcast(
            shape), ALU.add))
        for k, one in enumerate(picks):
            step.then(nc.vector.tensor_tensor(self.where[:, :, :], counts[:, 0:NT, :], one[:, :, :], ALU.mult))
            step.then(nc.vector.tensor_reduce(self.slot[:, :], self.where[:, :, :], AX.X, ALU.add))
            step.then(nc.vector.tensor_copy(slots[:, k, :], self.slot[:, :]))


def experts_in_blocks(c, name, rows, slots, block_expert, K, E, func, b1, affine, finish):
    nc = c.nc
    RING = 3
    PEEL = 5
    assert (BLOCKS - PEEL) % RING == 0
    ROUNDS = (BLOCKS - PEEL) // RING
    CHUNKS = [(0, 6), (6, 12), (12, 18), (18, BLOCKS)]
    OUT_CHUNKS = [(0, 8), (8, 16), (16, 21), (21, BLOCKS)]
    w1, w2 = c.w[name + "_w1"], c.w[name + "_w2"]
    LOADS1 = 16 * (1 if b1 is None else 2)
    turns = [(blk, k) for blk in range(BLOCKS) for k in range(2)]
    turns = [turns[i:i + 4] for i in range(0, len(turns), 4)]
    with ExitStack() as mem:
        def sb(what, shape):
            return mem.enter_context(nc.sbuf_tensor(f"{name}_{what}", shape, F32))
        xs = sb("rows", [P, BLOCKS, D])
        xT = sb("rowsT", [HF, 2, BLOCKS * P])
        hid = [sb(f"hidden{u}", [P, FT, P]) for u in range(RING)]
        outs = sb("outs", [P, NT, K, D])
        r1 = [sb(f"w1_{u}", [HF, 2, FF]) for u in range(RING)]
        r2 = [sb(f"w2_{u}", [P, FT, D]) for u in range(RING)]
        rb = [sb(f"b1_{u}", [P, FT]) for u in range(RING)]
        names = " ".join(f"w1_in{u} w2_in{u}" for u in range(RING))
        names += " " + " ".join(f"chunk{n}" for n in range(4))
        soft = c.soft
        c.soft_at["scattered"] += 16 * K * NT
        for n in range(4):
            c.soft_at[f"stored{n}"] += 16
            c.soft_at[f"back{n}"] += 16 * K * 2
        done = dict(c.soft_at)
        with stage(nc, "turned vector_took scalar_took hidden_ready hidden_taken outputs_ready outputs_taken "
                   + "vector_step " + names) as (block, s):

            @block.gpsimd
            def _(pool):
                pool.wait_ge(c.rows_zeroed, 16)
                for k in range(K):
                    for t in range(NT):
                        at = bass.IndirectOffsetOnAxis(ap=slots[:, k, t:t + 1], axis=0)
                        nc.gpsimd.indirect_dma_start(c.block_rows, at, rows[:, t, :], None).then_inc(soft["scattered"], 16)
                for n, (lo, hi) in enumerate(OUT_CHUNKS):
                    pool.wait_ge(s["outputs_taken"], hi)
                    pool.dma_start(blocks_of(c.block_outs)[:, lo:hi, :], xs[:, lo:hi, :]).then_inc(soft[f"stored{n}"], 16)
                for n in range(4):
                    pool.wait_ge(soft[f"stored{n}"], done[f"stored{n}"])
                for t in range(NT):
                    for k in range(K):
                        at = bass.IndirectOffsetOnAxis(ap=slots[:, k, t:t + 1], axis=0)
                        nc.gpsimd.indirect_dma_start(outs[:, t, k, :], None, c.block_outs, at).then_inc(soft[f"back{t // 2}"], 16)

            @block.sync
            def _(sp):
                def load(b, u, first=False):
                    e = sp.value_load(block_expert.rearrange("p (b one) -> p b one", one=1)[0:1, b, :], min_val=0, max_val=E - 1)
                    if not first:
                        sp.wait_ge(s["hidden_ready"], 2 * b - 4)
                    sp.dma_start(r1[u][:, :, :], w1[e]).then_inc(s[f"w1_in{u}"], 16)
                    if b1 is not None:
                        if not first:
                            sp.wait_ge(s["hidden_taken"], 2 * b - 4)
                        sp.dma_start(rb[u][:, :], b1[e]).then_inc(s[f"w1_in{u}"], 16)
                    if not first:
                        sp.wait_ge(s["outputs_ready"], b - 2)
                    sp.dma_start(r2[u][:, :, :], w2[e]).then_inc(s[f"w2_in{u}"], 16)

                for b in range(PEEL):
                    load(b, b % RING, first=b < RING)
                with sp.Fori(0, ROUNDS, 1) as i:
                    for j in range(RING):
                        load(RING * i + (PEEL + j), (PEEL + j) % RING)

            @block.tensor
            def _(pe):
                for n, turn in enumerate(turns):
                    bank = c.bank[n % NB]
                    if n >= NB:
                        pe.wait_ge(s[("scalar_took", "vector_took")[n % 2]], (n - NB) // 2 + 1)
                    for i, (blk, k) in enumerate(turn):
                        chunk = [m for m, (lo, hi) in enumerate(CHUNKS) if lo <= blk < hi][0]
                        pe.wait_ge(s[f"chunk{chunk}"], 16)
                        last = pe.transpose(bank[0:HF, i * P:(i + 1) * P], xs[:, blk, k * HF:(k + 1) * HF], c.ident[:, :])
                    last.then_inc(s["turned"], 1)

                def hidden(b, i, u, peeled=True):
                    pe.wait_ge(s[f"w1_in{u}"], LOADS1 * (i + 1))
                    if not peeled or b >= RING:
                        pe.wait_ge(s["outputs_taken"], b - 2)
                    for m in range(FT):
                        for k in range(2):
                            last = pe.matmul(c.bank[2 * u + m // 4][:, m % 4 * P:(m % 4 + 1) * P],
                                             r1[u][:, k, m * P:(m + 1) * P], block_columns(xT, k, b),
                                             start=(k == 0), stop=(k == 1))
                        if m in (3, FT - 1):
                            last.then_inc(s["hidden_ready"], 1)

                def outputs(b, i, u):
                    pe.wait_ge(s[f"w2_in{u}"], 16 * (i + 1))
                    pe.wait_ge(s["hidden_taken"], 2 * b + 2)
                    for m in range(FT):
                        last = pe.matmul(c.bank[2 * u + 1][:, 0:D], hid[u][:, m, :], r2[u][:, m, :],
                                         start=(m == 0), stop=(m == FT - 1))
                    last.then_inc(s["outputs_ready"], 1)

                pe.wait_ge(s["scalar_took"], (len(turns) + 1) // 2)
                pe.wait_ge(s["vector_took"], len(turns) // 2)
                hidden(0, 0, 0)
                for b in range(1, PEEL):
                    hidden(b, b // RING, b % RING)
                    outputs(b - 1, (b - 1) // RING, (b - 1) % RING)
                with pe.Fori(0, ROUNDS, 1) as i:
                    for j in range(RING):
                        at, before = PEEL + j, PEEL + j - 1
                        hidden(RING * i + at, i + at // RING, at % RING, peeled=False)
                        outputs(RING * i + before, i + before // RING, before % RING)
                outputs(BLOCKS - 1, (BLOCKS - 1) // RING, (BLOCKS - 1) % RING)

            def take_turned(eng, who, took):
                for n, turn in enumerate(turns):
                    if n % 2 == who:
                        eng.wait_ge(s["turned"], n + 1)
                        src = c.bank[n % NB][0:HF, 0:len(turn) * P].rearrange("p (b k n) -> p k b n", k=2, n=P)
                        first, count = turn[0][0], len(turn) // 2
                        dst = xT[:, :, first * P:(first + count) * P].rearrange("p k (b n) -> p k b n", n=P)
                        for k in range(2):
                            if affine is None:
                                last = (nc.vector.tensor_copy if who else nc.scalar.copy)(dst[:, k], src[:, k])
                            elif who:
                                last = nc.vector.tensor_scalar(dst[:, k], src[:, k], affine[0][0:HF, k:k + 1],
                                                               affine[1][0:HF, k:k + 1], ALU.mult, ALU.add)
                            else:
                                last = nc.scalar.activation(dst[:, k], src[:, k], ACT.Identity, bias=affine[1][0:HF, k:k + 1],
                                                            scale=affine[0][0:HF, k:k + 1])
                        last.then_inc(took, 1)

            @block.scalar
            def _(act):
                act.wait_ge(soft["scattered"], done["scattered"])
                for n, (lo, hi) in enumerate(CHUNKS):
                    act.dma_start(xs[:, lo:hi, :], blocks_of(c.block_rows)[:, lo:hi, :]).then_inc(s[f"chunk{n}"], 16)
                take_turned(act, 0, s["scalar_took"])

                def hidden(b, u):
                    for part, ms in enumerate(((0, 1, 2, 3), (4, 5))):
                        act.wait_ge(s["hidden_ready"], 2 * b + part + 1)
                        src = c.bank[2 * u + part]
                        if b1 is None:
                            last = nc.scalar.activation(hid[u][:, ms[0]:ms[-1] + 1, :].rearrange("p m n -> p (m n)"),
                                                        src[:, 0:len(ms) * P], func)
                        else:
                            for m in ms:
                                last = nc.scalar.activation(hid[u][:, m, :], src[:, m % 4 * P:(m % 4 + 1) * P], func,
                                                            bias=rb[u][:, m:m + 1])
                        last.then_inc(s["hidden_taken"], 1)

                for b in range(PEEL):
                    hidden(b, b % RING)
                with act.Fori(0, ROUNDS, 1) as i:
                    for j in range(RING):
                        hidden(RING * i + (PEEL + j), (PEEL + j) % RING)

            @block.vector
            def _(dve):
                take_turned(dve, 1, s["vector_took"])

                def outputs(b, u):
                    dve.wait_ge(s["outputs_ready"], b + 1)
                    nc.vector.tensor_scalar(xs[:, b, :], c.bank[2 * u + 1][:, 0:D], 1.0, None, ALU.mult
                                            ).then_inc(s["outputs_taken"], 1)

                for b in range(PEEL):
                    outputs(b, b % RING)
                with dve.Fori(0, ROUNDS, 1) as i:
                    for j in range(RING):
                        outputs(RING * i + (PEEL + j), (PEEL + j) % RING)
                finish(dve, Steps(dve, s["vector_step"]), outs, lambda t: (soft[f"back{t // 2}"], done[f"back{t // 2}"]))


def blocks_of(rows):
    return rows.rearrange("(b p) d -> p b d", p=P)


def block_columns(xT, k, b):
    return xT.rearrange("p k (b n) -> p k b n", n=P)[:, k, b, :]


def top2_ffn(c, name, router, func, eps, b1=None, b2=None, affine=None):
    nc = c.nc
    with ExitStack() as mem:
        gate = [mem.enter_context(nc.sbuf_tensor(f"{name}_gate{k}", [P, NT], F32)) for k in range(2)]
        slots = mem.enter_context(nc.sbuf_tensor(name + "_slots", [P, 2, NT], U32))
        block_expert = mem.enter_context(nc.sbuf_tensor(name + "_block_expert", [P, BLOCKS], I32))
        route_top2(c, router, gate, slots, block_expert, eps, b2)

        def finish(dve, step, outs, arrived):
            for t in range(NT):
                dve.wait_ge(*arrived(t))
                for k in range(2):
                    step.then(nc.vector.scalar_tensor_tensor(c.H[:, t, :], outs[:, t, k, :], gate[k][:, t:t + 1],
                                                             c.H[:, t, :], ALU.mult, ALU.add))

        experts_in_blocks(c, name, c.XN, slots, block_expert, 2, 8, func, b1, affine, finish)


TTT = 512
TH = TTT // P
LR = 0.01


def test_time_training(c):
    nc = c.nc
    with ExitStack() as mem:
        def sb(name, shape):
            return mem.enter_context(nc.sbuf_tensor(name, shape, F32))
        U, S, V = sb("ttt_u", [P, B, TTT]), sb("ttt_s", [P, B, TTT]), sb("ttt_v", [P, B, TTT])
        SV, A, DU, DV = (sb("ttt_" + n, [P, B, TTT]) for n in ("sv", "a", "du", "dv"))
        AT = sb("ttt_aT", [P, TH, B * P])
        G, GT = sb("ttt_g", [P, B, D]), sb("ttt_gT", [HF, 2, B * P])
        gate = sb("ttt_gate", [P, TH, B * P])
        order = []
        for b in range(B):
            order += [(("u", b), "s"), (("v", b), "v")]
        order += [(("aT", m), "s") for m in range(TH)]
        order += [(("o", b), "v") for b in range(B)]
        order += [(("gT", k), "s") for k in range(2)]
        order += [(("da", b), "v") for b in range(B)]
        order += [(("g1", m2), "v") for m2 in range(2)]
        order += [(("g2", k), "v") for k in range(2)] + [(("g0", k), "v") for k in range(2)]
        for m in range(TH):
            order += [(("u1", m), "s"), (("v1", m), "v")]
        order += [(("o1", b2), "v") for b2 in range(2)]
        with stage(nc, JOB_SEMS + "u_copied hidden_ready g_ready") as (block, s):
            jobs = Jobs(c, s, order)
            tok = lambda b, chunk: slice((TPB * b + chunk) * P, (TPB * b + chunk + 1) * P)
            chunk1 = lambda k: c.XT[:, k, :].rearrange("p (b i n) -> p b i n", b=B, i=TPB)[:, :, 1, :]

            @block.tensor
            def _(pe):
                for name in ("ttt_w0", "ttt_w1", "ttt_w2", "ttt_w1T"):
                    pe.wait_ge(c.weights_in[name], 16)
                for key, _ in order:
                    kind, n, bank = key[0], key[1], jobs.bank(key)
                    jobs.bank_free(pe, key)
                    if kind in "uv":
                        w = c.tile["ttt_w0"] if kind == "u" else c.tile["ttt_w2"]
                        for k in range(2):
                            last = pe.matmul(bank, c.XT[:, k, tok(n, 0)], w[:, k, :], start=(k == 0), stop=(k == 1))
                    elif kind == "aT":
                        pe.wait_ge(s["hidden_ready"], B)
                        for b in range(B):
                            last = pe.transpose(bank[:, b * P:(b + 1) * P], A[:, b, n * P:(n + 1) * P], c.ident[:, :])
                    elif kind == "o":
                        pe.wait_ge(*jobs.taken(("aT", TH - 1)))
                        for m in range(TH):
                            last = pe.matmul(bank[:, 0:D], AT[:, m, n * P:(n + 1) * P], c.tile["ttt_w1"][:, m, :],
                                             start=(m == 0), stop=(m == TH - 1))
                    elif kind == "gT":
                        pe.wait_ge(s["g_ready"], B)
                        for b in range(B):
                            last = pe.transpose(bank[0:HF, b * P:(b + 1) * P], G[:, b, n * HF:(n + 1) * HF], c.ident[:, :])
                    elif kind == "da":
                        for k in range(2):
                            pe.wait_ge(*jobs.taken(("gT", k)))
                            last = pe.matmul(bank, GT[:, k, n * P:(n + 1) * P], c.tile["ttt_w1T"][:, k, :],
                                             start=(k == 0), stop=(k == 1))
                    elif kind == "g1":
                        for i in range(2):
                            for b in range(B):
                                last = pe.matmul(bank[:, i * D:(i + 1) * D], A[:, b, (2 * n + i) * P:(2 * n + i + 1) * P],
                                                 G[:, b, :], start=(b == 0), stop=(b == B - 1))
                    elif kind in ("g0", "g2"):
                        src = DU if kind == "g0" else DV
                        pe.wait_ge(*jobs.taken(("da", B - 1)))
                        for b in range(B):
                            last = pe.matmul(bank[0:HF, :], c.XN[:, TPB * b, n * HF:(n + 1) * HF], src[:, b, :],
                                             start=(b == 0), stop=(b == B - 1))
                    elif kind in ("u1", "v1"):
                        w = c.tile["ttt_w0"] if kind == "u1" else c.tile["ttt_w2"]
                        for k in range(2):
                            pe.wait_ge(*jobs.taken(("g0", k)))
                            last = pe.matmul(bank.rearrange("p (b n) -> p b n", b=B), w[:, k, n * P:(n + 1) * P], chunk1(k),
                                             start=(k == 0), stop=(k == 1))
                    else:
                        pe.wait_ge(*jobs.taken(("v1", TH - 1)))
                        for i in range(2):
                            b = 2 * n + i
                            for m in range(TH):
                                last = pe.matmul(bank[:, i * D:(i + 1) * D], AT[:, m, b * P:(b + 1) * P], c.tile["ttt_w1"][:, m, :],
                                                 start=(m == 0), stop=(m == TH - 1))
                    last.then_inc(s["product_ready"], 1)

            @block.scalar
            def _(act):
                for b in range(B):
                    act.wait_ge(*jobs.ready(("u", b)))
                    nc.scalar.copy(U[:, b, :], jobs.bank(("u", b))).then_inc(s["scalar_step"], 1)
                    nc.scalar.activation(S[:, b, :], jobs.bank(("u", b)), ACT.Sigmoid).then_inc(s["scalar_took"], 1)
                for m in range(TH):
                    act.wait_ge(*jobs.ready(("aT", m)))
                    nc.scalar.copy(AT[:, m, :], jobs.bank(("aT", m))).then_inc(s["scalar_took"], 1)
                for k in range(2):
                    act.wait_ge(*jobs.ready(("gT", k)))
                    nc.scalar.copy(GT[:, k, :], jobs.bank(("gT", k))[0:HF, :]).then_inc(s["scalar_took"], 1)
                for m in range(TH):
                    act.wait_ge(*jobs.ready(("u1", m)))
                    nc.scalar.activation(gate[:, m, :], jobs.bank(("u1", m)), ACT.Silu).then_inc(s["scalar_took"], 1)

            @block.vector
            def _(dve):
                step = Steps(dve, s["vector_step"])
                for b in range(B):
                    dve.wait_ge(*jobs.ready(("v", b)))
                    nc.vector.tensor_copy(V[:, b, :], jobs.bank(("v", b))).then_inc(s["vector_took"], 1)
                    dve.wait_ge(*jobs.taken(("u", b)))
                    dve.wait_ge(*jobs.taken(("v", b)))
                    step.then(nc.vector.tensor_tensor(SV[:, b, :], S[:, b, :], V[:, b, :], ALU.mult))
                    nc.vector.tensor_tensor(A[:, b, :], U[:, b, :], SV[:, b, :], ALU.mult).then_inc(s["hidden_ready"], 1)
                for b in range(B):
                    step.mark(nc.vector.tensor_tensor(V[:, b, :], U[:, b, :], S[:, b, :], ALU.mult))
                for b in range(B):
                    dve.wait_ge(s["vector_step"], step.n - B + 1 if b == 0 else step.n)
                    step.then(nc.vector.tensor_tensor(U[:, b, :], U[:, b, :], V[:, b, :], ALU.subtract))
                    step.mark(nc.vector.scalar_tensor_tensor(SV[:, b, :], U[:, b, :], 1.0, SV[:, b, :], ALU.add, ALU.mult))
                for b in range(B):
                    dve.wait_ge(*jobs.ready(("o", b)))
                    o = jobs.bank(("o", b))[:, 0:D]
                    step.then(nc.vector.tensor_tensor(G[:, b, :], o, c.XN[:, TPB * b, :], ALU.subtract))
                    nc.vector.tensor_scalar(G[:, b, :], G[:, b, :], 2.0 / (B * P * D), None, ALU.mult).then_inc(s["g_ready"], 1)
                    nc.vector.tensor_tensor(c.H[:, TPB * b, :], c.H[:, TPB * b, :], o, ALU.add).then_inc(s["vector_took"], 1)
                for b in range(B):
                    dve.wait_ge(*jobs.ready(("da", b)))
                    nc.vector.tensor_tensor(DV[:, b, :], jobs.bank(("da", b)), V[:, b, :], ALU.mult)
                    nc.vector.tensor_tensor(DU[:, b, :], jobs.bank(("da", b)), SV[:, b, :], ALU.mult).then_inc(s["vector_took"], 1)
                for m2 in range(2):
                    dve.wait_ge(*jobs.ready(("g1", m2)))
                    w = c.tile["ttt_w1"][:, 2 * m2:2 * m2 + 2, :]
                    nc.vector.scalar_tensor_tensor(w, jobs.bank(("g1", m2))[:, 0:2 * D].rearrange("p (i d) -> p i d", i=2),
                                                   -LR, w, ALU.mult, ALU.add).then_inc(s["vector_took"], 1)
                for kind, w in (("g2", c.tile["ttt_w2"]), ("g0", c.tile["ttt_w0"])):
                    for k in range(2):
                        dve.wait_ge(*jobs.ready((kind, k)))
                        nc.vector.scalar_tensor_tensor(w[:, k, :], jobs.bank((kind, k))[0:HF, :], -LR, w[:, k, :], ALU.mult,
                                                       ALU.add).then_inc(s["vector_took"], 1)
                for m in range(TH):
                    dve.wait_ge(*jobs.ready(("v1", m)))
                    dve.wait_ge(*jobs.taken(("u1", m)))
                    nc.vector.tensor_tensor(AT[:, m, :], gate[:, m, :], jobs.bank(("v1", m)), ALU.mult
                                            ).then_inc(s["vector_took"], 1)
                for b2 in range(2):
                    dve.wait_ge(*jobs.ready(("o1", b2)))
                    h = c.H.rearrange("p (b i) d -> p b i d", b=B)[:, 2 * b2:2 * b2 + 2, 1, :]
                    nc.vector.tensor_tensor(h, h, jobs.bank(("o1", b2))[:, 0:2 * D].rearrange("p (i d) -> p i d", i=2),
                                            ALU.add).then_inc(s["vector_took"], 1)


SE = 16
CAP = 64


def switch_ffn(c):
    nc = c.nc
    with ExitStack() as mem:
        def sb(name, shape):
            return mem.enter_context(nc.sbuf_tensor(name, shape, F32))
        NM = sb("sw_normed", [P, NT, D])
        best, drop, keep = sb("sw_best", [P, NT]), sb("sw_drop", [P, NT]), sb("sw_keep", [P, NT])
        slots = mem.enter_context(nc.sbuf_tensor("sw_slots", [P, 1, NT], U32))
        block_expert = mem.enter_context(nc.sbuf_tensor("sw_block_expert", [P, BLOCKS], I32))
        switch_route(c, NM, best, drop, keep, slots, block_expert)

        def finish(dve, step, outs, arrived):
            step.then(nc.vector.tensor_tensor(c.H[:, :, :], c.H[:, :, :], c.XN[:, :, :], ALU.add))
            for t in range(NT):
                step.then(nc.vector.scalar_tensor_tensor(c.H[:, t, :], NM[:, t, :], drop[:, t:t + 1], c.H[:, t, :],
                                                         ALU.mult, ALU.add))
            for t in range(NT):
                dve.wait_ge(*arrived(t))
                step.mark(nc.vector.scalar_tensor_tensor(c.H[:, t, :], outs[:, t, 0, :], keep[:, t:t + 1], c.H[:, t, :],
                                                         ALU.mult, ALU.add))

        experts_in_blocks(c, "switch", NM, slots, block_expert, 1, SE, ACT.Relu, None, None, finish)


def switch_route(c, NM, best, drop, keep, slots, block_expert):
    nc = c.nc
    E = SE
    shape = [P, NT, E]
    with ExitStack() as mem:
        def sb(name, shape_):
            return mem.enter_context(nc.sbuf_tensor(name, shape_, F32))
        square = sb("sw_square", [P, 2, D])
        ss, rms = sb("sw_ss", [P, NT]), sb("sw_rms", [P, NT])
        probs, eq, one, work = sb("sw_probs", shape), sb("sw_eq", shape), sb("sw_one", shape), sb("sw_work", shape)
        mx, sm = sb("sw_mx", [P, NT]), sb("sw_sm", [P, NT])
        nth = sb("sw_nth", [P, NT])
        places = Places(c, mem, E)
        order = [(("turn", g, k), "sv"[k]) for g in range(2) for k in range(2)]
        order += [(("logits",), "v"), (("image_count",), "v"), (("count",), "v")]
        with stage(nc, JOB_SEMS + "squared rms_ready normed shifted exped chosen") as (block, s):
            jobs = Jobs(c, s, order)

            @block.scalar
            def _(act):
                for t in range(NT):
                    if t >= 2:
                        act.wait_ge(s["squared"], t - 1)
                    nc.scalar.activation(square[:, t % 2, :], c.XN[:, t, :], ACT.Square,
                                         accum_out=ss[:, t:t + 1]).then_inc(s["squared"], 1)
                act.wait_ge(s["squared"], NT)
                nc.scalar.activation(rms[:, :], ss[:, :], ACT.Sqrt, bias=c.eps6, scale=1.0 / D).then_inc(s["rms_ready"], 1)
                for g in range(2):
                    act.wait_ge(*jobs.ready(("turn", g, 0)))
                    nc.scalar.copy(c.XT[:, 0, g * BANK:(g + 1) * BANK], jobs.bank(("turn", g, 0))[0:HF, :]
                                   ).then_inc(s["scalar_took"], 1)
                act.wait_ge(s["shifted"], 1)
                nc.scalar.activation(probs[:, :, :], probs[:, :, :], ACT.Exp).then_inc(s["exped"], 1)

            @block.tensor
            def _(pe):
                pe.wait_ge(c.weights_in["switch_router"], 16)
                for key, _ in order:
                    kind, bank = key[0], jobs.bank(key)
                    if kind == "turn":
                        _, g, k = key
                        pe.wait_ge(s["normed"], 4 * (g + 1))
                        for i in range(4):
                            last = pe.transpose(bank[0:HF, i * P:(i + 1) * P], NM[:, 4 * g + i, k * HF:(k + 1) * HF],
                                                c.ident[:, :])
                    elif kind == "logits":
                        for k in range(2):
                            pe.wait_ge(*jobs.taken(("turn", 1, k)))
                        for t in range(NT):
                            for k in range(2):
                                last = pe.matmul(bank[:, t * E:(t + 1) * E], c.XT[:, k, t * P:(t + 1) * P],
                                                 c.tile["switch_router"][:, k, :], start=(k == 0), stop=(k == 1))
                    elif kind == "count":
                        last = places.count(pe, bank, one)
                    else:
                        pe.wait_ge(s["chosen"], 1)
                        o = one.rearrange("p (b i) e -> p b i e", b=B)
                        dst = bank[:, 0:2 * B * E].rearrange("p (i b e) -> p i b e", i=2, b=B)
                        pe.matmul(dst[:, 0], c.tri[:, :], o[:, :, 0, :], start=True, stop=True)
                        pe.matmul(dst[:, 1], c.full[:, :], o[:, :, 0, :], start=True, stop=False)
                        last = pe.matmul(dst[:, 1], c.tri[:, :], o[:, :, 1, :], start=False, stop=True)
                    last.then_inc(s["product_ready"], 1)

            @block.vector
            def _(dve):
                step = Steps(dve, s["vector_step"])
                dve.wait_ge(s["rms_ready"], 1)
                step.then(nc.vector.reciprocal(rms[:, :], rms[:, :]))
                for t in range(NT):
                    nc.vector.scalar_tensor_tensor(NM[:, t, :], c.XN[:, t, :], rms[:, t:t + 1], c.row("switch_ln_w"),
                                                   ALU.mult, ALU.mult).then_inc(s["normed"], 1)
                for g in range(2):
                    dve.wait_ge(*jobs.ready(("turn", g, 1)))
                    nc.vector.tensor_copy(c.XT[:, 1, g * BANK:(g + 1) * BANK], jobs.bank(("turn", g, 1))[0:HF, :]
                                          ).then_inc(s["vector_took"], 1)
                dve.wait_ge(*jobs.ready(("logits",)))
                nc.vector.tensor_copy(probs[:, :, :], jobs.bank(("logits",))[:, 0:NT * E].rearrange(
                    "p (t e) -> p t e", e=E)).then_inc(s["vector_took"], 1)
                dve.wait_ge(*jobs.taken(("logits",)))
                softmax_rows(c, dve, step, s, probs[:, :, :], (mx[:, :], sm[:, :]), shape)
                pick_first_best(c, step, probs[:, :, :], best[:, :], eq[:, :, :], one[:, :, :], c.rank[:, 0:E], shape)
                nc.vector.tensor_copy(work[:, :, :], one[:, :, :]).then_inc(s["chosen"], 1)
                dve.wait_ge(s["chosen"], 1)
                dve.wait_ge(*jobs.ready(("image_count",)))
                src = jobs.bank(("image_count",))[:, 0:2 * B * E].rearrange("p (i b e) -> p b i e", i=2, b=B)
                w4 = work.rearrange("p (b i) e -> p b i e", b=B)
                nc.vector.tensor_tensor(w4, w4, src, ALU.mult).then_inc(s["vector_took"], 1)
                dve.wait_ge(*jobs.ready(("count",)))
                places.find(dve, step, jobs, (one,), slots, block_expert)
                step.then(nc.vector.tensor_reduce(nth[:, :], work[:, :, :], AX.X, ALU.add))
                step.then(nc.vector.tensor_scalar(drop[:, :], nth[:, :], float(CAP), None, ALU.is_gt))
                step.then(nc.vector.tensor_scalar(keep[:, :], nth[:, :], float(CAP), None, ALU.is_le))
                step.then(nc.vector.tensor_tensor(drop[:, :], drop[:, :], best[:, :], ALU.mult))
                step.then(nc.vector.tensor_tensor(keep[:, :], keep[:, :], best[:, :], ALU.mult))


def softmax_attention(c):
    nc = c.nc
    with ExitStack() as mem:
        def sb(name, shape):
            return mem.enter_context(nc.sbuf_tensor(name, shape, F32))
        QT, KT, V = sb("att_QT", [P, HG, T]), sb("att_KT", [P, HG, T]), sb("att_V", [P, NT, D])
        AO = sb("att_rows", [P, NT, D])
        attention_project(c, QT, KT, V)
        attention_heads(c, QT, KT, V, AO)
        attention_out(c, AO)


def attention_project(c, QT, KT, V):
    nc = c.nc
    order = [(("qk", m, g), "s") for m in range(2 * HG) for g in range(2)] + [(("v", t), "v") for t in range(0, NT, 2)]
    with stage(nc, JOB_SEMS) as (block, s):
        jobs = Jobs(c, s, order)

        @block.tensor
        def _(pe):
            for name in ("att_qk", "att_v"):
                pe.wait_ge(c.weights_in[name], 16)
            for key, _ in order:
                bank = jobs.bank(key)
                jobs.bank_free(pe, key)
                if key[0] == "qk":
                    _, m, g = key
                    for k in range(2):
                        last = pe.matmul(bank, c.tile["att_qk"][:, k, m * P:(m + 1) * P], c.XT[:, k, g * BANK:(g + 1) * BANK],
                                         start=(k == 0), stop=(k == 1))
                else:
                    for i in range(2):
                        t = key[1] + i
                        for k in range(2):
                            last = pe.matmul(bank[:, i * D:(i + 1) * D], c.XT[:, k, t * P:(t + 1) * P], c.tile["att_v"][:, k, :],
                                             start=(k == 0), stop=(k == 1))
                last.then_inc(s["product_ready"], 1)

        @block.scalar
        def _(act):
            for key in jobs.by("s"):
                _, m, g = key
                act.wait_ge(*jobs.ready(key))
                dst = QT if m < HG else KT
                nc.scalar.activation(dst[:, m % HG, g * BANK:(g + 1) * BANK], jobs.bank(key), ACT.Identity,
                                     bias=c.col("att_b_qk")[:, m:m + 1]).then_inc(s["scalar_took"], 1)

        @block.vector
        def _(dve):
            for key in jobs.by("v"):
                t = key[1]
                dve.wait_ge(*jobs.ready(key))
                nc.vector.tensor_tensor(V[:, t:t + 2, :], jobs.bank(key)[:, 0:2 * D].rearrange("p (t d) -> p t d", t=2),
                                        c.row("att_b_v").unsqueeze(1).to_broadcast([P, 2, D]),
                                        ALU.add).then_inc(s["vector_took"], 1)


def attention_heads(c, QT, KT, V, AO):
    nc = c.nc
    LAG, RINGP = 3, 4
    AT_WINDOW = (0, 64, P - HD)
    SCALE = HD ** -0.5
    with ExitStack() as mem:
        def sb(name, shape):
            return mem.enter_context(nc.sbuf_tensor(name, shape, F32))
        prob = sb("att_prob", [P, RINGP, 2, N])
        probT = sb("att_probT", [P, 2, TPB, NH, TPB, P])
        negmax = sb("att_negmax", [P, 48, 2])
        sums, inv = sb("att_sums", [P, NT, NH]), sb("att_inv", [P, NT, NH])
        units = [(b, r, n) for b in range(B) for r in range(4) for n in range(3)]

        def members(u):
            _, r, n = u
            pairs = [(i, hg) for i in range(TPB) for hg in range(HG)]
            return [(i, 4 * hg + r) for i, hg in pairs[2 * n:2 * n + 2]]

        order = []
        for j in range(len(units) + LAG + 2):
            if j < len(units):
                order.append((("s", j), "s"))
            if 0 <= j - LAG < len(units):
                order.append((("t", j - LAG), "s" if j % 4 == 0 else "v"))
            if j >= 12 + LAG + 1 and (j - LAG - 1) % 12 == 0:
                order += [(("o", (j - LAG - 1) // 12 - 1, i, q), "v") for i in range(TPB) for q in range(HG)]
        assert len(order) == 2 * len(units) + NT * HG
        with stage(nc, JOB_SEMS + "max_ready exped") as (block, s):
            jobs = Jobs(c, s, order)

            @block.tensor
            def _(pe):
                for key, _ in order:
                    kind, bank = key[0], jobs.bank(key)
                    jobs.bank_free(pe, key)
                    if kind == "s":
                        b = units[key[1]][0]
                        for x, (i, h) in enumerate(members(units[key[1]])):
                            r, t = head_rows(h), TPB * b + i
                            last = pe.matmul(bank[:, x * N:(x + 1) * N], QT[r, h // 4, t * P:(t + 1) * P],
                                             KT[r, h // 4, b * N:(b + 1) * N], start=True, stop=True,
                                             tile_position=(SLOT * (h % 4), 0))
                    elif kind == "t":
                        j = key[1]
                        pe.wait_ge(*jobs.taken(("s", j)))
                        for x in range(2):
                            for kt in range(TPB):
                                at = (2 * x + kt) * P
                                last = pe.transpose(bank[:, at:at + P], prob[:, j % RINGP, x, kt * P:(kt + 1) * P],
                                                    c.ident[:, :])
                    else:
                        _, b, i, q = key
                        for j in range(12 * b + 8, 12 * b + 12):
                            pe.wait_ge(*jobs.taken(("t", j)))
                        for x in range(4):
                            h = 4 * q + x
                            w0 = h * HD - AT_WINDOW[q]
                            for kt in range(TPB):
                                last = pe.matmul(bank[:, x * P:(x + 1) * P], probT[:, b % 2, i, h, kt, :],
                                                 V[:, TPB * b + kt, w0:w0 + P], start=(kt == 0), stop=(kt == 1))
                    last.then_inc(s["product_ready"], 1)

            def turned(copy, took, eng, j):
                b = units[j][0]
                eng.wait_ge(*jobs.ready(("t", j)))
                if b >= 2:
                    eng.wait_ge(*jobs.ready(("o", b - 2, TPB - 1, HG - 1)))
                src = jobs.bank(("t", j))
                for x, (i, h) in enumerate(members(units[j])):
                    last = copy(probT[:, b % 2, i, h, :, :].rearrange("p k q -> p (k q)"), src[:, 2 * x * P:2 * (x + 1) * P])
                last.then_inc(took, 1)

            @block.scalar
            def _(act):
                for key, who in order:
                    if who != "s":
                        continue
                    kind, j = key
                    if kind == "t":
                        turned(nc.scalar.copy, s["scalar_took"], act, j)
                        continue
                    act.wait_ge(s["max_ready"], j + 1)
                    if j >= RINGP:
                        act.wait_ge(*jobs.ready(("t", j - RINGP)))
                    b = units[j][0]
                    for x, (i, h) in enumerate(members(units[j])):
                        last = nc.scalar.activation(prob[:, j % RINGP, x, :], jobs.bank(key)[:, x * N:(x + 1) * N], ACT.Exp,
                                                    bias=negmax[:, j, x:x + 1], scale=SCALE,
                                                    accum_out=sums[:, TPB * b + i, h:h + 1])
                    last.then_inc(s["scalar_took"], 1)

            @block.vector
            def _(dve):
                step = Steps(dve, s["vector_step"])
                for key, who in order:
                    if key[0] == "s":
                        j = key[1]
                        dve.wait_ge(*jobs.ready(key))
                        step.then(nc.vector.tensor_reduce(negmax[:, j, :], jobs.bank(key).rearrange("p (x k) -> p x k", x=2),
                                                          AX.X, ALU.max, negate=True))
                        nc.vector.tensor_scalar(negmax[:, j, :], negmax[:, j, :], SCALE, None,
                                                ALU.mult).then_inc(s["max_ready"], 1)
                    elif who == "v" and key[0] == "t":
                        turned(nc.vector.tensor_copy, s["vector_took"], dve, key[1])
                    elif who == "v":
                        _, b, i, q = key
                        t = TPB * b + i
                        dve.wait_ge(*jobs.ready(key))
                        if q == 0:
                            dve.wait_ge(*jobs.taken(("s", 12 * b + 11)))
                            step.then(nc.vector.reciprocal(inv[:, t, :], sums[:, t, :]))
                        heads, at = slice(4 * q, 4 * q + 4), AT_WINDOW[q]
                        nc.vector.tensor_tensor(AO[:, t, :].rearrange("p (h d) -> p h d", h=NH)[:, heads],
                                                jobs.bank(key).rearrange("p (h x) -> p h x", h=4)[:, :, at:at + HD],
                                                inv[:, t, heads].unsqueeze(2).to_broadcast([P, 4, HD]),
                                                ALU.mult).then_inc(s["vector_took"], 1)


def attention_out(c, AO):
    nc = c.nc
    with ExitStack() as mem:
        AOT = mem.enter_context(nc.sbuf_tensor("att_rowsT", [HF, 2, T], F32))
        order = [(("turn", g, k), "sv"[k]) for g in range(2) for k in range(2)] + [(("out", t), "v") for t in range(0, NT, 2)]
        with stage(nc, JOB_SEMS) as (block, s):
            jobs = Jobs(c, s, order)

            @block.tensor
            def _(pe):
                pe.wait_ge(c.weights_in["att_out"], 16)
                for key, _ in order:
                    bank = jobs.bank(key)
                    jobs.bank_free(pe, key)
                    if key[0] == "turn":
                        _, g, k = key
                        for i in range(4):
                            last = pe.transpose(bank[0:HF, i * P:(i + 1) * P], AO[:, 4 * g + i, k * HF:(k + 1) * HF],
                                                c.ident[:, :])
                    else:
                        for k in range(2):
                            pe.wait_ge(*jobs.taken(("turn", key[1] // 4, k)))
                        for i in range(2):
                            t = key[1] + i
                            for k in range(2):
                                last = pe.matmul(bank[:, i * D:(i + 1) * D], AOT[:, k, t * P:(t + 1) * P], c.tile["att_out"][:, k, :],
                                                 start=(k == 0), stop=(k == 1))
                    last.then_inc(s["product_ready"], 1)

            @block.scalar
            def _(act):
                for _, g, k in jobs.by("s"):
                    act.wait_ge(*jobs.ready(("turn", g, 0)))
                    nc.scalar.copy(AOT[:, 0, g * BANK:(g + 1) * BANK], jobs.bank(("turn", g, 0))[0:HF, :]
                                   ).then_inc(s["scalar_took"], 1)

            @block.vector
            def _(dve):
                for g in range(2):
                    dve.wait_ge(*jobs.ready(("turn", g, 1)))
                    nc.vector.tensor_copy(AOT[:, 1, g * BANK:(g + 1) * BANK], jobs.bank(("turn", g, 1))[0:HF, :]
                                          ).then_inc(s["vector_took"], 1)
                add_rows(c, dve, Steps(dve, s["vector_step"]), jobs, s, "out", c.row("att_b_out"))


def keep_rows(c):
    with stage(c.nc, "") as (block, s):
        @block.vector
        def _(dve):
            c.nc.vector.tensor_tensor(c.H[:, :, :], c.H[:, :, :], c.XN[:, :, :], ALU.add)


def first_layers(c):
    norm_and_turn(c, c.H, c.XN, c.XT, D, c.eps5)
    gated_convolutions(c)
    norm_and_turn(c, c.H, c.XN, c.XT, D, c.eps5)
    entangled_ffn(c)
    norm_and_turn(c, c.H, c.XN, c.XT, D, c.eps5)
    nystrom_attention(c)


def later_layers(c):
    c.allocate_weights(LATE, c.ctx)

    def load_late(sp):
        c.load_weights(sp, LATE)
        sp.dma_start(blocks_of(c.block_rows), c.zero_row[:, :].unsqueeze(1).to_broadcast([P, BLOCKS, D])).then_inc(
            c.rows_zeroed, 16)

    norm_and_turn(c, c.H, c.XN, c.XT, D, c.eps5, sync=load_late)
    top2_ffn(c, "moe1", c.tile["moe1_gate"], ACT.Gelu, 1e-9, c.w["moe1_b1"], c.tile["moe1_b2"])
    norm_and_turn(c, c.H, c.XN, c.XT, D, c.eps5)
    test_time_training(c)
    norm_and_turn(c, c.H, c.XN, c.XT, D, c.eps5)
    switch_ffn(c)
    norm_and_turn(c, c.H, c.XN, c.XT, D, c.eps5)
    softmax_attention(c)
    norm_and_turn(c, c.H, c.XN, c.XT, D, c.eps5)
    keep_rows(c)
    norm_and_turn(c, c.XN, c.XN, c.XT, D, c.eps5, c.col("moe3_gamma"), c.col("moe3_beta"))
    top2_ffn(c, "moe3", c.tile["moe3_router"], ACT.Silu, 0.0,
             affine=(c.col("moe3_gamma"), c.col("moe3_beta")))


ROWS = [("conv_b", DT), ("tok_out_b0", DT), ("tok_out_b1", DT), ("tok_ff2_b0", DT), ("tok_ff2_b1", DT),
        ("head_b", D), ("mix_b", D), ("ffn_b_proj", D), ("nys_b_proj", D), ("att_b_v", D), ("att_b_out", D),
        ("switch_ln_w", D), ("alpha", 6), ("mem_Wg_b", 4)]
COLS = [("tok_ln1_g0", 1), ("tok_ln1_b0", 1), ("tok_ln1_g1", 1), ("tok_ln1_b1", 1),
        ("tok_ln2_g0", 1), ("tok_ln2_b0", 1), ("tok_ln2_g1", 1), ("tok_ln2_b1", 1), ("lnf_g", 1), ("lnf_b", 1),
        ("tok_ff1_b0", 4), ("tok_ff1_b1", 4), ("router_b", 2), ("mixg_b", 2), ("ffn_b_fc", 6),
        ("conv_taps", 6 * 3 * 4), ("conv_bias", 6 * 3), ("att_b_qk", 2 * HG),
        ("moe3_gamma", 2), ("moe3_beta", 2)]


def spans(table):
    at, out = 0, {}
    for name, width in table:
        out[name] = (at, width)
        at += width
    return out, at


ROW_AT, ROW_LEN = spans(ROWS)
COL_AT, COL_LEN = spans(COLS)

TOK = ("tok_qkv", "tok_out", "tok_ff1", "tok_ff2", "head_w")
EARLY = ("gate_wT", "router_wT", "mixg_wT", "mix_wT", "mem_qk", "ffn_fcT", "ffn_proj", "nys_qk", "nys_v", "nys_proj")
LATE = ("ttt_w0", "ttt_w2", "ttt_w1", "ttt_w1T", "att_qk", "att_v", "att_out", "moe1_b2", "moe1_gate", "switch_router",
        "moe3_router")


def tokenizer(c, scope):
    c.X = c.sb("tok_residual", [P, NT, DT], scope)
    c.YT = c.sb("tok_rowsT", [P, 1, T], scope)
    tokenizer_patches(c, c.w)
    for layer in range(2):
        norm_and_turn(c, c.X, c.XN, c.YT, DT, c.eps5, c.col(f"tok_ln1_g{layer}"), c.col(f"tok_ln1_b{layer}"))
        tokenizer_attention(c, layer)
        norm_and_turn(c, c.X, c.XN, c.YT, DT, c.eps5, c.col(f"tok_ln2_g{layer}"), c.col(f"tok_ln2_b{layer}"))
        tokenizer_ffn(c, layer)
    norm_and_turn(c, c.X, c.XN, c.YT, DT, c.eps5, c.col("lnf_g"), c.col("lnf_b"))
    tokenizer_head(c)


def tower(nc, w, out):
    with ExitStack() as ctx:
        c = Core(nc, ctx)
        c.w, c.stack = w, ctx
        out_done = ctx.enter_context(nc.semaphore("out_done"))
        c.allocate()
        prepare(c)
        with ExitStack() as early:
            c.allocate_weights(EARLY, early)
            with ExitStack() as tok:
                c.allocate_weights(TOK, tok)
                tokenizer(c, tok)
            first_layers(c)
        later_layers(c)
        with stage(nc, "") as (block, s):
            @block.sync
            def _(sp):
                sp.dma_start(out.rearrange("b (t p) d -> p (b t) d", p=P), c.H[:, :, :]).then_inc(out_done, 16)
                sp.wait_ge(out_done, 16)



def _layouts(a):
    f = np.ascontiguousarray
    o = {}
    o["patches"] = f(a["x"].reshape(B, 32, 16, 2, 4, 16, 8).transpose(1, 4, 3, 6, 0, 2, 5).reshape(P, 16, T))
    o["conv_w"] = f(a["L0_tok_conv_w"].reshape(P, 32, 2, 4, 8).transpose(1, 3, 2, 4, 0).reshape(P, 16, P))
    o["tok_qkv"] = f(a["L0_tok_qkv_w"].transpose(1, 0, 2))
    o["tok_out"] = f(a["L0_tok_out_w"].reshape(2, 4, P, DT).transpose(2, 0, 1, 3))
    o["tok_ff1"] = f(a["L0_tok_ff1_w"].transpose(1, 0, 2))
    o["tok_ff2"] = f(a["L0_tok_ff2_w"].reshape(2, 4, P, DT).transpose(2, 0, 1, 3))
    o["head_w"] = a["L0_tok_head_w"]

    def split(m):
        return f(m.reshape(2, HF, -1).transpose(1, 0, 2))

    def tiles(m, p=P):
        return f(m.reshape(-1, p, m.shape[-1]).transpose(1, 0, 2))

    def pad_heads(m):
        z = np.zeros((m.shape[0], NH, SLOT), m.dtype)
        z[:, :, :HD] = m.reshape(m.shape[0], NH, HD)
        return z.reshape(m.shape[0], NH * SLOT)

    o["gate_wT"] = split(a["L0_attn_gate_w"].T)
    o["router_wT"] = split(np.repeat(a["L0_attn_router_w"], HD, axis=0).T)
    o["mixg_wT"] = split(a["L0_attn_mixg_w"].T)
    o["mix_wT"] = split(a["L0_attn_mix_w"].T)
    m = np.zeros((64, 64 + 64 + 4), np.float32)
    for h in range(4):
        r = slice(16 * h, 16 * h + 16)
        m[r, 16 * h:16 * h + 16] = a["L0_attn_mem_Wq"][h].T
        m[r, 64 + 16 * h:64 + 16 * h + 16] = a["L0_attn_mem_Wk"][h].T
        m[r, 128 + h] = a["L0_attn_mem_Wg_w"][h, 0]
    o["mem_qk"] = m
    o["mem_v"] = f(a["L0_attn_mem_Wv"].transpose(1, 0, 2).reshape(P, 64))
    o["mem_out"] = f(a["L0_attn_mem_Wout"].transpose(2, 0, 1).reshape(P, 64))
    o["ffn_fcT"] = split(a["L0_ffn_w_fc"].T)
    o["ffn_proj"] = tiles(f(a["L0_ffn_w_proj"].T))
    q, k, v = (a["L1_attn_w_qkv"][:, i * D:(i + 1) * D] for i in range(3))
    o["nys_qk"] = split(np.concatenate([pad_heads(q), pad_heads(k)], 1))
    o["nys_v"] = split(v)
    o["nys_proj"] = split(a["L1_attn_w_proj"])
    o["moe1_w1"] = f(a["L1_ffn_w1"].reshape(8, 2, HF, FF).transpose(0, 2, 1, 3))
    o["moe1_w2"] = f(a["L1_ffn_w2"].reshape(8, FT, P, D).transpose(0, 2, 1, 3))
    o["moe1_b1"] = f(a["L1_ffn_b1"].reshape(8, FT, P).transpose(0, 2, 1))
    o["moe1_b2"] = a["L1_ffn_b2"]
    o["moe1_gate"] = split(a["L1_ffn_gate_w"].T)
    o["ttt_w0"], o["ttt_w2"] = split(a["L2_attn_w0"]), split(a["L2_attn_w2"])
    o["ttt_w1"], o["ttt_w1T"] = tiles(a["L2_attn_w1"]), split(f(a["L2_attn_w1"].T))
    o["switch_router"] = split(a["L2_ffn_w_router"])
    o["switch_w1"] = f(a["L2_ffn_wi"].reshape(16, 2, HF, FF).transpose(0, 2, 1, 3))
    o["switch_w2"] = f(a["L2_ffn_wo"].reshape(16, FT, P, D).transpose(0, 2, 1, 3))
    wq, wk, wv = (a["L3_attn_w_qkv"][i * D:(i + 1) * D].T for i in range(3))
    o["att_qk"] = split(np.concatenate([pad_heads(wq), pad_heads(wk)], 1))
    o["att_v"], o["att_out"] = split(f(wv)), split(f(a["L3_attn_w_out"].T))
    o["moe3_router"] = split(a["L3_ffn_router_w"])
    o["moe3_w1"] = f(a["L3_ffn_w1"].reshape(8, 2, HF, FF).transpose(0, 2, 1, 3))
    o["moe3_w2"] = f(a["L3_ffn_w2"].reshape(8, FT, P, D).transpose(0, 2, 1, 3))

    bqkv = a["L3_attn_b_qkv"]
    rows = {"conv_b": a["L0_tok_conv_b"], "head_b": a["L0_tok_head_b"], "mix_b": a["L0_attn_mix_b"],
            "ffn_b_proj": a["L0_ffn_b_proj"], "nys_b_proj": a["L1_attn_b_proj"], "att_b_v": bqkv[2 * D:],
            "att_b_out": a["L3_attn_b_out"], "switch_ln_w": a["L2_ffn_ln_w"],
            "alpha": np.concatenate([a["L0_ffn_alpha_e"], a["L0_ffn_alpha_r"]]), "mem_Wg_b": a["L0_attn_mem_Wg_b"][:, 0]}
    for i in range(2):
        rows[f"tok_out_b{i}"], rows[f"tok_ff2_b{i}"] = a["L0_tok_out_b"][i], a["L0_tok_ff2_b"][i]
    o["rows"] = np.concatenate([rows[n] for n, _ in ROWS])[None]
    cols = np.zeros((P, COL_LEN), np.float32)

    def col(name, m):
        at, n = COL_AT[name]
        m = m.reshape(n, -1)
        cols[:m.shape[1], at:at + n] = m.T

    for i in range(2):
        for n in ("ln1_g", "ln1_b", "ln2_g", "ln2_b"):
            col(f"tok_{n}{i}", a[f"L0_tok_{n}"][i])
        col(f"tok_ff1_b{i}", a["L0_tok_ff1_b"][i])
    col("lnf_g", a["L0_tok_lnf_g"])
    col("lnf_b", a["L0_tok_lnf_b"])
    col("router_b", np.repeat(a["L0_attn_router_b"], HD))
    col("mixg_b", a["L0_attn_mixg_b"])
    col("ffn_b_fc", a["L0_ffn_b_fc"])
    cw = a["L0_attn_conv_w"].reshape(6, 2, 3, HD, 4)
    taps = np.broadcast_to(cw[:, :, None], (6, 2, B, 3, HD, 4)).transpose(1, 2, 4, 0, 3, 5).reshape(P, 72)
    cb = a["L0_attn_conv_b"].reshape(6, 2, 3, HD)
    bias = np.broadcast_to(cb[:, :, None], (6, 2, B, 3, HD)).transpose(1, 2, 4, 0, 3).reshape(P, 18)
    cols[:, COL_AT["conv_taps"][0]:][:, :72] = taps
    cols[:, COL_AT["conv_bias"][0]:][:, :18] = bias
    bq, bk = pad_heads(bqkv[None, :D])[0], pad_heads(bqkv[None, D:2 * D])[0]
    col("att_b_qk", np.concatenate([bq, bk]))
    col("moe3_gamma", a["L3_ffn_ln_gamma"])
    col("moe3_beta", a["L3_ffn_ln_beta"])
    o["cols"] = cols
    return {k: f(v) for k, v in o.items()}


def kernel(**inputs):
    import concourse.bacc as _bacc
    from concourse.bass_utils import run_bass_kernel_spmd as _run

    nc = _bacc.Bacc("TRN2", target_bir_lowering=False, num_devices=1)
    arrays = _layouts({k: np.asarray(v) for k, v in inputs.items()})
    w = {}
    for name, a in arrays.items():
        w[name] = nc.dram_tensor(name + "_dram", a.shape, mybir.dt.from_np(a.dtype), kind="ExternalInput").ap()
    out = nc.dram_tensor("out_0_dram", (B, N, D), F32, kind="ExternalOutput").ap()
    tower(nc, w, out)
    r = _run(nc, [{name + "_dram": a for name, a in arrays.items()}], core_ids=[0])
    return r.results[0]["out_0_dram"]
```
